# Optimizing a Trainium2 kernel written in Bass

```python
import numpy as np
import jax
import jax.numpy as jnp

def _softmax(x, axis=-1):
    return jax.nn.softmax(x, axis=axis)

def _gelu(x):
    return jax.nn.gelu(x, approximate=True)

def _silu(x):
    return jax.nn.silu(x)

def _sigmoid(x):
    return jax.nn.sigmoid(x)

def _layernorm(x, axis=-1, eps=1e-05):
    m = jnp.mean(x, axis=axis, keepdims=True)
    v = jnp.var(x, axis=axis, keepdims=True)
    return (x - m) / jnp.sqrt(v + eps)

def _scatter_add(tgt, idx, src, axis=0):
    return tgt.at[idx].add(src)

def _segment_sum(src, seg, n):
    return jax.ops.segment_sum(src, seg, n)
kernel_name = 'mk_gps_d2_gnn_r8_1a3e74'

def setup_inputs(seed: int=0):
    np.random.seed(seed)
    _w = jnp.asarray

    def _rec_inputs():
        import jax
        import jax.numpy as jnp
        _gk = jax.random.key(seed)
        x = -0.0003713 + 1 * jax.random.normal(jax.random.fold_in(_gk, 1), (6250, 256), jnp.float32)
        src = jax.random.randint(jax.random.fold_in(_gk, 2), (200000,), 0, 6250, jnp.int32)
        dst = jnp.minimum((6250 * jax.random.uniform(jax.random.fold_in(_gk, 3), (200000,)) ** 2.0).astype(jnp.int32), 49999)
        _o = jnp.argsort(dst, stable=True)
        src = src[_o]
        dst = dst[_o]
        edge_weight = jax.random.uniform(jax.random.fold_in(_gk, 12), (200000,), jnp.float32, 0.0, 1)
        return (x, src, dst, edge_weight)
    x, src, dst, edge_weight = _rec_inputs()

    def _L0_gnn_setup():
        import jax, jax.numpy as jnp
        import numpy as np
        N = 6250
        E = 100000
        D = 256
        SMALL = 25
        key = jax.random.key(seed)
        k1, k2, k3, k4, k5 = jax.random.split(key, 5)
        x = jax.random.normal(k1, (N, D), jnp.float32)
        src = jax.random.randint(k2, (E,), 0, N)
        dst = jax.random.randint(k3, (E,), 0, N)
        Wq = jax.random.normal(k4, (D, SMALL), jnp.float32) / np.float32(np.sqrt(D))
        bq = jnp.zeros((SMALL,), jnp.float32)
        Wk = jax.random.normal(k5, (D, SMALL), jnp.float32) / np.float32(np.sqrt(D))
        bk = jnp.zeros((SMALL,), jnp.float32)
        return {'x': x, 'src': src, 'dst': dst, 'Wq': Wq, 'bq': bq, 'Wk': Wk, 'bk': bk}
    _L0_gnn_all = _L0_gnn_setup()
    _L0_gnn_in = {k: v for k, v in _L0_gnn_all.items() if k in ('Wq', 'bq', 'Wk', 'bk')}
    del _L0_gnn_all

    def _L0_mix_setup():
        import jax, jax.numpy as jnp
        import numpy as np
        N, F, C, H = (32, 512, 256, 8)
        D = C // H
        EPS_ATTN = 1e-06
        EPS_LN = 1e-05

        def layer_norm(x, g, b):
            mu = jnp.mean(x, axis=-1, keepdims=True)
            var = jnp.var(x, axis=-1, keepdims=True)
            return (x - mu) * jax.lax.rsqrt(var + EPS_LN) * g + b
        key = jax.random.key(seed)
        ks = jax.random.split(key, 8)
        s = 1.0 / np.sqrt(C)
        return {'x': jax.random.normal(ks[0], (N, F, C), jnp.float32), 'Wqkv': jax.random.uniform(ks[1], (3 * C, C), jnp.float32, -s, s), 'ln1_g': jnp.ones((C,), jnp.float32), 'ln1_b': jnp.zeros((C,), jnp.float32), 'W1': jax.random.uniform(ks[2], (C, C), jnp.float32, -s, s), 'b1': jax.random.uniform(ks[3], (C,), jnp.float32, -s, s), 'W2': jax.random.uniform(ks[4], (C, C), jnp.float32, -s, s), 'b2': jax.random.uniform(ks[5], (C,), jnp.float32, -s, s), 'ln2_g': jnp.ones((C,), jnp.float32), 'ln2_b': jnp.zeros((C,), jnp.float32)}
    _L0_mix_all = _L0_mix_setup()
    _L0_mix_in = {k: v for k, v in _L0_mix_all.items() if k in ('Wqkv', 'ln1_g', 'ln1_b', 'W1', 'b1', 'W2', 'b2', 'ln2_g', 'ln2_b')}
    del _L0_mix_all

    def _L0_ffn_setup():
        import jax, jax.numpy as jnp
        import numpy as np
        B, S, D = (8, 512, 256)
        H = 4 * D
        CAPACITY = 0.5
        key = jax.random.key(seed)
        ks = jax.random.split(key, 6)
        x = jax.random.normal(ks[0], (B, S, D), dtype=jnp.float32)
        attention_mask = jnp.zeros((B, 1, 1, S), dtype=jnp.float32)
        wr = jax.random.normal(ks[1], (D, 1), dtype=jnp.float32) * 0.02
        br = jnp.zeros((1,), dtype=jnp.float32)
        w1 = jax.random.normal(ks[2], (D, H), dtype=jnp.float32) * 0.02
        b1 = jnp.zeros((H,), dtype=jnp.float32)
        w2 = jax.random.normal(ks[3], (H, D), dtype=jnp.float32) * 0.02
        b2 = jnp.zeros((D,), dtype=jnp.float32)
        return {'x': x, 'attention_mask': attention_mask, 'wr': wr, 'br': br, 'w1': w1, 'b1': b1, 'w2': w2, 'b2': b2}
    _L0_ffn_all = _L0_ffn_setup()
    _L0_ffn_in = {k: v for k, v in _L0_ffn_all.items() if k in ('attention_mask', 'wr', 'br', 'w1', 'b1', 'w2', 'b2')}
    del _L0_ffn_all

    def _L1_gnn_setup():
        import jax, jax.numpy as jnp
        import numpy as np
        N_NODES = 12500
        N_EDGES = 400000
        D_IN = 256
        D_OUT = 256
        key = jax.random.key(seed)
        k1, k2, k3, k4, k5, k6 = jax.random.split(key, 6)
        x = jax.random.normal(k1, (N_NODES, D_IN), dtype=jnp.float32)
        edge_val = jax.random.uniform(k2, (N_EDGES,), dtype=jnp.float32)
        stdv = 1.0 / np.sqrt(D_OUT)
        W = jax.random.uniform(k3, (D_IN, D_OUT), dtype=jnp.float32, minval=-stdv, maxval=stdv)
        b = jax.random.uniform(k4, (D_OUT,), dtype=jnp.float32, minval=-stdv, maxval=stdv)
        edge_row = jax.random.randint(k5, (N_EDGES,), 0, N_NODES, dtype=jnp.int32)
        edge_col = jax.random.randint(k6, (N_EDGES,), 0, N_NODES, dtype=jnp.int32)
        return {'x': x, 'edge_val': edge_val, 'W': W, 'b': b, 'edge_row': edge_row, 'edge_col': edge_col}
    _L1_gnn_all = _L1_gnn_setup()
    _L1_gnn_in = {k: v for k, v in _L1_gnn_all.items() if k in ('W', 'b')}
    del _L1_gnn_all

    def _L1_mix_setup():
        import jax, jax.numpy as jnp
        import numpy as np
        NHEAD = 8
        ATT_EPS = 1e-06
        LN_EPS = 1e-05

        def _layernorm(x, g, b):
            mu = jnp.mean(x, axis=-1, keepdims=True)
            var = jnp.mean(jnp.square(x - mu), axis=-1, keepdims=True)
            return (x - mu) * jax.lax.rsqrt(var + LN_EPS) * g + b
        key = jax.random.key(seed)
        ks = jax.random.split(key, 7)
        N, L, C = (4, 2048, 256)
        s = 1.0 / np.sqrt(C)
        return {'x': jax.random.normal(ks[0], (N, L, C), jnp.float32), 'Wq': jax.random.normal(ks[1], (C, C), jnp.float32) * s, 'Wk': jax.random.normal(ks[2], (C, C), jnp.float32) * s, 'Wv': jax.random.normal(ks[3], (C, C), jnp.float32) * s, 'Wm': jax.random.normal(ks[4], (C, C), jnp.float32) * s, 'W1': jax.random.normal(ks[5], (2 * C, 2 * C), jnp.float32) * (1.0 / np.sqrt(2 * C)), 'W2': jax.random.normal(ks[6], (2 * C, C), jnp.float32) * (1.0 / np.sqrt(2 * C)), 'g1': jnp.ones((C,), jnp.float32), 'b1': jnp.zeros((C,), jnp.float32), 'g2': jnp.ones((C,), jnp.float32), 'b2': jnp.zeros((C,), jnp.float32)}
    _L1_mix_all = _L1_mix_setup()
    _L1_mix_in = {k: v for k, v in _L1_mix_all.items() if k in ('Wq', 'Wk', 'Wv', 'Wm', 'W1', 'W2', 'g1', 'b1', 'g2', 'b2')}
    del _L1_mix_all

    def _L1_ffn_setup():
        import math
        import jax, jax.numpy as jnp
        import numpy as np
        CAPACITY_FACTOR = 1.25
        TOP_K = 2
        LN_EPS = 1e-05

        def _layer_norm(x, gamma, beta):
            mu = jnp.mean(x, axis=-1, keepdims=True)
            var = jnp.var(x, axis=-1, keepdims=True)
            return (x - mu) * jax.lax.rsqrt(var + LN_EPS) * gamma + beta
        key = jax.random.key(seed)
        ks = jax.random.split(key, 4)
        B, S, D, F, E = (8, 512, 256, 512, 8)
        x = jax.random.normal(ks[0], (B, S, D), dtype=jnp.float32)
        Wr = jax.random.normal(ks[1], (D, E), dtype=jnp.float32) / np.sqrt(D)
        br = jnp.zeros((E,), jnp.float32)
        W1 = jax.random.normal(ks[2], (E, D, F), dtype=jnp.float32) / np.sqrt(D)
        b1 = jnp.zeros((E, F), jnp.float32)
        W2 = jax.random.normal(ks[3], (E, F, D), dtype=jnp.float32) / np.sqrt(F)
        b2 = jnp.zeros((E, D), jnp.float32)
        gamma = jnp.ones((D,), jnp.float32)
        beta = jnp.zeros((D,), jnp.float32)
        return {'x': x, 'Wr': Wr, 'br': br, 'W1': W1, 'b1': b1, 'W2': W2, 'b2': b2, 'gamma': gamma, 'beta': beta}
    _L1_ffn_all = _L1_ffn_setup()
    _L1_ffn_in = {k: v for k, v in _L1_ffn_all.items() if k in ('Wr', 'br', 'W1', 'b1', 'W2', 'b2', 'gamma', 'beta')}
    del _L1_ffn_all
    return {'x': x, 'src': src, 'dst': dst, 'edge_weight': edge_weight, 'L0_gnn_Wq': _L0_gnn_in['Wq'], 'L0_gnn_bq': _L0_gnn_in['bq'], 'L0_gnn_Wk': _L0_gnn_in['Wk'], 'L0_gnn_bk': _L0_gnn_in['bk'], 'L0_mix_Wqkv': _L0_mix_in['Wqkv'], 'L0_mix_ln1_g': _L0_mix_in['ln1_g'], 'L0_mix_ln1_b': _L0_mix_in['ln1_b'], 'L0_mix_W1': _L0_mix_in['W1'], 'L0_mix_b1': _L0_mix_in['b1'], 'L0_mix_W2': _L0_mix_in['W2'], 'L0_mix_b2': _L0_mix_in['b2'], 'L0_mix_ln2_g': _L0_mix_in['ln2_g'], 'L0_mix_ln2_b': _L0_mix_in['ln2_b'], 'L0_ffn_attention_mask': _L0_ffn_in['attention_mask'], 'L0_ffn_wr': _L0_ffn_in['wr'], 'L0_ffn_br': _L0_ffn_in['br'], 'L0_ffn_w1': _L0_ffn_in['w1'], 'L0_ffn_b1': _L0_ffn_in['b1'], 'L0_ffn_w2': _L0_ffn_in['w2'], 'L0_ffn_b2': _L0_ffn_in['b2'], 'L1_gnn_W': _L1_gnn_in['W'], 'L1_gnn_b': _L1_gnn_in['b'], 'L1_mix_Wq': _L1_mix_in['Wq'], 'L1_mix_Wk': _L1_mix_in['Wk'], 'L1_mix_Wv': _L1_mix_in['Wv'], 'L1_mix_Wm': _L1_mix_in['Wm'], 'L1_mix_W1': _L1_mix_in['W1'], 'L1_mix_W2': _L1_mix_in['W2'], 'L1_mix_g1': _L1_mix_in['g1'], 'L1_mix_b1': _L1_mix_in['b1'], 'L1_mix_g2': _L1_mix_in['g2'], 'L1_mix_b2': _L1_mix_in['b2'], 'L1_ffn_Wr': _L1_ffn_in['Wr'], 'L1_ffn_br': _L1_ffn_in['br'], 'L1_ffn_W1': _L1_ffn_in['W1'], 'L1_ffn_b1': _L1_ffn_in['b1'], 'L1_ffn_W2': _L1_ffn_in['W2'], 'L1_ffn_b2': _L1_ffn_in['b2'], 'L1_ffn_gamma': _L1_ffn_in['gamma'], 'L1_ffn_beta': _L1_ffn_in['beta']}

def reference(x, src, dst, edge_weight, L0_gnn_Wq, L0_gnn_bq, L0_gnn_Wk, L0_gnn_bk, L0_mix_Wqkv, L0_mix_ln1_g, L0_mix_ln1_b, L0_mix_W1, L0_mix_b1, L0_mix_W2, L0_mix_b2, L0_mix_ln2_g, L0_mix_ln2_b, L0_ffn_attention_mask, L0_ffn_wr, L0_ffn_br, L0_ffn_w1, L0_ffn_b1, L0_ffn_w2, L0_ffn_b2, L1_gnn_W, L1_gnn_b, L1_mix_Wq, L1_mix_Wk, L1_mix_Wv, L1_mix_Wm, L1_mix_W1, L1_mix_W2, L1_mix_g1, L1_mix_b1, L1_mix_g2, L1_mix_b2, L1_ffn_Wr, L1_ffn_br, L1_ffn_W1, L1_ffn_b1, L1_ffn_W2, L1_ffn_b2, L1_ffn_gamma, L1_ffn_beta):
    import jax
    import jax.numpy as jnp

    def _L0_gnn_ref(x, src, dst, Wq, bq, Wk, bk):
        import jax, jax.numpy as jnp
        import numpy as np
        N = 6250
        E = 100000
        D = 256
        SMALL = 25
        d_k = np.float32(np.sqrt(SMALL))
        q = jnp.tanh(x @ Wq + bq)
        k = x @ Wk + bk
        loop = jnp.arange(N, dtype=src.dtype)
        s = jnp.concatenate([src, loop])
        d = jnp.concatenate([dst, loop])
        w = jnp.sum(q[s] * k[d], axis=1) / d_k
        wmax = jax.ops.segment_max(w, d, num_segments=N)
        ew = jnp.exp(w - wmax[d])
        denom = jax.ops.segment_sum(ew, d, num_segments=N)
        alpha = ew / denom[d]
        out = jax.ops.segment_sum(alpha[:, None] * x[s], d, num_segments=N)
        return out

    def _L0_mix_ref(x, Wqkv, ln1_g, ln1_b, W1, b1, W2, b2, ln2_g, ln2_b):
        import jax, jax.numpy as jnp
        import numpy as np
        N, F, C, H = (32, 512, 256, 8)
        D = C // H
        EPS_ATTN = 1e-06
        EPS_LN = 1e-05

        def layer_norm(x, g, b):
            mu = jnp.mean(x, axis=-1, keepdims=True)
            var = jnp.var(x, axis=-1, keepdims=True)
            return (x - mu) * jax.lax.rsqrt(var + EPS_LN) * g + b
        n, f, c = x.shape
        qkv = jnp.einsum('nfc,oc->nfo', x, Wqkv)
        q, k, v = jnp.split(qkv, 3, axis=-1)
        q = q.reshape(n, f, H, D)
        k = k.reshape(n, f, H, D)
        v = v.reshape(n, f, H, D)
        q = jax.nn.elu(q) + 1.0
        k = jax.nn.elu(k) + 1.0
        kv = jnp.einsum('nshd,nshm->nhmd', k, v)
        ksum = jnp.sum(k, axis=1)
        z = 1.0 / (jnp.einsum('nlhd,nhd->nlh', q, ksum) + EPS_ATTN)
        t = jnp.einsum('nlhd,nhmd,nlh->nlhm', q, kv, z)
        t = t.reshape(n, f, c)
        x1 = layer_norm(t + x, ln1_g, ln1_b)
        h = jax.nn.gelu(jnp.einsum('nfc,oc->nfo', x1, W1) + b1, approximate=False)
        y = jnp.einsum('nfc,oc->nfo', h, W2) + b2
        return layer_norm(y + x1, ln2_g, ln2_b)

    def _L0_ffn_ref(x, attention_mask, wr, br, w1, b1, w2, b2):
        import jax, jax.numpy as jnp
        import numpy as np
        B, S, D = (8, 512, 256)
        H = 4 * D
        CAPACITY = 0.5
        b, s, d = x.shape
        weights = (jnp.einsum('bsd,do->bso', x, wr) + br)[..., 0]
        k = max(1, int(CAPACITY * s))
        kk = k - 1 if k > 1 else 1
        _, idx = jax.lax.top_k(weights, k)
        sel_idx = idx[:, :kk]
        sel = jnp.take_along_axis(x, sel_idx[:, :, None], axis=1)
        h = jax.nn.gelu(jnp.einsum('bkd,dh->bkh', sel, w1) + b1)
        y = jnp.einsum('bkh,hd->bkd', h, w2) + b2
        w_sel = jnp.take_along_axis(weights, sel_idx, axis=1)
        y = y * w_sel[..., None]
        batch_idx = jnp.arange(b)[:, None]
        processed = jnp.zeros_like(x).at[batch_idx, sel_idx].set(y)
        return processed + x

    def _L1_gnn_ref(x, edge_val, W, b, edge_row, edge_col):
        import jax, jax.numpy as jnp
        import numpy as np
        N_NODES = 12500
        N_EDGES = 400000
        D_IN = 256
        D_OUT = 256
        support = jnp.matmul(x, W)
        gathered = support[edge_col] * edge_val[:, None]
        out = jax.ops.segment_sum(gathered, edge_row, num_segments=x.shape[0])
        return out + b

    def _L1_mix_ref(x, Wq, Wk, Wv, Wm, W1, W2, g1, b1, g2, b2):
        import jax, jax.numpy as jnp
        import numpy as np
        NHEAD = 8
        ATT_EPS = 1e-06
        LN_EPS = 1e-05

        def _layernorm(x, g, b):
            mu = jnp.mean(x, axis=-1, keepdims=True)
            var = jnp.mean(jnp.square(x - mu), axis=-1, keepdims=True)
            return (x - mu) * jax.lax.rsqrt(var + LN_EPS) * g + b
        N, L, C = x.shape
        H = NHEAD
        D = C // H
        q = (x @ Wq).reshape(N, L, H, D)
        k = (x @ Wk).reshape(N, L, H, D)
        v = (x @ Wv).reshape(N, L, H, D)
        Q = jax.nn.elu(q) + 1.0
        K = jax.nn.elu(k) + 1.0
        v = v / L
        KV = jnp.einsum('nshd,nshv->nhdv', K, v)
        Z = 1.0 / (jnp.einsum('nlhd,nhd->nlh', Q, K.sum(axis=1)) + ATT_EPS)
        msg = jnp.einsum('nlhd,nhdv,nlh->nlhv', Q, KV, Z) * L
        msg = msg.reshape(N, L, C) @ Wm
        msg = _layernorm(msg, g1, b1)
        h = jnp.concatenate([x, msg], axis=-1) @ W1
        h = jax.nn.relu(h) @ W2
        msg = _layernorm(h, g2, b2)
        return x + msg

    def _L1_ffn_ref(x, Wr, br, W1, b1, W2, b2, gamma, beta):
        import math
        import jax, jax.numpy as jnp
        import numpy as np
        CAPACITY_FACTOR = 1.25
        TOP_K = 2
        LN_EPS = 1e-05

        def _layer_norm(x, gamma, beta):
            mu = jnp.mean(x, axis=-1, keepdims=True)
            var = jnp.var(x, axis=-1, keepdims=True)
            return (x - mu) * jax.lax.rsqrt(var + LN_EPS) * gamma + beta
        B, S, D = x.shape
        E = Wr.shape[1]
        N = B * S
        K = TOP_K
        logits = jnp.mean(x, axis=1) @ Wr + br
        routing_weights = jax.nn.softmax(logits, axis=-1)
        capacity = float(math.ceil(N * CAPACITY_FACTOR / E))
        expected_loads = routing_weights.sum(axis=0) * (N / B)
        scale = jnp.where(expected_loads > capacity, capacity / expected_loads, 1.0)
        routing_weights = jax.nn.softmax(routing_weights * scale, axis=-1)
        rw_tok = jnp.broadcast_to(routing_weights[:, None, :], (B, S, E)).reshape(N, E)
        top_w, top_i = jax.lax.top_k(rw_tok, K)
        top_w = jax.nn.softmax(top_w, axis=-1)
        xf = x.reshape(N, D)
        h = jax.nn.gelu(jnp.einsum('nd,edf->enf', xf, W1) + b1[:, None, :], approximate=False)
        y = jnp.einsum('enf,efd->end', h, W2) + b2[:, None, :]
        w_dense = jnp.zeros((N, E), x.dtype).at[jnp.arange(N)[:, None], top_i].add(top_w)
        out = jnp.einsum('ne,end->nd', w_dense, y).reshape(B, S, D)
        out = _layer_norm(out + x, gamma, beta)
        return out
    xn = _layernorm(x, axis=-1)
    x = x + _L0_gnn_ref(xn, src, dst, L0_gnn_Wq, L0_gnn_bq, L0_gnn_Wk, L0_gnn_bk) + _L0_mix_ref(xn[None], L0_mix_Wqkv, L0_mix_ln1_g, L0_mix_ln1_b, L0_mix_W1, L0_mix_b1, L0_mix_W2, L0_mix_b2, L0_mix_ln2_g, L0_mix_ln2_b)[0]
    x = x + _L0_ffn_ref(_layernorm(x, axis=-1)[None], L0_ffn_attention_mask, L0_ffn_wr, L0_ffn_br, L0_ffn_w1, L0_ffn_b1, L0_ffn_w2, L0_ffn_b2)[0]
    xn = _layernorm(x, axis=-1)
    x = x + _L1_gnn_ref(xn, edge_weight, L1_gnn_W, L1_gnn_b, src, dst) + _L1_mix_ref(xn[None], L1_mix_Wq, L1_mix_Wk, L1_mix_Wv, L1_mix_Wm, L1_mix_W1, L1_mix_W2, L1_mix_g1, L1_mix_b1, L1_mix_g2, L1_mix_b2)[0]
    x = x + _L1_ffn_ref(_layernorm(x, axis=-1)[None], L1_ffn_Wr, L1_ffn_br, L1_ffn_W1, L1_ffn_b1, L1_ffn_W2, L1_ffn_b2, L1_ffn_gamma, L1_ffn_beta)[0]
    return x

_drawn_inputs = setup_inputs


def setup_inputs(seed=0):
    import zlib

    import numpy as np

    out = dict(_drawn_inputs(seed))
    spreads = {'L0_gnn_bq': (0.0, 0.8),
     'L0_gnn_bk': (0.0, 0.8),
     'L0_mix_ln1_g': (1.0, 0.2),
     'L0_mix_ln1_b': (0.0, 0.1),
     'L0_mix_ln2_g': (1.0, 0.2),
     'L0_mix_ln2_b': (0.0, 0.1),
     'L0_ffn_b1': (0.0, 0.8),
     'L0_ffn_b2': (0.0, 0.508),
     'L1_mix_g1': (1.0, 0.6),
     'L1_mix_b1': (0.0, 0.486),
     'L1_mix_g2': (1.0, 0.2),
     'L1_mix_b2': (0.0, 0.371),
     'L1_ffn_br': (0.0, 0.8),
     'L1_ffn_b1': (0.0, 0.8),
     'L1_ffn_b2': (0.0, 0.696),
     'L1_ffn_gamma': (1.0, 0.545),
     'L1_ffn_beta': (0.0, 0.468)}
    factors = {'L0_mix_Wqkv': 4.917,
     'L0_mix_b1': 4.384,
     'L0_ffn_wr': 4.602,
     'L0_ffn_w1': 4.693,
     'L0_ffn_w2': 3.949,
     'L1_gnn_b': 7.802,
     'L1_mix_Wq': 25.93,
     'L1_mix_Wk': 12.782}
    for name, (base, spread) in spreads.items():
        noise = np.random.default_rng([zlib.crc32(name.encode()), seed]).standard_normal(out[name].shape)
        drawn = base * np.exp(spread * noise) if base else spread * noise
        out[name] = jnp.asarray(drawn.astype(out[name].dtype))
    for name, factor in factors.items():
        out[name] = (out[name] * factor).astype(out[name].dtype)
    return out
```

```python
import concourse.bass as bass
from concourse import mybir
from contextlib import ExitStack
import numpy as np

F32 = mybir.dt.float32
I32 = mybir.dt.int32
BF16 = mybir.dt.bfloat16
ALU = mybir.AluOpType
ACT = mybir.ActivationFunctionType
AX = mybir.AxisListType

P = 128
N, D, E = 6250, 256, 200000
KF = D // P
B = 125
NB = N // B
CH = 2
NC = NB // CH
TOK = CH * B
SUB = 4
G = P * SUB
NG = -(-E // G)
EP = NG * G
EC = EP // P
NS = NG + NB - 1
RING = 4
RW = 3
SMALL = 25
HEADS, HD = 8, 32
HH = P // HD
LN_EPS, ATT_EPS = 1e-5, 1e-6
TOPK = N // 2 - 1
SCATTER = 17
BIG = 1e30


class Steps:

    def __init__(self, eng, sem):
        self.eng, self.sem, self.base, self.n = eng, sem, 0, 0

    def __call__(self, ins):
        ins.then_inc(self.sem, 1)
        self.n += 1
        self.eng.wait_ge(self.sem, self.base + self.n)

    def mark(self, ins):
        ins.then_inc(self.sem, 1)
        self.n += 1

    def all(self):
        self.eng.wait_ge(self.sem, self.base + self.n)


def settle(pool, cell, settled, before):
    pool.wait_ge(settled, before)
    pool.tensor_tensor(cell, cell, cell, ALU.add).then_inc(settled, 1)


class loop:

    def __init__(self, eng, times, steps=None, per=0):
        self.eng, self.times, self.steps, self.per = eng, times, steps, per

    def __enter__(self):
        self.f = self.eng.Fori(0, self.times)
        t = self.f.__enter__()
        if self.steps:
            s = self.steps
            self.before = s.base + s.n
            s.base, s.n = self.before + t * self.per, 0
        return t

    def __exit__(self, *a):
        if self.steps and a[0] is None:
            s = self.steps
            assert s.n == self.per, (s.n, self.per)
            s.base, s.n = self.before + self.times * self.per, 0
        return self.f.__exit__(*a)


def gps_kernel(nc, A, out):
    ctx = ExitStack()
    phase_sems = []

    def sem(name):
        held = nc.semaphore(name)
        phase_sems.append((held, held.__enter__()))
        return phase_sems[-1][1]

    def pool_dma_sem(name):
        return ctx.enter_context(nc.semaphore(name))

    def end_phase():
        with nc.Block() as block:
            @block.sync
            def _(sp):
                for _, s in phase_sems:
                    sp.sem_clear(s)
        while phase_sems:
            phase_sems.pop()[0].__exit__(None, None, None)

    def sb(c, name, shape, dt=F32):
        return c.enter_context(nc.sbuf_tensor(name, shape, dt))

    def pb(c, name, shape=(P, 512), dt=F32):
        return c.enter_context(nc.psum_tensor(name, list(shape), dt))

    def one(ap):
        return ap.rearrange("p a n -> p (a n)")

    def rows(dram):
        return dram.rearrange("(b p) d -> p b d", p=B)

    table0 = nc.dram_tensor("table0", [N, D + SMALL], F32).ap()
    table1 = nc.dram_tensor("table1", [N, D], F32).ap()
    rec_d = [nc.dram_tensor(f"records{i}", [EP, RW], F32).ap() for i in range(2)]

    with ctx:
        ident = sb(ctx, "ident", [P, P])
        ones = sb(ctx, "ones", [P, P])
        lower = sb(ctx, "lower", [P, P])
        iota_n = sb(ctx, "iota_n", [P, B])
        iota_p = sb(ctx, "iota_p", [P, 1])
        eps = sb(ctx, "eps", [P, 1])
        cell = sb(ctx, "cell", [1, RING], I32)
        step_blk = [sb(ctx, f"step_blk{i}", [1, NS], I32) for i in range(2)]
        step_grp = [sb(ctx, f"step_grp{i}", [1, NS], I32) for i in range(2)]
        step_node = [sb(ctx, f"step_node{i}", [P, NS]) for i in range(2)]

        s_c = sem("constants_step")
        with nc.Block() as block:
            @block.gpsimd
            def _(pool):
                st = Steps(pool, s_c)
                st(pool.memset(ident[:, :], 0.0))
                st(pool.affine_select(out=ident[:, :], in_=ident[:, :], compare_op=ALU.not_equal, fill=1.0,
                                      base=0, pattern=[[-1, P]], channel_multiplier=1))
                st(pool.memset(lower[:, :], 1.0))
                st(pool.affine_select(out=lower[:, :], in_=lower[:, :], compare_op=ALU.is_gt, fill=0.0,
                                      base=0, pattern=[[1, P]], channel_multiplier=-1))
                pool.memset(ones[:, :], 1.0)
                pool.memset(eps[:, :], LN_EPS)
                pool.memset(cell[:, :], 0)
                pool.iota(iota_n[:, :], pattern=[[1, B]], base=0, channel_multiplier=0,
                          allow_small_or_imprecise_dtypes=True)
                st(pool.iota(iota_p[:, :], pattern=[[0, 1]], base=0, channel_multiplier=1,
                             allow_small_or_imprecise_dtypes=True))
        end_phase()

        def sort_edges(which, key, other, val):
            t_ = f"sort{which}_"
            with ExitStack() as c:
                keyi = sb(c, t_ + "key", [P, EC], I32)
                othi = sb(c, t_ + "other", [P, EC], I32)
                rec = sb(c, t_ + "rec", [P, EC, RW])
                blki = sb(c, t_ + "blki", [P, EC], I32)
                blkf = sb(c, t_ + "blkf", [P, EC], BF16)
                mask = sb(c, t_ + "mask", [P, EC], BF16)
                one_ = sb(c, t_ + "one", [P, EC], BF16)
                scan = sb(c, t_ + "scan", [P, EC])
                pos = sb(c, t_ + "pos", [P, EC])
                cls = sb(c, t_ + "cls", [P, NB + 1])
                cnt = sb(c, t_ + "cnt", [P, NB + 1])
                tot = sb(c, t_ + "tot", [P, NB + 1])
                cum = sb(c, t_ + "cum", [P, NB + 1])
                base = sb(c, t_ + "base", [P, NB + 1])
                tcol = sb(c, t_ + "tcol", [NB, 1])
                bnd = sb(c, t_ + "bnd", [NB, 1])
                bndi = sb(c, t_ + "bndi", [NB, 1], I32)
                incl = sb(c, t_ + "incl", [P, P])
                ge = sb(c, t_ + "ge", [NB, NS])
                stepf = sb(c, t_ + "stepf", [P, NS])
                iota_s = sb(c, t_ + "iota_s", [P, NS])
                slot_pos = sb(c, t_ + "slot_pos", [P, 2, SCATTER], I32)
                slot_rec = sb(c, t_ + "slot_rec", [P, 2, SCATTER, RW])
                ps = pb(c, t_ + "ps")
                ps2 = pb(c, t_ + "ps2")
                loaded, own, count_done, sums_done = (sem(t_ + x) for x in ("loaded", "own", "counted", "summed"))
                tcol_done, cum_done, bnd_done, step_done = (sem(t_ + x) for x in ("tcol", "cumsum", "bounds", "steps"))
                filled, pool_c, pos_done, settled = (sem(t_ + x) for x in ("filled", "iota", "positions", "settled"))
                sent = [pool_dma_sem(t_ + f"sent{h}") for h in range(2)]

                with nc.Block() as block:
                    @block.sync
                    def _(sp):
                        sp.dma_start(keyi[:, :], key).then_inc(loaded, 16)
                        sp.dma_start(othi[:, :], other).then_inc(loaded, 16)
                        sp.dma_start(scan[:, :], val).then_inc(loaded, 16)

                    @block.gpsimd
                    def _(pool):
                        pool.iota(cls[:, :], pattern=[[1, NB + 1]], base=0, channel_multiplier=0,
                                  allow_small_or_imprecise_dtypes=True).then_inc(pool_c, 1)
                        pool.iota(iota_s[:, :], pattern=[[1, NS]], base=0, channel_multiplier=0,
                                  allow_small_or_imprecise_dtypes=True).then_inc(pool_c, 1)
                        pool.tensor_tensor(incl[:, :], lower[:, :], ident[:, :], ALU.add).then_inc(pool_c, 1)

                    @block.vector
                    def _(dve):
                        st = Steps(dve, own)
                        dve.memset(one_[:, :], 1.0)
                        st(dve.memset(pos[:, :], -1.0))
                        dve.wait_ge(pool_c, 3)
                        dve.wait_ge(loaded, 48)
                        st(dve.tensor_scalar(blki[:, :], keyi[:, :], -float(B // 2), 1.0 / B, ALU.add, ALU.mult))
                        st.mark(dve.tensor_copy(blkf[:, :], blki[:, :]))
                        st.mark(dve.tensor_copy(rec[:, :, 0], keyi[:, :]))
                        st.mark(dve.tensor_scalar(rec[:, :, 1], othi[:, :], float(N - 1), None, ALU.min))
                        st(dve.tensor_copy(rec[:, :, 2], scan[:, :]))
                        with loop(dve, NB + 1, st, 1) as b:
                            st(dve.tensor_scalar(mask[:, :], blkf[:, :], cls[:, bass.ds(b, 1)], 0.0,
                                                 ALU.is_equal, ALU.add, accum_out=cnt[:, bass.ds(b, 1)]))
                        dve.tensor_copy(tot[:, :], cnt[:, :]).then_inc(count_done, 1)
                        dve.wait_ge(sums_done, 1)
                        st(dve.tensor_copy(tot[:, :], ps[:, 64:64 + NB + 1]))
                        st(dve.tensor_tensor_scan(cum[:, :], ones[:, 0:NB + 1], tot[:, :], 0.0, ALU.mult, ALU.add))
                        st(dve.tensor_tensor(cum[:, :], cum[:, :], tot[:, :], ALU.subtract))
                        st(dve.tensor_tensor(base[:, :], cum[:, :], ps[:, 0:NB + 1], ALU.add))
                        dve.tensor_copy(tcol[:, :], ps[0:NB, 128:129]).then_inc(tcol_done, 1)
                        dve.wait_ge(cum_done, 1)
                        st(dve.tensor_scalar(bndi[:, :], ps2[0:NB, 0:1], 1.0 / G, 0.5 - 0.5 / G, ALU.mult, ALU.add))
                        st(dve.tensor_copy(bnd[:, :], bndi[:, :]))
                        st(dve.tensor_scalar(bnd[:, :], bnd[:, :], 1.0, iota_p[0:NB, 0:1], ALU.max, ALU.add))
                        dve.tensor_scalar(ge[:, :], iota_s[0:NB, :], bnd[:, 0:1], None, ALU.is_ge).then_inc(bnd_done, 1)
                        dve.wait_ge(step_done, 1)
                        st(dve.tensor_scalar(stepf[:, :], ps2[:, 0:NS], float(NB - 1), None, ALU.min))
                        st.mark(dve.tensor_scalar(step_node[which][:, :], stepf[:, :], float(B), None, ALU.mult))
                        st.mark(dve.tensor_copy(step_blk[which][:, :], stepf[0:1, :]))
                        st(dve.tensor_tensor(iota_s[:, :], iota_s[:, :], stepf[:, :], ALU.subtract))
                        st(dve.tensor_scalar(iota_s[:, :], iota_s[:, :], float(NG - 1), None, ALU.min))
                        st(dve.tensor_copy(step_grp[which][:, :], iota_s[0:1, :]))
                        with loop(dve, NB + 1, st, 4) as b:
                            st(dve.tensor_scalar(mask[:, :], blkf[:, :], cls[:, bass.ds(b, 1)], None, ALU.is_equal))
                            st(dve.tensor_tensor_scan(scan[:, :], one_[:, :], mask[:, :], base[:, bass.ds(b, 1)],
                                                      ALU.mult, ALU.add))
                            st(dve.tensor_tensor(scan[:, :], scan[:, :], mask[:, :], ALU.mult))
                            st(dve.tensor_tensor(pos[:, :], pos[:, :], scan[:, :], ALU.add))
                        dve.tensor_copy(blki[:, :], pos[:, :]).then_inc(pos_done, 1)

                    @block.tensor
                    def _(pe):
                        pe.wait_ge(count_done, 1)
                        pe.matmul(ps[:, 0:NB + 1], lower[:, :], tot[:, :], start=True, stop=True)
                        pe.matmul(ps[:, 64:64 + NB + 1], ones[:, :], tot[:, :], start=True, stop=True)
                        pe.matmul(ps[0:NB, 128:129], tot[:, 0:NB], ones[:, 0:1], start=True, stop=True).then_inc(sums_done, 1)
                        pe.wait_ge(tcol_done, 1)
                        pe.matmul(ps2[0:NB, 0:1], incl[0:NB, 0:NB], tcol[:, :], start=True, stop=True).then_inc(cum_done, 1)
                        pe.wait_ge(bnd_done, 1)
                        pe.matmul(ps2[:, 0:NS], ones[0:NB - 1, :], ge[0:NB - 1, :], start=True, stop=True).then_inc(step_done, 1)

                with nc.Block() as block:
                    @block.scalar
                    def _(act):
                        with loop(act, EC // (2 * SCATTER)) as t:
                            for h in range(2):
                                at = t * (2 * SCATTER) + h * SCATTER
                                act.wait_ge(sent[h], t * (16 * SCATTER))
                                act.activation(slot_rec[:, h, :, :], rec[:, bass.ds(at, SCATTER), :], ACT.Copy)
                                act.activation(slot_pos[:, h, :], blki[:, bass.ds(at, SCATTER)], ACT.Copy).then_inc(filled, 1)

                    @block.gpsimd
                    def _(pool):
                        with loop(pool, EC // (2 * SCATTER)) as t:
                            for h in range(2):
                                pool.wait_ge(filled, t * 2 + h + 1)
                                settle(pool, cell[0:1, 0:1], settled, t * 2 + h)
                                for j in range(SCATTER):
                                    pool.indirect_dma_start(
                                        out=rec_d[which],
                                        out_offset=bass.IndirectOffsetOnAxis(ap=slot_pos[:, h, j:j + 1], axis=0),
                                        in_=slot_rec[:, h, j, :], in_offset=None).then_inc(sent[h], 16)
                        for h in range(2):
                            pool.wait_ge(sent[h], (EC // (2 * SCATTER)) * 16 * SCATTER)

        def layer_norm(name, src, dst, affine=None, into=None, plus=None, store=None):
            with ExitStack() as c:
                stats = sb(c, name + "_stats", [B, NB, 6])
                mean = sb(c, name + "_mean", [B, NB])
                half = sb(c, name + "_half", [B, NB])
                var = sb(c, name + "_var", [B, NB])
                rstd = sb(c, name + "_rstd", [B, NB])
                gain = sb(c, name + "_gain", [B, D])
                offset = sb(c, name + "_offset", [B, D])
                own, var_done, sd_done, loaded, plus_done = (
                    sem(name + x) for x in ("_own", "_var", "_sd", "_loaded", "_plus"))
                stored = sem(name + "_stored")
                with nc.Block() as block:
                    @block.sync
                    def _(sp):
                        if affine:
                            sp.dma_start(gain[:, :], affine[0].partition_broadcast(B)).then_inc(loaded, 16)
                            sp.dma_start(offset[:, :], affine[1].partition_broadcast(B)).then_inc(loaded, 16)

                    if plus is not None:
                        @block.gpsimd
                        def _(pool):
                            with loop(pool, NB) as b:
                                pool.tensor_tensor(into[:, bass.ds(b, 1), :], into[:, bass.ds(b, 1), :],
                                                   plus[0:B, bass.ds(b, 1), :], ALU.add).then_inc(plus_done, 1)

                    @block.scalar
                    def _(act):
                        act.wait_ge(var_done, 1)
                        act.activation(rstd[:, :], var[:, :], ACT.Sqrt, bias=eps[0:B, 0:1]).then_inc(sd_done, 1)

                    @block.vector
                    def _(dve):
                        st = Steps(dve, own)
                        with loop(dve, NB, st, 1) as b:
                            st.mark(dve.bn_stats(one(stats[:, bass.ds(b, 1), :]), one(src[0:B, bass.ds(b, 1), :])))
                        st.all()
                        me, mo, qe, qo = (stats[:, :, i] for i in (1, 4, 2, 5))
                        st.mark(dve.tensor_tensor(mean[:, :], me, mo, ALU.add))
                        st.mark(dve.tensor_tensor(half[:, :], me, mo, ALU.subtract))
                        st(dve.tensor_tensor(var[:, :], qe, qo, ALU.add))
                        st.mark(dve.tensor_scalar(mean[:, :], mean[:, :], 0.5, None, ALU.mult))
                        st(dve.scalar_tensor_tensor(half[:, :], half[:, :], 0.25, half[:, :], ALU.mult, ALU.mult))
                        dve.scalar_tensor_tensor(var[:, :], var[:, :], 1.0 / D, half[:, :], ALU.mult, ALU.add).then_inc(var_done, 1)
                        dve.wait_ge(sd_done, 1)
                        st(dve.reciprocal(rstd[:, :], rstd[:, :]))
                        if affine:
                            dve.wait_ge(loaded, 32)
                            per = 3 if into is not None else 2
                            with loop(dve, NB, st, per) as b:
                                s, r = src[0:B, bass.ds(b, 1), :], bass.ds(b, 1)
                                st(dve.scalar_tensor_tensor(one(s), one(s), mean[:, r], gain[:, :], ALU.subtract, ALU.mult))
                                st(dve.scalar_tensor_tensor(one(s), one(s), rstd[:, r], offset[:, :], ALU.mult, ALU.add))
                                if into is not None:
                                    if plus is not None:
                                        dve.wait_ge(plus_done, b + 1)
                                    st.mark(dve.tensor_tensor(one(into[:, r, :]), one(into[:, r, :]), one(s), ALU.add))
                            st.all()
                        else:
                            with loop(dve, NB, st, 1) as b:
                                r = bass.ds(b, 1)
                                st.mark(dve.tensor_scalar(one(dst[0:B, r, :]), one(src[0:B, r, :]), mean[:, r], rstd[:, r],
                                                          ALU.subtract, ALU.mult))
                            st.all()

        def transposed(c, name, n_src):
            stage = sb(c, name + "_stage", [B, n_src, CH, D])
            xT = sb(c, name + "_xT", [P, n_src * KF, TOK])
            psT = [pb(c, f"{name}_psT{i}") for i in range(n_src)]
            staged, turned, xT_done = (sem(name + x) for x in ("_staged", "_turned", "_xT"))

            def pool_part(pool, srcs, k):
                for i, src in enumerate(srcs):
                    pool.wait_ge(turned, k)
                    pool.tensor_copy(stage[:, i, :, :], src[0:B, bass.ds(k * CH, CH), :]).then_inc(staged, 1)

            def pe_part(pe, k):
                pe.wait_ge(staged, k * n_src + n_src)
                for i in range(n_src):
                    for f in range(KF):
                        for b in range(CH):
                            at = (f * CH + b) * B
                            last = pe.transpose(psT[i][:, at:at + B], stage[:, i, b, f * P:(f + 1) * P], ident[0:B, 0:B])
                last.then_inc(turned, 1)
                pe.wait_ge(xT_done, k * n_src + n_src)

            def act_part(act, k):
                act.wait_ge(turned, k + 1)
                for i in range(n_src):
                    act.activation(xT[:, i * KF:(i + 1) * KF, :].rearrange("p f t -> p (f t)"),
                                   psT[i][:, 0:KF * TOK], ACT.Copy).then_inc(xT_done, 1)

            return xT, pool_part, pe_part, act_part

        def mlp(name, srcs, experts, width, func, per, final, setup=None, wsrc=None):
            nk, nf = KF * len(srcs), width // P
            with ExitStack() as c:
                xT, pool_part, pe_part, act_part = transposed(c, name, len(srcs))
                w1 = [sb(c, f"{name}_w1_{e}", [P, nk, width]) for e in range(len(experts))]
                w2 = [sb(c, f"{name}_w2_{e}", [P, nf, D]) for e in range(len(experts))]
                b1 = [sb(c, f"{name}_b1_{e}", [P, nf]) for e in range(len(experts))]
                b2 = [sb(c, f"{name}_b2_{e}", [B, D]) for e in range(len(experts))]
                hT = sb(c, name + "_hT", [P, len(experts) * nf, TOK])
                tmp = sb(c, name + "_tmp", [B, CH, D])
                psH = [pb(c, f"{name}_psH{i}") for i in range(2)]
                psY = [pb(c, f"{name}_psY{e}") for e in range(len(experts))]
                loaded, h_mm, h_done, y_mm, fin, own = (
                    sem(name + x) for x in ("_loaded", "_h_mm", "_h", "_y_mm", "_fin", "_own"))
                total = len(experts) * nf
                with nc.Block() as block:
                    @block.sync
                    def _(sp):
                        for e, w in enumerate(experts):
                            for dst, src in ((w1[e][:, :, :], w[0]), (b1[e][:, :], w[1]), (w2[e][:, :, :], w[2]), (b2[e][:, :], w[3])):
                                if src is not None:
                                    src = src(sp, e) if callable(src) else src
                                    sp.dma_start(dst, src).then_inc(loaded, 16)
                    n_loads = 16 * sum(x is not None for w in experts for x in w)

                    @block.gpsimd
                    def _(pool):
                        with loop(pool, NC) as k:
                            pool_part(pool, srcs, k)

                    @block.tensor
                    def _(pe):
                        pe.wait_ge(loaded, n_loads)
                        with loop(pe, NC) as k:
                            pe_part(pe, k)
                            for i in range(total):
                                e, f = divmod(i, nf)
                                if i >= 2:
                                    pe.wait_ge(h_done, k * total + i - 1)
                                for j in range(nk):
                                    last = pe.matmul(psH[i % 2][:, 0:TOK], w1[e][:, j, f * P:(f + 1) * P], xT[:, j, :],
                                                     start=(j == 0), stop=(j == nk - 1))
                                last.then_inc(h_mm, 1)
                            pe.wait_ge(fin, k)
                            pe.wait_ge(h_done, k * total + total)
                            for e in range(len(experts)):
                                for b in range(CH):
                                    for f in range(nf):
                                        last = pe.matmul(psY[e][0:B, b * D:(b + 1) * D],
                                                         hT[:, e * nf + f, b * B:(b + 1) * B], w2[e][:, f, :],
                                                         start=(f == 0), stop=(f == nf - 1))
                            last.then_inc(y_mm, 1)

                    @block.scalar
                    def _(act):
                        act.wait_ge(loaded, n_loads)
                        with loop(act, NC) as k:
                            act_part(act, k)
                            for i in range(total):
                                e, f = divmod(i, nf)
                                act.wait_ge(h_mm, k * total + i + 1)
                                kw = {} if experts[e][1] is None else {"bias": b1[e][:, f:f + 1]}
                                act.activation(hT[:, i, :], psH[i % 2][:, 0:TOK], func, **kw).then_inc(h_done, 1)

                    @block.vector
                    def _(dve):
                        st = Steps(dve, own)
                        dve.wait_ge(loaded, n_loads)
                        if setup:
                            setup(dve, st, b2)
                        with loop(dve, NC, st, per) as k:
                            dve.wait_ge(y_mm, k + 1)
                            final(dve, st, k, [p[0:B, :].rearrange("p (b d) -> p b d", b=CH) for p in psY], b2, tmp).then_inc(fin, 1)

        def linear(name, src, w_dram, bias, per, final):
            with ExitStack() as c:
                xT, pool_part, pe_part, act_part = transposed(c, name, 1)
                w = sb(c, name + "_w", [P, KF, D])
                b2 = sb(c, name + "_b", [B, D])
                psY = pb(c, name + "_psY")
                loaded, y_mm, fin, own = (sem(name + x) for x in ("_loaded", "_y_mm", "_fin", "_own"))
                with nc.Block() as block:
                    @block.sync
                    def _(sp):
                        sp.dma_start(w[:, :, :], w_dram).then_inc(loaded, 16)
                        if bias is not None:
                            sp.dma_start(b2[:, :], bias.partition_broadcast(B)).then_inc(loaded, 16)
                    n_loads = 32 if bias is not None else 16

                    @block.gpsimd
                    def _(pool):
                        with loop(pool, NC) as k:
                            pool_part(pool, [src], k)

                    @block.tensor
                    def _(pe):
                        pe.wait_ge(loaded, n_loads)
                        with loop(pe, NC) as k:
                            pe_part(pe, k)
                            pe.wait_ge(fin, k)
                            for b in range(CH):
                                for f in range(KF):
                                    last = pe.matmul(psY[0:B, b * D:(b + 1) * D], xT[:, f, b * B:(b + 1) * B], w[:, f, :],
                                                     start=(f == 0), stop=(f == KF - 1))
                            last.then_inc(y_mm, 1)

                    @block.scalar
                    def _(act):
                        with loop(act, NC) as k:
                            act_part(act, k)

                    @block.vector
                    def _(dve):
                        st = Steps(dve, own)
                        dve.wait_ge(loaded, n_loads)
                        with loop(dve, NC, st, per) as k:
                            dve.wait_ge(y_mm, k + 1)
                            final(dve, st, k, psY[0:B, :].rearrange("p (b d) -> p b d", b=CH), b2).then_inc(fin, 1)

        def attention_sums(c0, name, wkv_dram, edge=None, table=None):
            kvd = sb(c0, name + "_kvd", [P, KF, P + HH])
            with ExitStack() as c:
                xT, pool_part, pe_part, act_part = transposed(c, name, 1)
                wkv = sb(c, name + "_wkv", [P, KF, 2 * D])
                k_sb = sb(c, name + "_k", [B, CH, D])
                e_sb = sb(c, name + "_e", [B, CH, D])
                v_sb = sb(c, name + "_v", [B, CH, KF, P + 1])
                kva = sb(c, name + "_kva", [P, KF * (P + 1)])
                psKV = [pb(c, f"{name}_psKV{i}") for i in range(CH)]
                psA = pb(c, name + "_psA")
                if edge:
                    wqk = sb(c, name + "_wqk", [P, KF, 2 * SMALL])
                    bqk = sb(c, name + "_bqk", [1, 2 * SMALL])
                    bk = sb(c, name + "_bk", [SMALL, 1])
                    flat = U[:, :, :].rearrange("p b d -> p (b d)")
                    q_all = flat[:, 0:NB * SMALL].rearrange("p (b n) -> p b n", n=SMALL)
                    k_all = flat[:, NB * SMALL:2 * NB * SMALL].rearrange("p (b n) -> p b n", n=SMALL)
                    psQ = pb(c, name + "_psQ")
                    psK = pb(c, name + "_psK")
                loaded, kv_mm, e_done, k_done, v_done, a_mm, a_done, own, stored, setup = (
                    sem(name + x) for x in ("_loaded", "_kv_mm", "_e", "_k", "_v", "_a_mm", "_a", "_own", "_stored", "_setup"))
                qk_mm, qk_done, low_done = sem(name + "_qk_mm"), sem(name + "_qk"), sem(name + "_low")
                with nc.Block() as block:
                    @block.sync
                    def _(sp):
                        sp.dma_start(wkv[:, :, :], wkv_dram).then_inc(loaded, 16)
                        if edge:
                            sp.dma_start(wqk[:, :, :], edge["wqk"]).then_inc(loaded, 16)
                            sp.dma_start(bqk[:, :], edge["bqk"]).then_inc(loaded, 16)
                            sp.dma_start(bk[:, :], edge["bk"]).then_inc(loaded, 16)
                        for i in range(5):
                            n = NB // 5
                            sp.dma_start(rows(table)[:, i * n:(i + 1) * n, 0:D], XN[0:B, i * n:(i + 1) * n, :]).then_inc(stored, 16)
                        if edge:
                            sp.wait_ge(qk_done, 3 * NC)
                            sp.dma_start(rows(table)[:, :, D:D + SMALL], q_all[:, :, :]).then_inc(stored, 16)
                        sp.wait_ge(stored, 16 * (6 if edge else 5))

                    n_loads = 64 if edge else 16

                    @block.gpsimd
                    def _(pool):
                        with loop(pool, NC) as k:
                            pool_part(pool, [XN], k)

                    @block.tensor
                    def _(pe):
                        pe.wait_ge(loaded, n_loads)
                        pe.wait_ge(setup, 1)
                        with loop(pe, NC) as k:
                            pe_part(pe, k)
                            for b in range(CH):
                                for f in range(KF):
                                    last = pe.matmul(psKV[b][0:B, :], xT[:, f, b * B:(b + 1) * B], wkv[:, f, :],
                                                     start=(f == 0), stop=(f == KF - 1))
                            last.then_inc(kv_mm, 1)
                            if edge:
                                for b in range(CH):
                                    o = psQ[0:B, b * 64:b * 64 + 2 * SMALL]
                                    pe.matmul(o, ones[0:1, 0:B], bqk[:, :], start=True, stop=False)
                                    for f in range(KF):
                                        pe.matmul(o, xT[:, f, b * B:(b + 1) * B], wqk[:, f, :], start=False, stop=(f == KF - 1))
                                for f in range(KF):
                                    last = pe.matmul(psK[0:SMALL, 0:TOK], wqk[:, f, SMALL:2 * SMALL], xT[:, f, :],
                                                     start=(f == 0), stop=(f == KF - 1))
                                last.then_inc(qk_mm, 1)
                            pe.wait_ge(k_done, k + 1)
                            pe.wait_ge(v_done, k * CH + CH)
                            pe.wait_ge(a_done, k)
                            if edge:
                                pe.wait_ge(qk_done, 3 * k + 3)
                            for f in range(KF):
                                for b in range(CH):
                                    last = pe.matmul(psA[:, f * (P + 1):(f + 1) * (P + 1)], k_sb[:, b, f * P:(f + 1) * P],
                                                     v_sb[:, b, f, :], start=(b == 0), stop=(b == CH - 1))
                            last.then_inc(a_mm, 1)

                    @block.scalar
                    def _(act):
                        act.wait_ge(loaded, n_loads)
                        act.wait_ge(setup, 1)
                        with loop(act, NC) as k:
                            act_part(act, k)
                            act.wait_ge(low_done, k + 1)
                            for b in range(CH):
                                act.activation(v_sb[:, b, :, 0:P], psKV[b][0:B, D:2 * D].rearrange("p (f d) -> p f d", f=KF),
                                               ACT.Copy).then_inc(v_done, 1)
                            act.activation(e_sb[:, :, :], e_sb[:, :, :], ACT.Exp).then_inc(e_done, 1)
                            if edge:
                                act.wait_ge(qk_mm, k + 1)
                                q = psQ[0:B, 0:64 * CH].rearrange("p (b n) -> p b n", b=CH)
                                act.activation(q_all[:, bass.ds(k * CH, CH), :], q[:, :, 0:SMALL], ACT.Tanh).then_inc(qk_done, 1)
                                act.activation(k_all[:, bass.ds(k * CH, CH), :], q[:, :, SMALL:2 * SMALL], ACT.Copy).then_inc(qk_done, 1)
                                act.activation(edge["kT"][:, bass.ds(k * CH, CH), :], psK[0:SMALL, 0:TOK].rearrange("p (b n) -> p b n", b=CH),
                                               ACT.Identity, bias=bk[:, 0:1]).then_inc(qk_done, 1)

                    @block.vector
                    def _(dve):
                        st = Steps(dve, own)
                        dve.memset(kvd[:, :, :], 0.0)
                        st(dve.memset(kva[:, :], 0.0))
                        dve.memset(v_sb[:, :, :, P:P + 1], 1.0).then_inc(setup, 1)
                        with loop(dve, NC) as k:
                            dve.wait_ge(kv_mm, k + 1)
                            for b in range(CH):
                                last = dve.tensor_scalar(e_sb[:, b, :], psKV[b][0:B, 0:D], 0.0, None, ALU.min)
                            last.then_inc(low_done, 1)
                            dve.wait_ge(e_done, k + 1)
                            for b in range(CH):
                                last = dve.scalar_tensor_tensor(k_sb[:, b, :], psKV[b][0:B, 0:D], 0.0, e_sb[:, b, :], ALU.max, ALU.add)
                            last.then_inc(k_done, 1)
                            dve.wait_ge(a_mm, k + 1)
                            dve.wait_ge(a_done, k)
                            dve.tensor_tensor(kva[:, :], kva[:, :], psA[:, 0:KF * (P + 1)], ALU.add).then_inc(a_done, 1)
                        dve.wait_ge(a_done, NC)
                        for f in range(KF):
                            for h in range(HH):
                                r = slice(h * HD, (h + 1) * HD)
                                dve.tensor_copy(kvd[r, f, h * HD:(h + 1) * HD], kva[r, f * (P + 1) + h * HD:f * (P + 1) + (h + 1) * HD])
                                dve.tensor_copy(kvd[r, f, P + h:P + h + 1], kva[r, f * (P + 1) + P:f * (P + 1) + P + 1])
                        if edge:
                            dve.wait_ge(qk_done, 3 * NC)
                            st(dve.tensor_tensor(k_all[:, :, :], k_all[:, :, :], q_all[:, :, :], ALU.mult))
                            dve.tensor_reduce(edge["m"][:, :], k_all[:, :, :], AX.X, ALU.add)
                            dve.memset(edge["l"][:, :], 1.0)
            return kvd

        def attention_rows(name, wq_dram, kvd, residual):
            with ExitStack() as c:
                xT, pool_part, pe_part, act_part = transposed(c, name, 1)
                wq = sb(c, name + "_wq", [P, KF, D])
                e_sb = sb(c, name + "_e", [P, KF, TOK])
                qT = sb(c, name + "_qT", [P, KF, TOK])
                z = sb(c, name + "_z", [B, CH, HEADS])
                psQ = [pb(c, f"{name}_psQ{i}") for i in range(KF)]
                psM = [pb(c, f"{name}_psM{i}") for i in range(CH)]
                loaded, q_mm, low_done, e_done, q_done, m_mm, fin, own = (
                    sem(name + x) for x in ("_loaded", "_q_mm", "_low", "_e", "_q", "_m_mm", "_fin", "_own"))
                with nc.Block() as block:
                    @block.sync
                    def _(sp):
                        sp.dma_start(wq[:, :, :], wq_dram).then_inc(loaded, 16)

                    @block.gpsimd
                    def _(pool):
                        with loop(pool, NC) as k:
                            pool_part(pool, [XN], k)

                    @block.tensor
                    def _(pe):
                        pe.wait_ge(loaded, 16)
                        with loop(pe, NC) as k:
                            pe_part(pe, k)
                            for f in range(KF):
                                for j in range(KF):
                                    last = pe.matmul(psQ[f][:, 0:TOK], wq[:, j, f * P:(f + 1) * P], xT[:, j, :],
                                                     start=(j == 0), stop=(j == KF - 1))
                            last.then_inc(q_mm, 1)
                            pe.wait_ge(q_done, k + 1)
                            pe.wait_ge(fin, k)
                            for b in range(CH):
                                for f in range(KF):
                                    last = pe.matmul(psM[b][0:B, f * (P + HH):(f + 1) * (P + HH)], qT[:, f, b * B:(b + 1) * B],
                                                     kvd[:, f, :], start=True, stop=True)
                            last.then_inc(m_mm, 1)

                    @block.scalar
                    def _(act):
                        with loop(act, NC) as k:
                            act_part(act, k)
                            act.wait_ge(low_done, k + 1)
                            act.activation(e_sb[:, :, :], e_sb[:, :, :], ACT.Exp).then_inc(e_done, 1)

                    @block.vector
                    def _(dve):
                        st = Steps(dve, own)
                        with loop(dve, NC, st, 2 + CH if residual else 2) as k:
                            dve.wait_ge(q_mm, k + 1)
                            for f in range(KF):
                                last = dve.tensor_scalar(e_sb[:, f, :], psQ[f][:, 0:TOK], 0.0, None, ALU.min)
                            last.then_inc(low_done, 1)
                            dve.wait_ge(e_done, k + 1)
                            for f in range(KF):
                                last = dve.scalar_tensor_tensor(qT[:, f, :], psQ[f][:, 0:TOK], 0.0, e_sb[:, f, :], ALU.max, ALU.add)
                            last.then_inc(q_done, 1)
                            dve.wait_ge(m_mm, k + 1)
                            msg = [psM[b][0:B, 0:KF * (P + HH)].rearrange("p (f n) -> p f n", f=KF) for b in range(CH)]
                            for b in range(CH):
                                last = dve.tensor_scalar(z[:, b, :].rearrange("p (f h) -> p f h", f=KF), msg[b][:, :, P:P + HH],
                                                         ATT_EPS, None, ALU.add)
                            st(last)
                            st(dve.reciprocal(z[:, :, :], z[:, :, :]))
                            for b in range(CH):
                                u = one(U[:, bass.ds(k * CH + b, 1), :])
                                n = dve.tensor_tensor(u.rearrange("p (f h d) -> p f h d", f=KF, h=HH),
                                                      msg[b][:, :, 0:P].rearrange("p f (h d) -> p f h d", h=HH),
                                                      z[:, b, :].rearrange("p (f h) -> p f h", f=KF).unsqueeze(3).broadcast_to([B, KF, HH, HD]), ALU.mult)
                                if residual:
                                    st(n)
                                    n = dve.tensor_tensor(u, u, one(XN[0:B, bass.ds(k * CH + b, 1), :]), ALU.add)
                            n.then_inc(fin, 1)


        def edge_walk(name, which, table, width, own_part):
            W = width
            rec_t, idx = own_part["rec"], own_part["idx"]
            rows_t = XN[:, :, :].rearrange("p b d -> p (b d)")[:, 0:RING * SUB * W].rearrange("p (r s w) -> p r s w", r=RING, s=SUB)
            rec_v = rec_d[which].rearrange("(g p s) w -> g p (s w)", p=P, s=SUB)
            rec_ready = [sem(f"{name}_rec{s}") for s in range(RING)]
            rec_free = [sem(f"{name}_rec_free{s}") for s in range(RING)]
            idx_ready = [sem(f"{name}_idx{s}") for s in range(RING)]
            got = [pool_dma_sem(f"{name}_got{s}") for s in range(RING)]
            used = [sem(f"{name}_used{s}") for s in range(RING)]
            settled = sem(name + "_settled")

            def sp_part(sp):
                with loop(sp, NS // RING) as t:
                    for s in range(RING):
                        g = sp.value_load(step_grp[which][0:1, bass.ds(t * RING + s, 1)], min_val=0, max_val=NG - 1)
                        sp.wait_ge(rec_free[s], t)
                        sp.wait_ge(idx_ready[s], t)
                        sp.dma_start(rec_t[:, s, :, :].rearrange("p s w -> p (s w)"),
                                     rec_v[bass.ds(g, 1), :, :].rearrange("g p w -> (g p) w")).then_inc(rec_ready[s], 16)

            def act_idx(act, t, s):
                act.wait_ge(rec_ready[s], t * 16 + 16)
                act.wait_ge(got[s], t * (16 * SUB))
                act.activation(idx[:, s, :], rec_t[:, s, :, 1], ACT.Copy).then_inc(idx_ready[s], 1)

            def pool_part(pool):
                with loop(pool, NS // RING) as t:
                    for s in range(RING):
                        pool.wait_ge(idx_ready[s], t + 1)
                        pool.wait_ge(used[s], t)
                        settle(pool, cell[0:1, 0:1], settled, t * RING + s)
                        for j in range(SUB):
                            pool.indirect_dma_start(out=rows_t[:, s, j, :], out_offset=None, in_=table,
                                                    in_offset=bass.IndirectOffsetOnAxis(ap=idx[:, s, j:j + 1], axis=0)).then_inc(got[s], 16)

            return rows_t, rec_ready, rec_free, got, used, sp_part, act_idx, pool_part

        def each_step(eng, steps, per, first, body):
            first(0, 0)
            T = NS // RING
            with loop(eng, T - 1, steps, per) as t:
                for s in range(RING):
                    body(t, s, False)
            for s in range(RING):
                body(T - 1, s, True)

        def after(t, s, n=1):
            return (t, s + n) if s + n < RING else (t + 1, s + n - RING)

        def edge_softmax(edge):
            name, W = "gat", D + SMALL
            kT, m, l = edge["kT"], edge["m"], edge["l"]
            SC = 1.0 / float(np.sqrt(SMALL))
            with ExitStack() as c:
                rec_t = sb(c, name + "_rec", [P, RING, SUB, RW])
                idx = sb(c, name + "_idx", [P, RING, SUB], I32)
                node = sb(c, name + "_node", [P, NS])
                kTs = sb(c, name + "_kTs", [SMALL, 2, B])
                free = RING * SUB * W

                def room(p, n):
                    nonlocal free
                    free += 2 * n
                    return XN[0:p, :, :].rearrange("p b d -> p (b d)")[:, free - 2 * n:free].rearrange("p (a n) -> p a n", a=2)

                qT, S, pT, pE = room(SMALL, G), room(B, G), room(B, G), room(P, SUB * B)
                pen = sb(c, name + "_pen", [B, G])
                mx, mo, mn, nm, df, sc, rs = (sb(c, f"{name}_{x}", [B, 2]) for x in ("mx", "mo", "mn", "nm", "df", "sc", "rs"))
                psA, psB, psP = pb(c, name + "_psA"), pb(c, name + "_psB"), pb(c, name + "_psP")
                psS = [pb(c, f"{name}_psS{i}") for i in range(2)]
                psE = [pb(c, f"{name}_psE{i}") for i in range(2)]
                rows_t, rec_ready, rec_free, got, used, sp_part, act_idx, pool_part = edge_walk(
                    name, 0, table0, W, {"rec": rec_t, "idx": idx})
                qk_done, pen_done, s_mm, s_done, e_done, p_turned, p_done, own, ready = (
                    sem(f"{name}_{x}") for x in ("qk", "pen", "s_mm", "s", "e", "p_turned", "p", "own", "ready"))
                added = [sem(f"{name}_added{i}") for i in range(2)]
                step = lambda t, s: t * RING + s

                with nc.Block() as block:
                    @block.vector
                    def _(dve):
                        dve.tensor_copy(U[:, :, :], XN[0:B, :, :])
                        dve.tensor_scalar(node[:, :], step_node[0][:, :], iota_p[:, 0:1], None, ALU.add)

                with nc.Block() as block:
                    @block.sync
                    def _(sp):
                        sp_part(sp)

                    @block.gpsimd
                    def _(pool):
                        pool_part(pool)

                    @block.tensor
                    def _(pe):
                        def scores(t, s):
                            x, d = step(t, s), s % 2
                            pe.wait_ge(got[s], t * (16 * SUB) + 16 * SUB)
                            pe.wait_ge(rec_ready[s], t * 16 + 16)
                            if not (isinstance(t, int) and t == 0 and s == 0):
                                pe.wait_ge(qk_done, x)
                                pe.wait_ge(pen_done, x)
                            for j in range(SUB):
                                pe.transpose(psA[0:SMALL, j * P:(j + 1) * P], rows_t[:, s, j, D:W], ident[:, :])
                            for j in range(SUB):
                                last = pe.transpose(psB[0:B, j * P:(j + 1) * P],
                                                    rec_t[:, s, j, 0:1].broadcast_to([P, B]), ident[:, :])
                            last.then_inc(rec_free[s], 1)
                            pe.wait_ge(qk_done, x + 1)
                            if not (isinstance(t, int) and t == 0 and s == 0):
                                pe.wait_ge(s_done, x - 1)
                            pe.matmul(psS[d][0:B, :], kTs[:, d, :], qT[:, d, :], start=True, stop=True).then_inc(s_mm, 1)

                        def sums(t, s):
                            x, d = step(t, s), s % 2
                            pe.wait_ge(e_done, x + 1)
                            pe.wait_ge(p_done, x)
                            for j in range(SUB):
                                last = pe.transpose(psP[:, j * B:(j + 1) * B], pT[:, d, j * P:(j + 1) * P], ident[0:B, 0:B])
                            last.then_inc(p_turned, 1)
                            pe.wait_ge(p_done, x + 1)
                            pe.wait_ge(added[d], t * 2 + s // 2)
                            for j in range(SUB):
                                last = pe.matmul(psE[d][0:B, 0:D], pE[:, d, j * B:(j + 1) * B], rows_t[:, s, j, 0:D],
                                                 start=(j == 0), stop=(j == SUB - 1))
                            last.then_inc(used[s], 1)

                        def body(t, s, end):
                            if not (end and s == RING - 1):
                                scores(*after(t, s))
                            sums(t, s)

                        each_step(pe, None, 0, scores, body)

                    @block.scalar
                    def _(act):
                        def qk(t, s):
                            d = s % 2
                            b = act.value_load(step_blk[0][0:1, bass.ds(step(t, s), 1)], min_val=0, max_val=NB - 1)
                            act.wait_ge(rec_free[s], t + 1)
                            act.activation(kTs[:, d, :], one(kT[:, bass.ds(b, 1), :]), ACT.Copy)
                            act.activation(qT[:, d, :], psA[0:SMALL, :], ACT.Copy).then_inc(qk_done, 1)

                        def first(t, s):
                            for i in range(3):
                                act_idx(act, 0, i)
                            qk(0, 0)

                        def body(t, s, end):
                            d, x = s % 2, step(t, s)
                            if not (end and s > 0):
                                act_idx(act, *after(t, s, 3))
                            if not (end and s == RING - 1):
                                qk(*after(t, s))
                            act.wait_ge(s_done, x + 1)
                            act.activation(pT[:, d, :], S[:, d, :], ACT.Exp, bias=nm[:, d:d + 1], scale=SC, accum_out=rs[:, d:d + 1])
                            act.activation(sc[:, d:d + 1], df[:, d:d + 1], ACT.Exp).then_inc(e_done, 1)
                            act.wait_ge(p_turned, x + 1)
                            act.activation(pE[:, d, :], psP[:, 0:SUB * B], ACT.Copy).then_inc(p_done, 1)

                        each_step(act, None, 0, first, body)

                    @block.vector
                    def _(dve):
                        st = Steps(dve, own)

                        def scores(t, s):
                            x, d = step(t, s), s % 2
                            b = dve.value_load(step_blk[0][0:1, bass.ds(x, 1)], min_val=0, max_val=NB - 1)
                            mb = m[:, bass.ds(b, 1)]
                            dve.wait_ge(rec_free[s], t + 1)
                            dve.tensor_scalar(pen[:, :], psB[0:B, :], node[0:B, bass.ds(x, 1)], -BIG, ALU.not_equal, ALU.mult).then_inc(pen_done, 1)
                            dve.wait_ge(pen_done, x + 1)
                            dve.wait_ge(s_mm, x + 1)
                            if not (isinstance(t, int) and t == 0 and s == 0):
                                dve.wait_ge(e_done, x - 1)
                            st.all()
                            st.mark(dve.tensor_copy(mo[:, d:d + 1], mb))
                            st(dve.tensor_tensor_reduce(out=S[:, d, :], in0=psS[d][0:B, :], in1=pen[:, :], scale=1.0, scalar=-BIG,
                                                        op0=ALU.add, op1=ALU.max, accum_out=mx[:, d:d + 1]))
                            st(dve.tensor_tensor(mn[:, d:d + 1], mo[:, d:d + 1], mx[:, d:d + 1], ALU.max))
                            st(dve.tensor_scalar(nm[:, d:d + 1], mn[:, d:d + 1], -SC, None, ALU.mult))
                            dve.scalar_tensor_tensor(df[:, d:d + 1], mo[:, d:d + 1], SC, nm[:, d:d + 1], ALU.mult, ALU.add).then_inc(s_done, 1)
                            st.mark(dve.tensor_copy(mb, mn[:, d:d + 1]))

                        def body(t, s, end):
                            d = s % 2
                            if not (end and s == RING - 1):
                                scores(*after(t, s))
                            b = dve.value_load(step_blk[0][0:1, bass.ds(step(t, s), 1)], min_val=0, max_val=NB - 1)
                            lb, ub = l[:, bass.ds(b, 1)], one(U[:, bass.ds(b, 1), :])
                            dve.wait_ge(used[s], t + 1)
                            st.all()
                            st.mark(dve.scalar_tensor_tensor(lb, lb, sc[:, d:d + 1], rs[:, d:d + 1], ALU.mult, ALU.add))
                            dve.wait_ge(added[1 - d], t * 2 + (s + 1) // 2)
                            dve.scalar_tensor_tensor(ub, ub, sc[:, d:d + 1], psE[d][0:B, 0:D], ALU.mult, ALU.add).then_inc(added[d], 1)

                        each_step(dve, st, RING * 6, scores, body)

        def edge_sums():
            name = "gcn"
            with ExitStack() as c:
                rec_t = sb(c, name + "_rec", [P, RING, SUB, RW])
                idx = sb(c, name + "_idx", [P, RING, SUB], I32)
                lk = sb(c, name + "_lk", [P, 2, SUB])
                pE = sb(c, name + "_pE", [P, 2, SUB, B])
                psE = [pb(c, f"{name}_psE{i}") for i in range(2)]
                rows_t, rec_ready, rec_free, got, used, sp_part, act_idx, pool_part = edge_walk(
                    name, 1, table1, D, {"rec": rec_t, "idx": idx})
                own = sem(name + "_own")
                added = [sem(f"{name}_added{i}") for i in range(2)]

                with nc.Block() as block:
                    @block.vector
                    def _(dve):
                        dve.memset(U[:, :, :], 0.0)

                with nc.Block() as block:
                    @block.sync
                    def _(sp):
                        sp_part(sp)

                    @block.gpsimd
                    def _(pool):
                        pool_part(pool)

                    @block.scalar
                    def _(act):
                        def first(t, s):
                            for i in range(3):
                                act_idx(act, 0, i)

                        def body(t, s, end):
                            if not (end and s > 0):
                                act_idx(act, *after(t, s, 3))

                        each_step(act, None, 0, first, body)

                    @block.tensor
                    def _(pe):
                        with loop(pe, NS // RING) as t:
                            for s in range(RING):
                                d = s % 2
                                pe.wait_ge(got[s], t * (16 * SUB) + 16 * SUB)
                                pe.wait_ge(rec_free[s], t + 1)
                                pe.wait_ge(added[d], t * 2 + s // 2)
                                for j in range(SUB):
                                    last = pe.matmul(psE[d][0:B, 0:D], pE[:, d, j, :], rows_t[:, s, j, :],
                                                     start=(j == 0), stop=(j == SUB - 1))
                                last.then_inc(used[s], 1)

                    @block.vector
                    def _(dve):
                        st = Steps(dve, own)

                        def weights(t, s):
                            x, d = t * RING + s, s % 2
                            dve.wait_ge(rec_ready[s], t * 16 + 16)
                            dve.wait_ge(used[(s + 2) % RING], t + 1 if s >= 2 else t)
                            st(dve.tensor_scalar(lk[:, d, :], rec_t[:, s, :, 0], step_node[1][:, bass.ds(x, 1)], None, ALU.subtract))
                            for j in range(SUB):
                                last = dve.tensor_scalar(pE[:, d, j, :], iota_n[:, :], lk[:, d, j:j + 1], rec_t[:, s, j, 2:3],
                                                         ALU.is_equal, ALU.mult)
                            last.then_inc(rec_free[s], 1)

                        def body(t, s, end):
                            d = s % 2
                            if not (end and s == RING - 1):
                                weights(*after(t, s))
                            b = dve.value_load(step_blk[1][0:1, bass.ds(t * RING + s, 1)], min_val=0, max_val=NB - 1)
                            ub = one(U[:, bass.ds(b, 1), :])
                            dve.wait_ge(used[s], t + 1)
                            dve.wait_ge(added[1 - d], t * 2 + (s + 1) // 2)
                            dve.tensor_tensor(ub, ub, psE[d][0:B, 0:D], ALU.add).then_inc(added[d], 1)

                        each_step(dve, st, RING, weights, body)

        def route_rows(selw):
            name = "topk"
            with ExitStack() as c:
                wr = sb(c, name + "_wr", [B, D])
                br = sb(c, name + "_br", [B, 1])
                w = sb(c, name + "_w", [B, NB])
                v = sb(c, name + "_v", [B, NB])
                junk = sb(c, name + "_junk", [B, D])
                eq = sb(c, name + "_eq", [B, NB])
                gt = sb(c, name + "_gt", [B, NB])
                tot = sb(c, name + "_tot", [B, NB])
                cum = sb(c, name + "_cum", [B, NB])
                cnt, pos, sign, kk, thr, take = (sb(c, f"{name}_{x}", [B, 1]) for x in ("cnt", "pos", "sign", "kk", "thr", "take"))
                T, bit, cand, add = (sb(c, f"{name}_{x}", [B, 1], I32) for x in ("T", "bit", "cand", "add"))
                ps = pb(c, name + "_ps")
                loaded, own, cnt_done, sum_done, eq_done, rank_done = (
                    sem(f"{name}_{x}") for x in ("loaded", "own", "cnt", "sum", "eq", "rank"))
                BITS = 31
                with nc.Block() as block:
                    @block.sync
                    def _(sp):
                        sp.dma_start(wr[:, :], A["L0_ffn_wr"].partition_broadcast(B)).then_inc(loaded, 16)
                        sp.dma_start(br[:, :], A["L0_ffn_br"].partition_broadcast(B)).then_inc(loaded, 16)

                    @block.tensor
                    def _(pe):
                        with loop(pe, BITS + 2) as i:
                            pe.wait_ge(cnt_done, i + 1)
                            pe.matmul(ps[0:B, 0:1], ones[0:B, 0:B], cnt[:, :], start=True, stop=True).then_inc(sum_done, 1)
                        pe.wait_ge(eq_done, 1)
                        pe.matmul(ps[0:B, 64:64 + NB], lower[0:B, 0:B], eq[:, :], start=True, stop=True)
                        pe.matmul(ps[0:B, 128:128 + NB], ones[0:B, 0:B], eq[:, :], start=True, stop=True).then_inc(rank_done, 1)

                    @block.vector
                    def _(dve):
                        st = Steps(dve, own)
                        dve.wait_ge(loaded, 32)
                        with loop(dve, NB, st, 1) as b:
                            r = bass.ds(b, 1)
                            st(dve.scalar_tensor_tensor(junk[:, :], one(XN[0:B, r, :]), 1.0, wr[:, :], ALU.mult, ALU.mult,
                                                        accum_out=w[:, r]))
                        st(dve.tensor_scalar(w[:, :], w[:, :], br[:, 0:1], None, ALU.add))
                        dve.tensor_scalar(v[:, :], w[:, :], 0.0, 0.0, ALU.is_ge, ALU.add, accum_out=cnt[:, :]).then_inc(cnt_done, 1)
                        dve.wait_ge(sum_done, 1)
                        st(dve.tensor_scalar(pos[:, :], ps[0:B, 0:1], float(TOPK), None, ALU.is_ge))
                        st(dve.tensor_scalar(sign[:, :], pos[:, :], 2.0, -1.0, ALU.mult, ALU.add))
                        st(dve.tensor_scalar(kk[:, :], pos[:, :], float(2 * TOPK - N - 1), float(N - TOPK + 1), ALU.mult, ALU.add))
                        st(dve.tensor_scalar(v[:, :], w[:, :], sign[:, 0:1], None, ALU.mult))
                        st.mark(dve.memset(T[:, :], 0))
                        st(dve.memset(bit[:, :], 1 << (BITS - 1)))
                        with loop(dve, BITS, st, 5) as i:
                            st(dve.tensor_tensor(cand[:, :], T[:, :], bit[:, :], ALU.bitwise_or))
                            dve.tensor_scalar(eq[:, :], v[:, :], cand[:, 0:1].bitcast(F32), 0.0, ALU.is_ge, ALU.add,
                                              accum_out=cnt[:, :]).then_inc(cnt_done, 1)
                            dve.wait_ge(sum_done, i + 2)
                            st(dve.tensor_scalar(take[:, :], ps[0:B, 0:1], kk[:, 0:1], None, ALU.is_ge))
                            st(dve.tensor_tensor(add[:, :], take[:, :], bit[:, :], ALU.mult))
                            st(dve.tensor_tensor(T[:, :], T[:, :], add[:, :], ALU.bitwise_or))
                            st(dve.tensor_scalar(bit[:, :], bit[:, :], 1, None, ALU.logical_shift_right))
                        st(dve.tensor_scalar(thr[:, :], T[:, 0:1].bitcast(F32), sign[:, 0:1], None, ALU.mult))
                        dve.tensor_scalar(eq[:, :], w[:, :], thr[:, 0:1], None, ALU.is_equal).then_inc(eq_done, 1)
                        st.mark(dve.tensor_scalar(gt[:, :], w[:, :], thr[:, 0:1], None, ALU.is_gt))
                        dve.tensor_scalar(v[:, :], w[:, :], thr[:, 0:1], 0.0, ALU.is_gt, ALU.add, accum_out=cnt[:, :]).then_inc(cnt_done, 1)
                        dve.wait_ge(sum_done, BITS + 2)
                        dve.wait_ge(rank_done, 1)
                        st(dve.tensor_scalar(kk[:, :], ps[0:B, 0:1], -1.0, float(TOPK), ALU.mult, ALU.add))
                        st(dve.tensor_copy(tot[:, :], ps[0:B, 128:128 + NB]))
                        st(dve.tensor_tensor_scan(cum[:, :], ones[0:B, 0:NB], tot[:, :], 0.0, ALU.mult, ALU.add))
                        st(dve.tensor_tensor(cum[:, :], cum[:, :], tot[:, :], ALU.subtract))
                        st(dve.tensor_tensor(cum[:, :], cum[:, :], ps[0:B, 64:64 + NB], ALU.add))
                        st(dve.scalar_tensor_tensor(cum[:, :], cum[:, :], kk[:, 0:1], eq[:, :], ALU.is_lt, ALU.mult))
                        st(dve.tensor_tensor(gt[:, :], gt[:, :], cum[:, :], ALU.add))
                        dve.tensor_tensor(selw[:, :], gt[:, :], w[:, :], ALU.mult)

        def route_experts(topi, topw):
            name = "route"
            n_e = 8
            cap = float(-(-N * 125 // (n_e * 100)))
            with ExitStack() as c:
                wr = sb(c, name + "_wr", [P, KF, n_e])
                br = sb(c, name + "_br", [1, n_e])
                colsum = sb(c, name + "_colsum", [B, D])
                mT = sb(c, name + "_mT", [P, KF])
                lg, ex, rw, sc, top = (sb(c, f"{name}_{x}", [1, n_e]) for x in ("lg", "ex", "rw", "sc", "top"))
                mx, sm = sb(c, name + "_mx", [1, 1]), sb(c, name + "_sm", [1, 1])
                ps, ps2, ps3 = pb(c, name + "_ps"), pb(c, name + "_ps2"), pb(c, name + "_ps3")
                loaded, own, col_done, mean_mm, mT_done, lg_mm, to_exp, exp_done, w_done, w_mm = (
                    sem(f"{name}_{x}") for x in ("loaded", "own", "col", "mean_mm", "mT", "lg_mm", "to_exp", "exp", "w", "w_mm"))
                with nc.Block() as block:
                    @block.sync
                    def _(sp):
                        sp.dma_start(wr[:, :, :], A["L1_ffn_Wr"]).then_inc(loaded, 16)
                        sp.dma_start(br[:, :], A["L1_ffn_br"]).then_inc(loaded, 16)

                    @block.tensor
                    def _(pe):
                        pe.wait_ge(col_done, 1)
                        for f in range(KF):
                            last = pe.matmul(ps[:, f:f + 1], colsum[:, f * P:(f + 1) * P], ones[0:B, 0:1], start=True, stop=True)
                        last.then_inc(mean_mm, 1)
                        pe.wait_ge(mT_done, 1)
                        pe.wait_ge(loaded, 32)
                        for f in range(KF):
                            last = pe.matmul(ps2[0:1, 0:n_e], mT[:, f:f + 1], wr[:, f, :], start=(f == 0), stop=(f == KF - 1))
                        last.then_inc(lg_mm, 1)
                        pe.wait_ge(w_done, 1)
                        pe.matmul(ps3[0:B, 0:2], ones[0:1, 0:B], lg[:, 0:2], start=True, stop=True).then_inc(w_mm, 1)

                    @block.scalar
                    def _(act):
                        for i in range(3):
                            act.wait_ge(to_exp, i + 1)
                            k = n_e if i < 2 else 2
                            act.activation(ex[:, 0:k], lg[:, 0:k], ACT.Exp).then_inc(exp_done, 1)

                    @block.vector
                    def _(dve):
                        st = Steps(dve, own)
                        dve.tensor_reduce(colsum[:, :], XN[0:B, :, :].rearrange("p b d -> p d b"), AX.X, ALU.add).then_inc(col_done, 1)
                        dve.wait_ge(mean_mm, 1)
                        dve.tensor_scalar(mT[:, :], ps[:, 0:KF], 1.0 / N, None, ALU.mult).then_inc(mT_done, 1)
                        dve.wait_ge(lg_mm, 1)
                        dve.wait_ge(loaded, 32)
                        st(dve.tensor_tensor(lg[:, :], ps2[0:1, 0:n_e], br[:, :], ALU.add))

                        def softmax(i, k, dst):
                            st(dve.tensor_reduce(mx[:, :], lg[:, 0:k], AX.X, ALU.max))
                            dve.tensor_scalar(lg[:, 0:k], lg[:, 0:k], mx[:, 0:1], None, ALU.subtract).then_inc(to_exp, 1)
                            dve.wait_ge(exp_done, i + 1)
                            st(dve.tensor_reduce(sm[:, :], ex[:, 0:k], AX.X, ALU.add))
                            st(dve.reciprocal(sm[:, :], sm[:, :]))
                            st(dve.tensor_scalar(dst, ex[:, 0:k], sm[:, 0:1], None, ALU.mult))

                        softmax(0, n_e, rw[:, :])
                        st(dve.tensor_scalar(sc[:, :], rw[:, :], float(N), cap, ALU.mult, ALU.max))
                        st(dve.reciprocal(sc[:, :], sc[:, :]))
                        st(dve.tensor_scalar(sc[:, :], sc[:, :], cap, None, ALU.mult))
                        st(dve.tensor_tensor(lg[:, :], rw[:, :], sc[:, :], ALU.mult))
                        softmax(1, n_e, rw[:, :])
                        st(dve.max(top[:, :], rw[:, :]))
                        st(dve.max_index(topi[:, :], top[:, :], rw[:, :]))
                        st(dve.tensor_copy(lg[:, 0:2], top[:, 0:2]))
                        softmax(2, 2, rw[:, 0:2])
                        dve.tensor_copy(lg[:, 0:2], rw[:, 0:2]).then_inc(w_done, 1)
                        dve.wait_ge(w_mm, 1)
                        dve.tensor_copy(topw[:, :], ps3[0:B, 0:2])

        for which, (k_, o_) in enumerate((("dst", "src"), ("src", "dst"))):
            sort_edges(which, A[k_], A[o_], A["edge_weight"])
            end_phase()

        X = sb(ctx, "X", [B, NB, D])
        XN = sb(ctx, "XN", [P, NB, D])
        U = sb(ctx, "U", [B, NB, D])
        s_x = sem("x_loaded")
        with nc.Block() as block:
            @block.sync
            def _(sp):
                for i in range(5):
                    n = NB // 5
                    sp.dma_start(X[:, i * n:(i + 1) * n, :], rows(A["x"])[:, i * n:(i + 1) * n, :]).then_inc(s_x, 16)
                sp.wait_ge(s_x, 80)
        end_phase()

        def blk(k, b):
            return bass.ds(k * CH + b, 1)

        def bias_and_self(dve, st, k, ys, b2, tmp):
            st(dve.tensor_tensor(tmp[:, :, :], ys[0], b2[0][:, :].unsqueeze(1).broadcast_to([B, CH, D]), ALU.add))
            u = U[:, bass.ds(k * CH, CH), :]
            return dve.tensor_tensor(u, u, tmp[:, :, :], ALU.add)

        def plain(dve, st, k, ys, b2, tmp):
            return dve.tensor_copy(U[:, bass.ds(k * CH, CH), :], ys[0])

        layer_norm("ln_a", X, XN)
        end_phase()
        with ExitStack() as c0:
            edge = {"kT": sb(c0, "edge_kT", [SMALL, NB, B]), "m": sb(c0, "edge_m", [B, NB]), "l": sb(c0, "edge_l", [B, NB]),
                    "wqk": A["L0_gnn_Wqk"], "bqk": A["L0_gnn_bqk"], "bk": A["L0_gnn_bk"]}
            with ExitStack() as c1:
                kvd = attention_sums(c1, "sums0", A["L0_mix_Wkv"], edge, table0)
                end_phase()
                attention_rows("att0", A["L0_mix_Wq"], kvd, True)
                end_phase()
            layer_norm("ln_b", U, U, affine=(A["L0_mix_ln1_g"], A["L0_mix_ln1_b"]))
            end_phase()
            mlp("mix0", [U], [(A["L0_mix_W1"], A["L0_mix_b1"], A["L0_mix_W2"], A["L0_mix_b2"].partition_broadcast(B))],
                D, ACT.Gelu, 1, bias_and_self)
            end_phase()
            layer_norm("ln_c", U, U, affine=(A["L0_mix_ln2_g"], A["L0_mix_ln2_b"]), into=X)
            end_phase()
            edge_softmax(edge)
            end_phase()
            own = sem("gat_end")
            with nc.Block() as block:
                @block.vector
                def _(dve):
                    st = Steps(dve, own)
                    st(dve.reciprocal(edge["l"][:, :], edge["l"][:, :]))
                    with loop(dve, NB, st, 1) as b:
                        r = bass.ds(b, 1)
                        st.mark(dve.scalar_tensor_tensor(one(X[:, r, :]), one(U[:, r, :]), edge["l"][:, r], one(X[:, r, :]), ALU.mult, ALU.add))
            end_phase()

        layer_norm("ln_d", X, XN)
        end_phase()
        with ExitStack() as c0:
            selw = sb(c0, "selw", [B, NB])
            route_rows(selw)
            end_phase()

            def weighted(dve, st, k, ys, b2, tmp):
                st(dve.tensor_tensor(tmp[:, :, :], ys[0], b2[0][:, :].unsqueeze(1).broadcast_to([B, CH, D]), ALU.add))
                for b in range(CH):
                    st(dve.scalar_tensor_tensor(tmp[:, b, :], tmp[:, b, :], selw[:, blk(k, b)], one(XN[0:B, blk(k, b), :]), ALU.mult, ALU.add))
                x = X[:, bass.ds(k * CH, CH), :]
                return dve.tensor_tensor(x, x, tmp[:, :, :], ALU.add)

            mlp("ffn0", [XN], [(A["L0_ffn_w1"], A["L0_ffn_b1"], A["L0_ffn_w2"], A["L0_ffn_b2"].partition_broadcast(B))],
                4 * D, ACT.Gelu_apprx_tanh, 1 + CH, weighted)
            end_phase()

        layer_norm("ln_e", X, XN)
        end_phase()
        with ExitStack() as c1:
            kvd = attention_sums(c1, "sums1", A["L1_mix_Wkv"], None, table1)
            end_phase()
            attention_rows("att1", A["L1_mix_Wq"], kvd, False)
            end_phase()
        linear("merge", U, A["L1_mix_Wm"], None, 0, lambda dve, st, k, y, b: dve.tensor_copy(U[:, bass.ds(k * CH, CH), :], y))
        end_phase()
        layer_norm("ln_f", U, U, affine=(A["L1_mix_g1"], A["L1_mix_b1"]))
        end_phase()
        mlp("mix1", [XN, U], [(A["L1_mix_W1"], None, A["L1_mix_W2"], None)], 2 * D, ACT.Relu, 0, plain)
        end_phase()
        layer_norm("ln_g", U, U, affine=(A["L1_mix_g2"], A["L1_mix_b2"]), into=X, plus=XN)
        end_phase()
        edge_sums()
        end_phase()

        def into_x(dve, st, k, y, b2):
            x = X[:, bass.ds(k * CH, CH), :]
            st(dve.tensor_tensor(x, x, y, ALU.add))
            return dve.tensor_tensor(x, x, b2[:, :].unsqueeze(1).broadcast_to([B, CH, D]), ALU.add)

        linear("gcn_w", U, A["L1_gnn_W"], A["L1_gnn_b"], 1, into_x)
        end_phase()

        layer_norm("ln_h", X, XN)
        end_phase()
        topi = sb(ctx, "topi", [1, 8], mybir.dt.uint32)
        topw = sb(ctx, "topw", [B, 2])
        route_experts(topi, topw)
        end_phase()
        bb = sb(ctx, "expert_bias", [B, D])
        held = {}

        def expert(name, shape):
            def load(sp, e):
                if e not in held:
                    held[e] = sp.value_load(topi[0:1, e:e + 1], min_val=0, max_val=7)
                return shape(A[name][bass.ds(held[e], 1)])
            return load

        def both_biases(dve, st, b2):
            st(dve.tensor_scalar(bb[:, :], b2[0][:, :], topw[:, 0:1], None, ALU.mult))
            st(dve.scalar_tensor_tensor(bb[:, :], b2[1][:, :], topw[:, 1:2], bb[:, :], ALU.mult, ALU.add))

        def mixed(dve, st, k, ys, b2, tmp):
            xn, u = XN[0:B, bass.ds(k * CH, CH), :], U[:, bass.ds(k * CH, CH), :]
            st(dve.scalar_tensor_tensor(tmp[:, :, :], ys[0], topw[:, 0:1], xn, ALU.mult, ALU.add))
            st(dve.scalar_tensor_tensor(tmp[:, :, :], ys[1], topw[:, 1:2], tmp[:, :, :], ALU.mult, ALU.add))
            return dve.tensor_tensor(u, tmp[:, :, :], bb[:, :].unsqueeze(1).broadcast_to([B, CH, D]), ALU.add)

        spec = (expert("L1_ffn_W1", lambda a: a.rearrange("e p k f -> (e p) k f")), expert("L1_ffn_b1", lambda a: a.rearrange("e p f -> (e p) f")),
                expert("L1_ffn_W2", lambda a: a.rearrange("e p f d -> (e p) f d")), expert("L1_ffn_b2", lambda a: a.rearrange("e d -> (e d)").partition_broadcast(B)))
        mlp("ffn1", [XN], [spec, spec], 2 * D, ACT.Gelu, 2, mixed, setup=both_biases)
        end_phase()
        layer_norm("ln_i", U, U, affine=(A["L1_ffn_gamma"], A["L1_ffn_beta"]), into=X)
        end_phase()

        s_out = sem("out_written")
        with nc.Block() as block:
            @block.sync
            def _(sp):
                for i in range(5):
                    n = NB // 5
                    sp.dma_start(rows(out)[:, i * n:(i + 1) * n, :], X[:, i * n:(i + 1) * n, :]).then_inc(s_out, 16)
                sp.wait_ge(s_out, 80)


def lay_out(inputs):
    a = {k: np.asarray(v) for k, v in inputs.items()}

    def halves(w):
        return np.ascontiguousarray(w.reshape(-1, P, w.shape[-1]).transpose(1, 0, 2))

    def edges(v, fill):
        out = np.full((P * EC,), fill, v.dtype)
        out[:E] = v
        return out.reshape(P, EC)

    o = {"x": a["x"], "src": None, "dst": None}
    pad_key = NB * B + B // 2
    o["src"], o["dst"] = edges(a["src"], pad_key), edges(a["dst"], pad_key)
    o["edge_weight"] = edges(a["edge_weight"], 0)
    wq, wk = a["L0_gnn_Wq"], a["L0_gnn_Wk"]
    o["L0_gnn_Wqk"] = halves(np.concatenate([wq, wk], 1))
    o["L0_gnn_bqk"] = np.concatenate([a["L0_gnn_bq"], a["L0_gnn_bk"]])[None]
    o["L0_gnn_bk"] = a["L0_gnn_bk"][:, None]
    w = a["L0_mix_Wqkv"].T
    o["L0_mix_Wq"], o["L0_mix_Wkv"] = halves(w[:, :D]), halves(w[:, D:])
    o["L0_mix_W1"], o["L0_mix_W2"] = halves(a["L0_mix_W1"].T), halves(a["L0_mix_W2"].T)
    o["L0_mix_b1"] = np.ascontiguousarray(a["L0_mix_b1"].reshape(-1, P).T)
    for n in ("L0_mix_b2", "L0_mix_ln1_g", "L0_mix_ln1_b", "L0_mix_ln2_g", "L0_mix_ln2_b", "L0_ffn_b2", "L0_ffn_br",
              "L1_gnn_b", "L1_mix_g1", "L1_mix_b1", "L1_mix_g2", "L1_mix_b2", "L1_ffn_gamma", "L1_ffn_beta", "L1_ffn_b2"):
        o[n] = a[n]
    o["L0_ffn_wr"] = a["L0_ffn_wr"].reshape(-1)
    o["L0_ffn_w1"], o["L0_ffn_w2"] = halves(a["L0_ffn_w1"]), halves(a["L0_ffn_w2"])
    o["L0_ffn_b1"] = np.ascontiguousarray(a["L0_ffn_b1"].reshape(-1, P).T)
    o["L1_gnn_W"] = halves(a["L1_gnn_W"])
    o["L1_mix_Wq"] = halves(a["L1_mix_Wq"])
    o["L1_mix_Wkv"] = halves(np.concatenate([a["L1_mix_Wk"], a["L1_mix_Wv"]], 1))
    for n in ("L1_mix_Wm", "L1_mix_W1", "L1_mix_W2", "L1_ffn_Wr"):
        o[n] = halves(a[n])
    o["L1_ffn_br"] = a["L1_ffn_br"][None]
    o["L1_ffn_W1"] = np.stack([halves(x) for x in a["L1_ffn_W1"]])
    o["L1_ffn_W2"] = np.stack([halves(x) for x in a["L1_ffn_W2"]])
    o["L1_ffn_b1"] = np.ascontiguousarray(a["L1_ffn_b1"].reshape(8, -1, P).transpose(0, 2, 1))
    return o


def kernel(**inputs):
    import concourse.bacc as bacc
    from concourse.bass_utils import run_bass_kernel_spmd

    arrays = lay_out(inputs)
    nc = bacc.Bacc("TRN2", target_bir_lowering=False, num_devices=1)
    A = {n: nc.dram_tensor("in_" + n, v.shape, mybir.dt.from_np(v.dtype), kind="ExternalInput").ap() for n, v in arrays.items()}
    out = nc.dram_tensor("out_x", (N, D), F32, kind="ExternalOutput").ap()
    gps_kernel(nc, A, out)
    r = run_bass_kernel_spmd(nc, [{"in_" + n: v for n, v in arrays.items()}], core_ids=[0])
    return r.results[0]["out_x"]
```

```python
import concourse.bass as bass
from concourse import mybir
from contextlib import ExitStack
import numpy as np

F32 = mybir.dt.float32
I32 = mybir.dt.int32
BF16 = mybir.dt.bfloat16
ALU = mybir.AluOpType
ACT = mybir.ActivationFunctionType
AX = mybir.AxisListType

P = 128
N, D, E = 6250, 256, 200000
KF = D // P
B = 125
NB = N // B
CH = 2
NC = NB // CH
TOK = CH * B
SUB = 4
G = P * SUB
NG = -(-E // G)
EP = NG * G
EC = EP // P
NS = NG + NB - 1
RING = 8
IDX = 6
RW = 3
SMALL = 25
HEADS, HD = 8, 32
HH = P // HD
LN_EPS, ATT_EPS = 1e-5, 1e-6
TOPK = N // 2 - 1
SLOT = 17
BIG = 1e30
R, R_DVE = 5, 3


class Steps:

    def __init__(self, eng, sem):
        self.eng, self.sem, self.base, self.n = eng, sem, 0, 0

    def __call__(self, ins):
        ins.then_inc(self.sem, 1)
        self.n += 1
        self.eng.wait_ge(self.sem, self.base + self.n)

    def mark(self, ins):
        ins.then_inc(self.sem, 1)
        self.n += 1

    def all(self):
        self.eng.wait_ge(self.sem, self.base + self.n)


def settle(pool, cell, settled, before):
    pool.wait_ge(settled, before)
    pool.tensor_tensor(cell, cell, cell, ALU.add).then_inc(settled, 1)


class loop:

    def __init__(self, eng, times, steps=None, per=0):
        self.eng, self.times, self.steps, self.per = eng, times, steps, per

    def __enter__(self):
        self.f = self.eng.Fori(0, self.times)
        t = self.f.__enter__()
        if self.steps:
            s = self.steps
            self.before = s.base + s.n
            s.base, s.n = self.before + t * self.per, 0
        return t

    def __exit__(self, *a):
        if self.steps and a[0] is None:
            s = self.steps
            assert s.n == self.per, (s.n, self.per)
            s.base, s.n = self.before + self.times * self.per, 0
        return self.f.__exit__(*a)


def gps_kernel(nc, A, out):
    ctx = ExitStack()
    phase_sems = []

    def sem(name):
        held = nc.semaphore(name)
        phase_sems.append((held, held.__enter__()))
        return phase_sems[-1][1]

    def pool_dma_sem(name):
        return ctx.enter_context(nc.semaphore(name))

    def end_phase():
        with nc.Block() as block:
            @block.sync
            def _(sp):
                for _, s in phase_sems:
                    sp.sem_clear(s)
        while phase_sems:
            phase_sems.pop()[0].__exit__(None, None, None)

    def sb(c, name, shape, dt=F32):
        return c.enter_context(nc.sbuf_tensor(name, shape, dt))

    def pb(c, name, shape=(P, 512), dt=F32):
        return c.enter_context(nc.psum_tensor(name, list(shape), dt))

    def one(ap):
        return ap.rearrange("p a n -> p (a n)")

    def rows(dram):
        return dram.rearrange("(b p) d -> p b d", p=B)

    table0 = nc.dram_tensor("table0", [N, D + SMALL], F32).ap()
    table1 = nc.dram_tensor("table1", [N, D], F32).ap()
    spill_rec = [nc.dram_tensor(f"spill_rec{i}", [P, EC, RW], F32).ap() for i in range(2)]
    spill_pos = [nc.dram_tensor(f"spill_pos{i}", [P, EC], I32).ap() for i in range(2)]
    rec_d = [nc.dram_tensor(f"records{i}", [EP, RW], F32).ap() for i in range(2)]

    with ctx:
        ident = sb(ctx, "ident", [P, P])
        ones = sb(ctx, "ones", [P, P])
        lower = sb(ctx, "lower", [P, P])
        iota_n = sb(ctx, "iota_n", [P, B])
        iota_p = sb(ctx, "iota_p", [P, 1])
        eps = sb(ctx, "eps", [P, 1])
        ident16 = sb(ctx, "ident16", [P, P], BF16)
        cell = sb(ctx, "cell", [1, 1], I32)
        slot_pos = sb(ctx, "slot_pos", [P, 2, SLOT], I32)
        slot_rec = sb(ctx, "slot_rec", [P, 2, SLOT, RW])
        sent = [pool_dma_sem(f"sent{h}") for h in range(2)]
        sent_unsorted = [pool_dma_sem(f"sent_unsorted{h}") for h in range(2)]
        step_blk = [sb(ctx, f"step_blk{i}", [1, NS], I32) for i in range(2)]
        step_grp = [sb(ctx, f"step_grp{i}", [1, NS], I32) for i in range(2)]
        step_node = [sb(ctx, f"step_node{i}", [P, NS]) for i in range(2)]

        s_c = sem("constants_step")
        with nc.Block() as block:
            @block.gpsimd
            def _(pool):
                st = Steps(pool, s_c)
                st(pool.memset(ident[:, :], 0.0))
                st(pool.affine_select(out=ident[:, :], in_=ident[:, :], compare_op=ALU.not_equal, fill=1.0,
                                      base=0, pattern=[[-1, P]], channel_multiplier=1))
                st(pool.memset(lower[:, :], 1.0))
                st(pool.affine_select(out=lower[:, :], in_=lower[:, :], compare_op=ALU.is_gt, fill=0.0,
                                      base=0, pattern=[[1, P]], channel_multiplier=-1))
                pool.tensor_copy(ident16[:, :], ident[:, :])
                pool.memset(ones[:, :], 1.0)
                pool.memset(eps[:, :], LN_EPS)
                pool.memset(cell[:, :], 0)
                pool.iota(iota_n[:, :], pattern=[[1, B]], base=0, channel_multiplier=0,
                          allow_small_or_imprecise_dtypes=True)
                st(pool.iota(iota_p[:, :], pattern=[[0, 1]], base=0, channel_multiplier=1,
                             allow_small_or_imprecise_dtypes=True))
        end_phase()

        def sort_edges(which, key, other, val):
            t_ = f"sort{which}_"
            with ExitStack() as c:
                keyi = sb(c, t_ + "key", [P, EC], I32)
                othi = sb(c, t_ + "other", [P, EC], I32)
                rec = sb(c, t_ + "rec", [P, EC, RW])
                blki = sb(c, t_ + "blki", [P, EC], I32)
                blkf = sb(c, t_ + "blkf", [P, EC], BF16)
                mask = sb(c, t_ + "mask", [P, EC], BF16)
                one_ = sb(c, t_ + "one", [P, EC], BF16)
                scan = sb(c, t_ + "scan", [P, EC])
                pos = sb(c, t_ + "pos", [P, EC])
                cls = sb(c, t_ + "cls", [P, NB + 1])
                cnt = sb(c, t_ + "cnt", [P, NB + 1])
                tot = sb(c, t_ + "tot", [P, NB + 1])
                cum = sb(c, t_ + "cum", [P, NB + 1])
                base = sb(c, t_ + "base", [P, NB + 1])
                tcol = sb(c, t_ + "tcol", [NB, 1])
                bnd = sb(c, t_ + "bnd", [NB, 1])
                bndi = sb(c, t_ + "bndi", [NB, 1], I32)
                incl = sb(c, t_ + "incl", [P, P])
                after_ = sb(c, t_ + "after", [P, 2], I32)
                falls = sb(c, t_ + "falls", [P, 2])
                fallen = sb(c, t_ + "fallen", [1, 1], I32)
                ge = sb(c, t_ + "ge", [NB, NS])
                stepf = sb(c, t_ + "stepf", [P, NS])
                iota_s = sb(c, t_ + "iota_s", [P, NS])
                ps = pb(c, t_ + "ps")
                ps2 = pb(c, t_ + "ps2")
                loaded, own, count_done, sums_done = (sem(t_ + x) for x in ("loaded", "own", "counted", "summed"))
                tcol_done, cum_done, bnd_done, step_done = (sem(t_ + x) for x in ("tcol", "cumsum", "bounds", "steps"))
                pool_c, pos_done, rec_done, spilled, order_done, order_mm, order_set = (
                    sem(t_ + x) for x in ("iota", "positions", "records", "spilled", "order", "order_mm", "order_set"))

                with nc.Block() as block:
                    @block.sync
                    def _(sp):
                        sp.dma_start(keyi[:, :], key).then_inc(loaded, 16)
                        sp.dma_start(othi[:, :], other).then_inc(loaded, 16)
                        sp.dma_start(scan[:, :], val).then_inc(loaded, 16)
                        if which == 0:
                            sp.dma_start(after_[0:P - 1, :], key[1:P, 0:2]).then_inc(loaded, 16)
                        sp.wait_ge(rec_done, 1)
                        sp.dma_start(spill_rec[which], rec[:, :, :]).then_inc(spilled, 16)
                        if which == 0:
                            sp.dma_start(rec_d[0].rearrange("(p t) w -> p t w", p=P), rec[:, :, :]).then_inc(spilled, 16)
                            sp.wait_ge(spilled, 32)
                        else:
                            sp.wait_ge(pos_done, 1)
                            sp.dma_start(spill_pos[which], blki[:, :]).then_inc(spilled, 16)
                            sp.wait_ge(spilled, 32)

                    @block.gpsimd
                    def _(pool):
                        pool.iota(cls[:, :], pattern=[[1, NB + 1]], base=0, channel_multiplier=0,
                                  allow_small_or_imprecise_dtypes=True).then_inc(pool_c, 1)
                        pool.iota(iota_s[:, :], pattern=[[1, NS]], base=0, channel_multiplier=0,
                                  allow_small_or_imprecise_dtypes=True).then_inc(pool_c, 1)
                        pool.tensor_tensor(incl[:, :], lower[:, :], ident[:, :], ALU.add).then_inc(pool_c, 1)
                        if which == 0:
                            pool.memset(falls[:, :], 0.0).then_inc(pool_c, 1)

                    @block.vector
                    def _(dve):
                        st = Steps(dve, own)
                        dve.memset(one_[:, :], 1.0)
                        st(dve.memset(pos[:, :], -1.0))
                        dve.wait_ge(pool_c, 4 if which == 0 else 3)
                        dve.wait_ge(loaded, 64 if which == 0 else 48)
                        st(dve.tensor_scalar(blki[:, :], keyi[:, :], -float(B // 2), 1.0 / B, ALU.add, ALU.mult))
                        st.mark(dve.tensor_copy(blkf[:, :], blki[:, :]))
                        st.mark(dve.tensor_copy(rec[:, :, 0], keyi[:, :]))
                        st.mark(dve.tensor_scalar(rec[:, :, 1], othi[:, :], float(N - 1), None, ALU.min))
                        dve.tensor_copy(rec[:, :, 2], scan[:, :]).then_inc(rec_done, 1)
                        dve.wait_ge(rec_done, 1)
                        with loop(dve, NB + 1, st, 1) as b:
                            st(dve.tensor_scalar(mask[:, :], blkf[:, :], cls[:, bass.ds(b, 1)], 0.0,
                                                 ALU.is_equal, ALU.add, accum_out=cnt[:, bass.ds(b, 1)]))
                        dve.tensor_copy(tot[:, :], cnt[:, :]).then_inc(count_done, 1)
                        dve.wait_ge(sums_done, 1)
                        st(dve.tensor_copy(tot[:, :], ps[:, 64:64 + NB + 1]))
                        st(dve.tensor_tensor_scan(cum[:, :], ones[:, 0:NB + 1], tot[:, :], 0.0, ALU.mult, ALU.add))
                        st(dve.tensor_tensor(cum[:, :], cum[:, :], tot[:, :], ALU.subtract))
                        st(dve.tensor_tensor(base[:, :], cum[:, :], ps[:, 0:NB + 1], ALU.add))
                        dve.tensor_copy(tcol[:, :], ps[0:NB, 128:129]).then_inc(tcol_done, 1)
                        dve.wait_ge(cum_done, 1)
                        st(dve.tensor_scalar(bndi[:, :], ps2[0:NB, 0:1], 1.0 / G, 0.5 - 0.5 / G, ALU.mult, ALU.add))
                        st(dve.tensor_copy(bnd[:, :], bndi[:, :]))
                        st(dve.tensor_scalar(bnd[:, :], bnd[:, :], 1.0, iota_p[0:NB, 0:1], ALU.max, ALU.add))
                        dve.tensor_scalar(ge[:, :], iota_s[0:NB, :], bnd[:, 0:1], None, ALU.is_ge).then_inc(bnd_done, 1)
                        dve.wait_ge(step_done, 1)
                        st(dve.tensor_scalar(stepf[:, :], ps2[:, 0:NS], float(NB - 1), None, ALU.min))
                        st.mark(dve.tensor_scalar(step_node[which][:, :], stepf[:, :], float(B), None, ALU.mult))
                        st.mark(dve.tensor_copy(step_blk[which][:, :], stepf[0:1, :]))
                        st(dve.tensor_tensor(iota_s[:, :], iota_s[:, :], stepf[:, :], ALU.subtract))
                        st(dve.tensor_scalar(iota_s[:, :], iota_s[:, :], float(NG - 1), None, ALU.min))
                        st(dve.tensor_copy(step_grp[which][:, :], iota_s[0:1, :]))
                        def places():
                            with loop(dve, NB + 1, st, 4) as b:
                                st(dve.tensor_scalar(mask[:, :], blkf[:, :], cls[:, bass.ds(b, 1)], None, ALU.is_equal))
                                st(dve.tensor_tensor_scan(scan[:, :], one_[:, :], mask[:, :], base[:, bass.ds(b, 1)],
                                                          ALU.mult, ALU.add))
                                st(dve.tensor_tensor(scan[:, :], scan[:, :], mask[:, :], ALU.mult))
                                st(dve.tensor_tensor(pos[:, :], pos[:, :], scan[:, :], ALU.add))
                            dve.tensor_copy(blki[:, :], pos[:, :]).then_inc(pos_done, 1)

                        if which == 1:
                            places()
                        else:
                            st(dve.tensor_tensor(scan[:, 0:EC - 1], keyi[:, 1:EC], keyi[:, 0:EC - 1], ALU.is_lt))
                            st(dve.tensor_reduce(falls[:, 0:1], scan[:, 0:EC - 1], AX.X, ALU.add))
                            st(dve.tensor_tensor(falls[0:P - 1, 1:2], after_[0:P - 1, 0:1], keyi[0:P - 1, EC - 1:EC], ALU.is_lt))
                            dve.tensor_tensor(falls[:, 0:1], falls[:, 0:1], falls[:, 1:2], ALU.add).then_inc(order_done, 1)
                            dve.wait_ge(order_mm, 1)
                            dve.tensor_copy(fallen[:, :], ps[0:1, 256:257]).then_inc(order_set, 1)
                            dve.wait_ge(order_set, 1)
                            with dve.If(dve.value_load(fallen[0:1, 0:1], min_val=0, max_val=EP) > 0):
                                places()

                    @block.tensor
                    def _(pe):
                        pe.wait_ge(count_done, 1)
                        pe.matmul(ps[:, 0:NB + 1], lower[:, :], tot[:, :], start=True, stop=True)
                        pe.matmul(ps[:, 64:64 + NB + 1], ones[:, :], tot[:, :], start=True, stop=True)
                        pe.matmul(ps[0:NB, 128:129], tot[:, 0:NB], ones[:, 0:1], start=True, stop=True).then_inc(sums_done, 1)
                        pe.wait_ge(tcol_done, 1)
                        pe.matmul(ps2[0:NB, 0:1], incl[0:NB, 0:NB], tcol[:, :], start=True, stop=True).then_inc(cum_done, 1)
                        pe.wait_ge(bnd_done, 1)
                        pe.matmul(ps2[:, 0:NS], ones[0:NB - 1, :], ge[0:NB - 1, :], start=True, stop=True).then_inc(step_done, 1)
                        if which == 0:
                            pe.wait_ge(order_done, 1)
                            pe.matmul(ps[0:1, 256:257], falls[:, 0:1], ones[:, 0:1], start=True, stop=True).then_inc(order_mm, 1)

                if which == 0:
                    turns = EC // (2 * SLOT)
                    mv = Mover("unsorted", 0, 0, SLOT, turns, sent_unsorted, 0)
                    stored = sem(t_ + "pos_stored")
                    with nc.Block() as block:
                        @block.sync
                        def _(sp):
                            with sp.If(sp.value_load(fallen[0:1, 0:1], min_val=0, max_val=EP) > 0):
                                sp.dma_start(spill_pos[0], blki[:, :]).then_inc(stored, 16)
                                sp.wait_ge(stored, 16)
                                mv.sp(sp)

                        @block.gpsimd
                        def _(pool):
                            with pool.If(pool.value_load(fallen[0:1, 0:1], min_val=0, max_val=EP) > 0):
                                mv.pool(pool)

        class Mover:

            def __init__(self, name, which, at, m, turns, sent, before):
                self.which, self.at, self.m, self.turns = which, at, m, turns
                self.sent, self.before = sent, before
                if m:
                    self.filled = [sem(f"{name}_filled{h}") for h in range(2)]
                    self.settled = sem(name + "_settled")

            def sp(self, sp):
                m = self.m
                if m:
                    with loop(sp, self.turns) as k:
                        for h in range(2):
                            cols = bass.ds(k * (2 * m) + (self.at + h * m), m)
                            sp.wait_ge(self.sent[h], k * (16 * m) + self.before)
                            sp.dma_start(slot_rec[:, h, 0:m, :], spill_rec[self.which][:, cols, :]).then_inc(self.filled[h], 16)
                            sp.dma_start(slot_pos[:, h, 0:m], spill_pos[self.which][:, cols]).then_inc(self.filled[h], 16)

            def pool(self, pool):
                m = self.m
                if m:
                    with loop(pool, self.turns) as k:
                        for h in range(2):
                            pool.wait_ge(self.filled[h], k * 32 + 32)
                            settle(pool, cell[0:1, 0:1], self.settled, k * 2 + h)
                            for j in range(m):
                                pool.indirect_dma_start(
                                    out=rec_d[self.which],
                                    out_offset=bass.IndirectOffsetOnAxis(ap=slot_pos[:, h, j:j + 1], axis=0),
                                    in_=slot_rec[:, h, j, :], in_offset=None).then_inc(self.sent[h], 16)
                    for h in range(2):
                        pool.wait_ge(self.sent[h], self.before + 16 * m * self.turns)

        moved = [0]

        def mover(name, m, turns=NC):
            mv = Mover(name, 1, moved[0], m, turns, sent, 8 * moved[0])
            moved[0] += 2 * m * turns
            return mv

        def layer_norm(name, src, dst, affine=None, into=None, plus=None, store=None):
            with ExitStack() as c:
                stats = sb(c, name + "_stats", [B, NB, 6])
                mean = sb(c, name + "_mean", [B, NB])
                half = sb(c, name + "_half", [B, NB])
                var = sb(c, name + "_var", [B, NB])
                rstd = sb(c, name + "_rstd", [B, NB])
                gain = sb(c, name + "_gain", [B, D])
                offset = sb(c, name + "_offset", [B, D])
                shift = sb(c, name + "_shift", [B, NB])
                own, var_done, sd_done, loaded, plus_done, shift_done, scaled = (
                    sem(name + x) for x in ("_own", "_var", "_sd", "_loaded", "_plus", "_shift", "_scaled"))
                with nc.Block() as block:
                    @block.sync
                    def _(sp):
                        if affine:
                            sp.dma_start(gain[:, :], affine[0].partition_broadcast(B)).then_inc(loaded, 16)
                            sp.dma_start(offset[:, :], affine[1].partition_broadcast(B)).then_inc(loaded, 16)

                    @block.gpsimd
                    def _(pool):
                        if plus is not None:
                            with loop(pool, NB // R) as t:
                                for i in range(R):
                                    r = bass.ds(t * R + i, 1)
                                    pool.tensor_tensor(one(into[:, r, :]), one(into[:, r, :]), one(plus[0:B, r, :]), ALU.add).then_inc(plus_done, 1)
                            pool.wait_ge(plus_done, NB)
                        if into is not None:
                            with loop(pool, NB // R) as t:
                                pool.wait_ge(scaled, t * R + R)
                                for i in range(R):
                                    r = bass.ds(t * R + i, 1)
                                    pool.tensor_tensor(one(into[:, r, :]), one(into[:, r, :]), one(src[0:B, r, :]), ALU.add)

                    @block.scalar
                    def _(act):
                        act.wait_ge(var_done, 1)
                        act.activation(rstd[:, :], var[:, :], ACT.Sqrt, bias=eps[0:B, 0:1]).then_inc(sd_done, 1)
                        if not affine:
                            act.wait_ge(shift_done, 1)
                            with loop(act, NB // R) as t:
                                for i in range(R_DVE, R):
                                    r = bass.ds(t * R + i, 1)
                                    act.activation(one(dst[0:B, r, :]), one(src[0:B, r, :]), ACT.Identity, bias=shift[:, r], scale=rstd[:, r])

                    @block.vector
                    def _(dve):
                        st = Steps(dve, own)
                        with loop(dve, NB // R, st, R) as t:
                            for i in range(R):
                                r = bass.ds(t * R + i, 1)
                                st.mark(dve.bn_stats(one(stats[:, r, :]), one(src[0:B, r, :])))
                        st.all()
                        me, mo, qe, qo = (stats[:, :, i] for i in (1, 4, 2, 5))
                        st.mark(dve.tensor_tensor(mean[:, :], me, mo, ALU.add))
                        st.mark(dve.tensor_tensor(half[:, :], me, mo, ALU.subtract))
                        st(dve.tensor_tensor(var[:, :], qe, qo, ALU.add))
                        st.mark(dve.tensor_scalar(mean[:, :], mean[:, :], 0.5, None, ALU.mult))
                        st(dve.scalar_tensor_tensor(half[:, :], half[:, :], 0.25, half[:, :], ALU.mult, ALU.mult))
                        dve.scalar_tensor_tensor(var[:, :], var[:, :], 1.0 / D, half[:, :], ALU.mult, ALU.add).then_inc(var_done, 1)
                        dve.wait_ge(sd_done, 1)
                        st(dve.reciprocal(rstd[:, :], rstd[:, :]))
                        if affine:
                            dve.wait_ge(loaded, 32)
                            with loop(dve, NB // R, st, R) as t:
                                for i in range(R):
                                    r = bass.ds(t * R + i, 1)
                                    s = one(src[0:B, r, :])
                                    st.mark(dve.scalar_tensor_tensor(s, s, mean[:, r], gain[:, :], ALU.subtract, ALU.mult))
                                st.all()
                                for i in range(R):
                                    r = bass.ds(t * R + i, 1)
                                    s = one(src[0:B, r, :])
                                    dve.scalar_tensor_tensor(s, s, rstd[:, r], offset[:, :], ALU.mult, ALU.add).then_inc(scaled, 1)
                        else:
                            dve.scalar_tensor_tensor(shift[:, :], mean[:, :], -1.0, rstd[:, :], ALU.mult, ALU.mult).then_inc(shift_done, 1)
                            with loop(dve, NB // R) as t:
                                for i in range(R_DVE):
                                    r = bass.ds(t * R + i, 1)
                                    dve.tensor_scalar(one(dst[0:B, r, :]), one(src[0:B, r, :]), mean[:, r], rstd[:, r],
                                                      ALU.subtract, ALU.mult)

        def transposed(c, name, srcs):
            n_src = len(srcs)
            stage = sb(c, name + "_stage", [B, n_src, CH, D])
            xT = sb(c, name + "_xT", [P, n_src * KF, TOK])
            psT = [pb(c, f"{name}_psT{i}") for i in range(n_src)]
            staged, turned, xT_done = (sem(name + x) for x in ("_staged", "_turned", "_xT"))

            def stage_rows(act, k):
                for i, src in enumerate(srcs):
                    act.wait_ge(turned, k)
                    act.activation(stage[:, i, :, :], src[0:B, bass.ds(k * CH, CH), :], ACT.Copy).then_inc(staged, 1)

            def turn(pe, k):
                pe.wait_ge(staged, k * n_src + n_src)
                for i in range(n_src):
                    for f in range(KF):
                        for b in range(CH):
                            at = (f * CH + b) * B
                            last = pe.transpose(psT[i][:, at:at + B], stage[:, i, b, f * P:(f + 1) * P], ident[0:B, 0:B])
                last.then_inc(turned, 1)

            def pe_chunks(pe, first, second):
                def chunk(k, end):
                    pe.wait_ge(xT_done, k * n_src + n_src)
                    first(k)
                    if not end:
                        turn(pe, k + 1)
                    second(k)

                turn(pe, 0)
                with loop(pe, NC - 1) as k:
                    chunk(k, False)
                chunk(NC - 1, True)

            def act_chunks(act, rest):
                def chunk(k, end):
                    act.wait_ge(turned, k + 1)
                    for i in range(n_src):
                        act.activation(xT[:, i * KF:(i + 1) * KF, :].rearrange("p f t -> p (f t)"),
                                       psT[i][:, 0:KF * TOK], ACT.Copy).then_inc(xT_done, 1)
                    if not end:
                        stage_rows(act, k + 1)
                    rest(k)

                stage_rows(act, 0)
                with loop(act, NC - 1) as k:
                    chunk(k, False)
                chunk(NC - 1, True)

            return xT, pe_chunks, act_chunks

        def mlp(name, srcs, experts, width, func, per, final, setup=None, m=0):
            nk, nf = KF * len(srcs), width // P
            with ExitStack() as c:
                xT, pe_chunks, act_chunks = transposed(c, name, srcs)
                w1 = [sb(c, f"{name}_w1_{e}", [P, nk, width]) for e in range(len(experts))]
                w2 = [sb(c, f"{name}_w2_{e}", [P, nf, D]) for e in range(len(experts))]
                b1 = [sb(c, f"{name}_b1_{e}", [P, nf]) for e in range(len(experts))]
                b2 = [sb(c, f"{name}_b2_{e}", [B, D]) for e in range(len(experts))]
                hT = sb(c, name + "_hT", [P, len(experts) * nf, TOK])
                tmp = sb(c, name + "_tmp", [B, CH, D])
                psH = [pb(c, f"{name}_psH{i}") for i in range(2)]
                psY = [pb(c, f"{name}_psY{e}") for e in range(len(experts))]
                loaded, h_mm, h_done, y_mm, fin, own = (
                    sem(name + x) for x in ("_loaded", "_h_mm", "_h", "_y_mm", "_fin", "_own"))
                total = len(experts) * nf
                mv = mover(name, m)
                with nc.Block() as block:
                    @block.sync
                    def _(sp):
                        for e, w in enumerate(experts):
                            for dst, src in ((w1[e][:, :, :], w[0]), (b1[e][:, :], w[1]), (w2[e][:, :, :], w[2]), (b2[e][:, :], w[3])):
                                if src is not None:
                                    src = src(sp, e) if callable(src) else src
                                    sp.dma_start(dst, src).then_inc(loaded, 16)
                        mv.sp(sp)
                    n_loads = 16 * sum(x is not None for w in experts for x in w)

                    @block.gpsimd
                    def _(pool):
                        mv.pool(pool)

                    @block.tensor
                    def _(pe):
                        pe.wait_ge(loaded, n_loads)

                        def first(k):
                            for i in range(total):
                                e, f = divmod(i, nf)
                                if i >= 2:
                                    pe.wait_ge(h_done, k * total + i - 1)
                                for j in range(nk):
                                    last = pe.matmul(psH[i % 2][:, 0:TOK], w1[e][:, j, f * P:(f + 1) * P], xT[:, j, :],
                                                     start=(j == 0), stop=(j == nk - 1))
                                last.then_inc(h_mm, 1)

                        def second(k):
                            pe.wait_ge(fin, k)
                            pe.wait_ge(h_done, k * total + total)
                            for e in range(len(experts)):
                                for b in range(CH):
                                    for f in range(nf):
                                        last = pe.matmul(psY[e][0:B, b * D:(b + 1) * D],
                                                         hT[:, e * nf + f, b * B:(b + 1) * B], w2[e][:, f, :],
                                                         start=(f == 0), stop=(f == nf - 1))
                            last.then_inc(y_mm, 1)

                        pe_chunks(pe, first, second)

                    @block.scalar
                    def _(act):
                        act.wait_ge(loaded, n_loads)

                        def rest(k):
                            for i in range(total):
                                e, f = divmod(i, nf)
                                act.wait_ge(h_mm, k * total + i + 1)
                                kw = {} if experts[e][1] is None else {"bias": b1[e][:, f:f + 1]}
                                act.activation(hT[:, i, :], psH[i % 2][:, 0:TOK], func, **kw).then_inc(h_done, 1)

                        act_chunks(act, rest)

                    @block.vector
                    def _(dve):
                        st = Steps(dve, own)
                        dve.wait_ge(loaded, n_loads)
                        if setup:
                            setup(dve, st, b2)
                        with loop(dve, NC, st, per) as k:
                            dve.wait_ge(y_mm, k + 1)
                            final(dve, st, k, [p[0:B, :].rearrange("p (b d) -> p b d", b=CH) for p in psY], b2, tmp).then_inc(fin, 1)

        def linear(name, src, w_dram, bias, per, final, m=0, turns=NC):
            with ExitStack() as c:
                xT, pe_chunks, act_chunks = transposed(c, name, [src])
                w = sb(c, name + "_w", [P, KF, D])
                b2 = sb(c, name + "_b", [B, D])
                psY = pb(c, name + "_psY")
                loaded, y_mm, fin, own = (sem(name + x) for x in ("_loaded", "_y_mm", "_fin", "_own"))
                mv = mover(name, m, turns)
                with nc.Block() as block:
                    @block.sync
                    def _(sp):
                        sp.dma_start(w[:, :, :], w_dram).then_inc(loaded, 16)
                        if bias is not None:
                            sp.dma_start(b2[:, :], bias.partition_broadcast(B)).then_inc(loaded, 16)
                        mv.sp(sp)
                    n_loads = 32 if bias is not None else 16

                    @block.gpsimd
                    def _(pool):
                        mv.pool(pool)

                    @block.tensor
                    def _(pe):
                        pe.wait_ge(loaded, n_loads)

                        def first(k):
                            pe.wait_ge(fin, k)
                            for b in range(CH):
                                for f in range(KF):
                                    last = pe.matmul(psY[0:B, b * D:(b + 1) * D], xT[:, f, b * B:(b + 1) * B], w[:, f, :],
                                                     start=(f == 0), stop=(f == KF - 1))
                            last.then_inc(y_mm, 1)

                        pe_chunks(pe, first, lambda k: None)

                    @block.scalar
                    def _(act):
                        act_chunks(act, lambda k: None)

                    @block.vector
                    def _(dve):
                        st = Steps(dve, own)
                        dve.wait_ge(loaded, n_loads)
                        with loop(dve, NC, st, per) as k:
                            dve.wait_ge(y_mm, k + 1)
                            final(dve, st, k, psY[0:B, :].rearrange("p (b d) -> p b d", b=CH), b2).then_inc(fin, 1)

        def attention_sums(c0, name, wkv_dram, edge=None, table=None, m=0):
            kvd = sb(c0, name + "_kvd", [P, KF, P + HH])
            with ExitStack() as c:
                xT, pe_chunks, act_chunks = transposed(c, name, [XN])
                wkv = sb(c, name + "_wkv", [P, KF, 2 * D])
                k_sb = sb(c, name + "_k", [B, CH, D])
                e_sb = sb(c, name + "_e", [B, CH, D])
                v_sb = sb(c, name + "_v", [B, CH, KF, P + 1])
                kva = sb(c, name + "_kva", [P, KF * (P + 1)])
                psKV = [pb(c, f"{name}_psKV{i}") for i in range(CH)]
                psA = pb(c, name + "_psA")
                if edge:
                    wqk = sb(c, name + "_wqk", [P, KF, 2 * SMALL])
                    bqk = sb(c, name + "_bqk", [1, 2 * SMALL])
                    bk = sb(c, name + "_bk", [SMALL, 1])
                    flat = U[:, :, :].rearrange("p b d -> p (b d)")
                    q_all = flat[:, 0:NB * SMALL].rearrange("p (b n) -> p b n", n=SMALL)
                    k_all = flat[:, NB * SMALL:2 * NB * SMALL].rearrange("p (b n) -> p b n", n=SMALL)
                    psQ = pb(c, name + "_psQ")
                    psK = pb(c, name + "_psK")
                loaded, kv_mm, e_done, k_done, v_done, a_mm, a_done, own, stored, setup = (
                    sem(name + x) for x in ("_loaded", "_kv_mm", "_e", "_k", "_v", "_a_mm", "_a", "_own", "_stored", "_setup"))
                mv = mover(name, m)
                qk_mm, qk_done, low_done = sem(name + "_qk_mm"), sem(name + "_qk"), sem(name + "_low")
                with nc.Block() as block:
                    @block.sync
                    def _(sp):
                        sp.dma_start(wkv[:, :, :], wkv_dram).then_inc(loaded, 16)
                        if edge:
                            sp.dma_start(wqk[:, :, :], edge["wqk"]).then_inc(loaded, 16)
                            sp.dma_start(bqk[:, :], edge["bqk"]).then_inc(loaded, 16)
                            sp.dma_start(bk[:, :], edge["bk"]).then_inc(loaded, 16)
                        for i in range(5):
                            n = NB // 5
                            sp.dma_start(rows(table)[:, i * n:(i + 1) * n, 0:D], XN[0:B, i * n:(i + 1) * n, :]).then_inc(stored, 16)
                        mv.sp(sp)
                        if edge:
                            sp.wait_ge(qk_done, 3 * NC)
                            sp.dma_start(rows(table)[:, :, D:D + SMALL], q_all[:, :, :]).then_inc(stored, 16)
                        sp.wait_ge(stored, 16 * (6 if edge else 5))

                    n_loads = 64 if edge else 16

                    @block.gpsimd
                    def _(pool):
                        mv.pool(pool)

                    @block.tensor
                    def _(pe):
                        pe.wait_ge(loaded, n_loads)
                        pe.wait_ge(setup, 1)

                        def first(k):
                            for b in range(CH):
                                for f in range(KF):
                                    last = pe.matmul(psKV[b][0:B, :], xT[:, f, b * B:(b + 1) * B], wkv[:, f, :],
                                                     start=(f == 0), stop=(f == KF - 1))
                            last.then_inc(kv_mm, 1)
                            if edge:
                                for b in range(CH):
                                    o = psQ[0:B, b * 64:b * 64 + 2 * SMALL]
                                    pe.matmul(o, ones[0:1, 0:B], bqk[:, :], start=True, stop=False)
                                    for f in range(KF):
                                        pe.matmul(o, xT[:, f, b * B:(b + 1) * B], wqk[:, f, :], start=False, stop=(f == KF - 1))
                                for f in range(KF):
                                    last = pe.matmul(psK[0:SMALL, 0:TOK], wqk[:, f, SMALL:2 * SMALL], xT[:, f, :],
                                                     start=(f == 0), stop=(f == KF - 1))
                                last.then_inc(qk_mm, 1)

                        def second(k):
                            pe.wait_ge(k_done, k + 1)
                            pe.wait_ge(v_done, k * CH + CH)
                            pe.wait_ge(a_done, k)
                            if edge:
                                pe.wait_ge(qk_done, 3 * k + 3)
                            for f in range(KF):
                                for b in range(CH):
                                    last = pe.matmul(psA[:, f * (P + 1):(f + 1) * (P + 1)], k_sb[:, b, f * P:(f + 1) * P],
                                                     v_sb[:, b, f, :], start=(b == 0), stop=(b == CH - 1))
                            last.then_inc(a_mm, 1)

                        pe_chunks(pe, first, second)

                    @block.scalar
                    def _(act):
                        act.wait_ge(loaded, n_loads)
                        act.wait_ge(setup, 1)

                        def rest(k):
                            act.wait_ge(low_done, k + 1)
                            for b in range(CH):
                                act.activation(v_sb[:, b, :, 0:P], psKV[b][0:B, D:2 * D].rearrange("p (f d) -> p f d", f=KF),
                                               ACT.Copy).then_inc(v_done, 1)
                            act.activation(e_sb[:, :, :], e_sb[:, :, :], ACT.Exp).then_inc(e_done, 1)
                            if edge:
                                act.wait_ge(qk_mm, k + 1)
                                q = psQ[0:B, 0:64 * CH].rearrange("p (b n) -> p b n", b=CH)
                                act.activation(q_all[:, bass.ds(k * CH, CH), :], q[:, :, 0:SMALL], ACT.Tanh).then_inc(qk_done, 1)
                                act.activation(k_all[:, bass.ds(k * CH, CH), :], q[:, :, SMALL:2 * SMALL], ACT.Copy).then_inc(qk_done, 1)
                                act.activation(edge["kT"][:, bass.ds(k * CH, CH), :], psK[0:SMALL, 0:TOK].rearrange("p (b n) -> p b n", b=CH),
                                               ACT.Identity, bias=bk[:, 0:1]).then_inc(qk_done, 1)

                        act_chunks(act, rest)

                    @block.vector
                    def _(dve):
                        st = Steps(dve, own)
                        dve.memset(kvd[:, :, :], 0.0)
                        st(dve.memset(kva[:, :], 0.0))
                        dve.memset(v_sb[:, :, :, P:P + 1], 1.0).then_inc(setup, 1)
                        with loop(dve, NC) as k:
                            dve.wait_ge(kv_mm, k + 1)
                            for b in range(CH):
                                last = dve.tensor_scalar(e_sb[:, b, :], psKV[b][0:B, 0:D], 0.0, None, ALU.min)
                            last.then_inc(low_done, 1)
                            dve.wait_ge(e_done, k + 1)
                            for b in range(CH):
                                last = dve.scalar_tensor_tensor(k_sb[:, b, :], psKV[b][0:B, 0:D], 0.0, e_sb[:, b, :], ALU.max, ALU.add)
                            last.then_inc(k_done, 1)
                            dve.wait_ge(a_mm, k + 1)
                            dve.wait_ge(a_done, k)
                            dve.tensor_tensor(kva[:, :], kva[:, :], psA[:, 0:KF * (P + 1)], ALU.add).then_inc(a_done, 1)
                        dve.wait_ge(a_done, NC)
                        for f in range(KF):
                            for h in range(HH):
                                r = slice(h * HD, (h + 1) * HD)
                                dve.tensor_copy(kvd[r, f, h * HD:(h + 1) * HD], kva[r, f * (P + 1) + h * HD:f * (P + 1) + (h + 1) * HD])
                                dve.tensor_copy(kvd[r, f, P + h:P + h + 1], kva[r, f * (P + 1) + P:f * (P + 1) + P + 1])
                        if edge:
                            dve.wait_ge(qk_done, 3 * NC)
                            st(dve.tensor_tensor(k_all[:, :, :], k_all[:, :, :], q_all[:, :, :], ALU.mult))
                            dve.tensor_reduce(edge["m"][:, :], k_all[:, :, :], AX.X, ALU.add)
                            dve.memset(edge["l"][:, :], 1.0)
            return kvd

        def attention_rows(name, wq_dram, kvd, residual, m=0):
            with ExitStack() as c:
                xT, pe_chunks, act_chunks = transposed(c, name, [XN])
                wq = sb(c, name + "_wq", [P, KF, D])
                e_sb = sb(c, name + "_e", [P, KF, TOK])
                qT = sb(c, name + "_qT", [P, KF, TOK])
                z = sb(c, name + "_z", [B, CH, HEADS])
                psQ = [pb(c, f"{name}_psQ{i}") for i in range(KF)]
                psM = [pb(c, f"{name}_psM{i}") for i in range(CH)]
                loaded, q_mm, low_done, e_done, q_done, m_mm, fin, own = (
                    sem(name + x) for x in ("_loaded", "_q_mm", "_low", "_e", "_q", "_m_mm", "_fin", "_own"))
                mv = mover(name, m)
                with nc.Block() as block:
                    @block.sync
                    def _(sp):
                        sp.dma_start(wq[:, :, :], wq_dram).then_inc(loaded, 16)
                        mv.sp(sp)

                    @block.gpsimd
                    def _(pool):
                        mv.pool(pool)

                    @block.tensor
                    def _(pe):
                        pe.wait_ge(loaded, 16)

                        def first(k):
                            for f in range(KF):
                                for j in range(KF):
                                    last = pe.matmul(psQ[f][:, 0:TOK], wq[:, j, f * P:(f + 1) * P], xT[:, j, :],
                                                     start=(j == 0), stop=(j == KF - 1))
                            last.then_inc(q_mm, 1)

                        def second(k):
                            pe.wait_ge(q_done, k + 1)
                            pe.wait_ge(fin, k)
                            for b in range(CH):
                                for f in range(KF):
                                    last = pe.matmul(psM[b][0:B, f * (P + HH):(f + 1) * (P + HH)], qT[:, f, b * B:(b + 1) * B],
                                                     kvd[:, f, :], start=True, stop=True)
                            last.then_inc(m_mm, 1)

                        pe_chunks(pe, first, second)

                    @block.scalar
                    def _(act):
                        def rest(k):
                            act.wait_ge(low_done, k + 1)
                            act.activation(e_sb[:, :, :], e_sb[:, :, :], ACT.Exp).then_inc(e_done, 1)

                        act_chunks(act, rest)

                    @block.vector
                    def _(dve):
                        st = Steps(dve, own)
                        with loop(dve, NC, st, 2 + CH if residual else 2) as k:
                            dve.wait_ge(q_mm, k + 1)
                            for f in range(KF):
                                last = dve.tensor_scalar(e_sb[:, f, :], psQ[f][:, 0:TOK], 0.0, None, ALU.min)
                            last.then_inc(low_done, 1)
                            dve.wait_ge(e_done, k + 1)
                            for f in range(KF):
                                last = dve.scalar_tensor_tensor(qT[:, f, :], psQ[f][:, 0:TOK], 0.0, e_sb[:, f, :], ALU.max, ALU.add)
                            last.then_inc(q_done, 1)
                            dve.wait_ge(m_mm, k + 1)
                            msg = [psM[b][0:B, 0:KF * (P + HH)].rearrange("p (f n) -> p f n", f=KF) for b in range(CH)]
                            for b in range(CH):
                                last = dve.tensor_scalar(z[:, b, :].rearrange("p (f h) -> p f h", f=KF), msg[b][:, :, P:P + HH],
                                                         ATT_EPS, None, ALU.add)
                            st(last)
                            st(dve.reciprocal(z[:, :, :], z[:, :, :]))
                            for b in range(CH):
                                u = one(U[:, bass.ds(k * CH + b, 1), :])
                                n = dve.tensor_tensor(u.rearrange("p (f h d) -> p f h d", f=KF, h=HH),
                                                      msg[b][:, :, 0:P].rearrange("p f (h d) -> p f h d", h=HH),
                                                      z[:, b, :].rearrange("p (f h) -> p f h", f=KF).unsqueeze(3).broadcast_to([B, KF, HH, HD]), ALU.mult)
                                if residual:
                                    st(n)
                                    n = dve.tensor_tensor(u, u, one(XN[0:B, bass.ds(k * CH + b, 1), :]), ALU.add)
                            n.then_inc(fin, 1)


        def edge_walk(name, which, table, width, rec_t, idx, rec_free):
            W = width
            rows_t = XN[:, :, :].rearrange("p b d -> p (b d)")[:, 0:RING * SUB * W].rearrange("p (r s w) -> p r s w", r=RING, s=SUB)
            rec_v = rec_d[which].rearrange("(g p s) w -> g p (s w)", p=P, s=SUB)
            rec_ready = [sem(f"{name}_rec{s}") for s in range(RING)]
            idx_ready = [sem(f"{name}_idx{s}") for s in range(RING)]
            got = [pool_dma_sem(f"{name}_got{s}") for s in range(RING)]
            used = [sem(f"{name}_used{s}") for s in range(RING)]
            settled = sem(name + "_settled")

            def sp_part(sp):
                with loop(sp, NS // RING) as t:
                    for s in range(RING):
                        g = sp.value_load(step_grp[which][0:1, bass.ds(t * RING + s, 1)], min_val=0, max_val=NG - 1)
                        sp.wait_ge(rec_free[s], t)
                        sp.wait_ge(idx_ready[s], t)
                        sp.dma_start(rec_t[:, s, :, :].rearrange("p s w -> p (s w)"),
                                     rec_v[bass.ds(g, 1), :, :].rearrange("g p w -> (g p) w")).then_inc(rec_ready[s], 16)

            def act_idx(act, t, s):
                act.wait_ge(rec_ready[s], t * 16 + 16)
                act.wait_ge(got[s], t * (16 * SUB))
                act.activation(idx[:, s, :], rec_t[:, s, :, 1], ACT.Copy).then_inc(idx_ready[s], 1)

            def pool_part(pool):
                with loop(pool, NS // RING) as t:
                    for s in range(RING):
                        pool.wait_ge(idx_ready[s], t + 1)
                        pool.wait_ge(used[s], t)
                        settle(pool, cell[0:1, 0:1], settled, t * RING + s)
                        for j in range(SUB):
                            pool.indirect_dma_start(out=rows_t[:, s, j, :], out_offset=None, in_=table,
                                                    in_offset=bass.IndirectOffsetOnAxis(ap=idx[:, s, j:j + 1], axis=0)).then_inc(got[s], 16)

            return rows_t, rec_ready, got, used, sp_part, act_idx, pool_part

        def each_step(eng, steps, per, body):
            T = NS // RING
            for s in range(RING):
                body(0, s)
            with loop(eng, T - 2, steps, per) as u:
                for s in range(RING):
                    body(u + 1, s)
            for s in range(RING):
                body(T - 1, s)

        def step(t, s):
            return t * RING + s

        def near(t, s, n):
            if isinstance(t, int) and not 0 <= t * RING + s + n < NS:
                return None
            return t + (s + n) // RING, (s + n) % RING

        def begins(t, s, n=1):
            return isinstance(t, int) and t * RING + s < n

        def edge_softmax(edge):
            name, W = "gat", D + SMALL
            kT, m, l = edge["kT"], edge["m"], edge["l"]
            SC = 1.0 / float(np.sqrt(SMALL))
            with ExitStack() as c:
                rec_t = sb(c, name + "_rec", [P, RING, SUB, RW])
                idx = sb(c, name + "_idx", [P, RING, SUB], I32)
                lf = sb(c, name + "_lf", [P, RING, SUB])
                lk = sb(c, name + "_lk", [P, RING, SUB], BF16)
                kTs = sb(c, name + "_kTs", [SMALL, 2, B])
                free = RING * SUB * W

                def room(p, n):
                    nonlocal free
                    free += 2 * n
                    return XN[0:p, :, :].rearrange("p b d -> p (b d)")[:, free - 2 * n:free].rearrange("p (a n) -> p a n", a=2)

                qT, S, pT = room(SMALL, G), room(B, G), room(B, G)
                pE = sb(c, name + "_pE", [P, 2, SUB * B])
                pen = sb(c, name + "_pen", [B, 2, G])
                mx, mo, mn, nm, df, sc, rs, scl, rsl = (
                    sb(c, f"{name}_{x}", [B, 2]) for x in ("mx", "mo", "mn", "nm", "df", "sc", "rs", "scl", "rsl"))
                psA, psB, psP = pb(c, name + "_psA"), pb(c, name + "_psB", dt=BF16), pb(c, name + "_psP")
                psS = [pb(c, f"{name}_psS{i}") for i in range(2)]
                psE = [pb(c, f"{name}_psE{i}") for i in range(2)]
                qk_done, pen_done, s_mm, s_done, e_done, p_turned, p_done, own, ready = (
                    sem(f"{name}_{x}") for x in ("qk", "pen", "s_mm", "s", "e", "p_turned", "p", "own", "ready"))
                added = [sem(f"{name}_added{i}") for i in range(2)]
                near_done = [sem(f"{name}_near{s}") for s in range(RING)]
                turned = [sem(f"{name}_turned{s}") for s in range(RING)]
                rows_t, rec_ready, got, used, sp_part, act_idx, pool_part = edge_walk(
                    name, 0, table0, W, rec_t, idx, near_done)

                with nc.Block() as block:
                    @block.vector
                    def _(dve):
                        dve.tensor_copy(U[:, :, :], XN[0:B, :, :])

                with nc.Block() as block:
                    @block.sync
                    def _(sp):
                        sp_part(sp)

                    @block.gpsimd
                    def _(pool):
                        pool_part(pool)

                    @block.tensor
                    def _(pe):
                        def turn(t, s):
                            x = step(t, s)
                            pe.wait_ge(got[s], t * (16 * SUB) + 16 * SUB)
                            pe.wait_ge(near_done[s], t + 1)
                            if not begins(t, s):
                                pe.wait_ge(qk_done, x)
                                pe.wait_ge(pen_done, x)
                            for j in range(SUB):
                                pe.transpose(psA[0:SMALL, j * P:(j + 1) * P], rows_t[:, s, j, D:W], ident[:, :])
                            for j in range(SUB):
                                last = pe.transpose(psB[0:B, j * P:(j + 1) * P],
                                                    lk[:, s, j:j + 1].broadcast_to([P, B]), ident16[:, :])
                            last.then_inc(turned[s], 1)

                        def scores(t, s):
                            x, d = step(t, s), s % 2
                            pe.wait_ge(qk_done, x + 1)
                            if not begins(t, s, 2):
                                pe.wait_ge(s_done, x - 1)
                            pe.matmul(psS[d][0:B, :], kTs[:, d, :], qT[:, d, :], start=True, stop=True).then_inc(s_mm, 1)

                        def weights(t, s):
                            x, d = step(t, s), s % 2
                            pe.wait_ge(e_done, x + 1)
                            pe.wait_ge(p_done, x)
                            for j in range(SUB):
                                last = pe.transpose(psP[:, j * B:(j + 1) * B], pT[:, d, j * P:(j + 1) * P], ident[0:B, 0:B])
                            last.then_inc(p_turned, 1)

                        def sums(t, s):
                            x, d = step(t, s), s % 2
                            pe.wait_ge(p_done, x + 1)
                            pe.wait_ge(added[d], t * (RING // 2) + s // 2)
                            for j in range(SUB):
                                last = pe.matmul(psE[d][0:B, 0:D], pE[:, d, j * B:(j + 1) * B], rows_t[:, s, j, 0:D],
                                                 start=(j == 0), stop=(j == SUB - 1))
                            last.then_inc(used[s], 1)

                        def body(t, s):
                            if near(t, s, 1):
                                scores(*near(t, s, 1))
                            if near(t, s, 2):
                                turn(*near(t, s, 2))
                            if near(t, s, -1):
                                sums(*near(t, s, -1))
                            weights(t, s)

                        turn(0, 0)
                        turn(0, 1)
                        scores(0, 0)
                        each_step(pe, None, 0, body)
                        sums(NS // RING - 1, RING - 1)

                    @block.scalar
                    def _(act):
                        def qk(t, s):
                            d = s % 2
                            b = act.value_load(step_blk[0][0:1, bass.ds(step(t, s), 1)], min_val=0, max_val=NB - 1)
                            act.wait_ge(turned[s], t + 1)
                            if not begins(t, s, 2):
                                act.wait_ge(s_mm, step(t, s) - 1)
                            act.activation(kTs[:, d, :], one(kT[:, bass.ds(b, 1), :]), ACT.Copy)
                            act.activation(qT[:, d, :], psA[0:SMALL, :], ACT.Copy).then_inc(qk_done, 1)

                        def body(t, s):
                            d, x = s % 2, step(t, s)
                            if near(t, s, IDX):
                                act_idx(act, *near(t, s, IDX))
                            act.wait_ge(s_done, x + 1)
                            act.activation(pT[:, d, :], S[:, d, :], ACT.Exp, bias=nm[:, d:d + 1], scale=SC, accum_out=rs[:, d:d + 1])
                            act.activation(sc[:, d:d + 1], df[:, d:d + 1], ACT.Exp).then_inc(e_done, 1)
                            if near(t, s, 2):
                                qk(*near(t, s, 2))
                            act.wait_ge(p_turned, x + 1)
                            act.activation(pE[:, d, :], psP[:, 0:SUB * B], ACT.Copy).then_inc(p_done, 1)

                        for i in range(IDX):
                            act_idx(act, 0, i)
                        qk(0, 0)
                        qk(0, 1)
                        each_step(act, None, 0, body)

                    @block.vector
                    def _(dve):
                        st = Steps(dve, own)

                        def targets(t, s):
                            x = step(t, s)
                            dve.wait_ge(rec_ready[s], t * 16 + 16)
                            st(dve.tensor_scalar(lf[:, s, :], rec_t[:, s, :, 0], step_node[0][:, bass.ds(x, 1)], -1.0, ALU.subtract, ALU.max))
                            dve.tensor_scalar(lk[:, s, :], lf[:, s, :], float(B), None, ALU.min).then_inc(near_done[s], 1)

                        def masks(t, s):
                            d = s % 2
                            dve.wait_ge(turned[s], t + 1)
                            dve.tensor_scalar(pen[:, d, :], psB[0:B, :], iota_p[0:B, 0:1], -BIG, ALU.not_equal, ALU.mult).then_inc(pen_done, 1)

                        def maxima(t, s):
                            x, d = step(t, s), s % 2
                            b = dve.value_load(step_blk[0][0:1, bass.ds(x, 1)], min_val=0, max_val=NB - 1)
                            mb = m[:, bass.ds(b, 1)]
                            dve.wait_ge(pen_done, x + 1)
                            dve.wait_ge(s_mm, x + 1)
                            if not begins(t, s, 2):
                                dve.wait_ge(e_done, x - 1)
                            st.all()
                            st.mark(dve.tensor_copy(mo[:, d:d + 1], mb))
                            st(dve.tensor_tensor_reduce(out=S[:, d, :], in0=psS[d][0:B, :], in1=pen[:, d, :], scale=1.0, scalar=-BIG,
                                                        op0=ALU.add, op1=ALU.max, accum_out=mx[:, d:d + 1]))
                            st(dve.tensor_tensor(mn[:, d:d + 1], mo[:, d:d + 1], mx[:, d:d + 1], ALU.max))
                            st(dve.tensor_scalar(nm[:, d:d + 1], mn[:, d:d + 1], -SC, None, ALU.mult))
                            dve.scalar_tensor_tensor(df[:, d:d + 1], mo[:, d:d + 1], SC, nm[:, d:d + 1], ALU.mult, ALU.add).then_inc(s_done, 1)
                            st.mark(dve.tensor_copy(mb, mn[:, d:d + 1]))

                        def add(t, s):
                            d = s % 2
                            b = dve.value_load(step_blk[0][0:1, bass.ds(step(t, s), 1)], min_val=0, max_val=NB - 1)
                            lb, ub = l[:, bass.ds(b, 1)], one(U[:, bass.ds(b, 1), :])
                            dve.wait_ge(used[s], t + 1)
                            st.all()
                            st.mark(dve.scalar_tensor_tensor(lb, lb, scl[:, d:d + 1], rsl[:, d:d + 1], ALU.mult, ALU.add))
                            dve.wait_ge(added[1 - d], t * (RING // 2) + (s + 1) // 2)
                            dve.scalar_tensor_tensor(ub, ub, scl[:, d:d + 1], psE[d][0:B, 0:D], ALU.mult, ALU.add).then_inc(added[d], 1)

                        def keep(t, s):
                            d = s % 2
                            dve.wait_ge(e_done, step(t, s) + 1)
                            st.mark(dve.tensor_copy(scl[:, d:d + 1], sc[:, d:d + 1]))
                            st.mark(dve.tensor_copy(rsl[:, d:d + 1], rs[:, d:d + 1]))

                        def body(t, s):
                            if near(t, s, 1):
                                maxima(*near(t, s, 1))
                            if near(t, s, 3):
                                targets(*near(t, s, 3))
                            if near(t, s, 2):
                                masks(*near(t, s, 2))
                            if near(t, s, -1):
                                add(*near(t, s, -1))
                            keep(t, s)

                        for i in range(3):
                            targets(0, i)
                        masks(0, 0)
                        masks(0, 1)
                        maxima(0, 0)
                        each_step(dve, st, RING * 9, body)
                        add(NS // RING - 1, RING - 1)

        def edge_sums():
            name = "gcn"
            with ExitStack() as c:
                rec_t = sb(c, name + "_rec", [P, RING, SUB, RW])
                idx = sb(c, name + "_idx", [P, RING, SUB], I32)
                lk = sb(c, name + "_lk", [P, 2, SUB])
                pE = sb(c, name + "_pE", [P, 2, SUB, B])
                psE = [pb(c, f"{name}_psE{i}") for i in range(2)]
                rec_free = [sem(f"{name}_rec_free{s}") for s in range(RING)]
                rows_t, rec_ready, got, used, sp_part, act_idx, pool_part = edge_walk(
                    name, 1, table1, D, rec_t, idx, rec_free)
                own = sem(name + "_own")
                added = [sem(f"{name}_added{i}") for i in range(2)]

                with nc.Block() as block:
                    @block.vector
                    def _(dve):
                        dve.memset(U[:, :, :], 0.0)

                with nc.Block() as block:
                    @block.sync
                    def _(sp):
                        sp_part(sp)

                    @block.gpsimd
                    def _(pool):
                        pool_part(pool)

                    @block.scalar
                    def _(act):
                        with loop(act, NS // RING) as t:
                            for s in range(RING):
                                act_idx(act, t, s)

                    @block.tensor
                    def _(pe):
                        with loop(pe, NS // RING) as t:
                            for s in range(RING):
                                d = s % 2
                                pe.wait_ge(got[s], t * (16 * SUB) + 16 * SUB)
                                pe.wait_ge(rec_free[s], t + 1)
                                pe.wait_ge(added[d], t * (RING // 2) + s // 2)
                                for j in range(SUB):
                                    last = pe.matmul(psE[d][0:B, 0:D], pE[:, d, j, :], rows_t[:, s, j, :],
                                                     start=(j == 0), stop=(j == SUB - 1))
                                last.then_inc(used[s], 1)

                    @block.vector
                    def _(dve):
                        st = Steps(dve, own)

                        def weights(t, s):
                            x, d = t * RING + s, s % 2
                            dve.wait_ge(rec_ready[s], t * 16 + 16)
                            if near(t, s, -2):
                                u, v = near(t, s, -2)
                                dve.wait_ge(used[v], u + 1)
                            st(dve.tensor_scalar(lk[:, d, :], rec_t[:, s, :, 0], step_node[1][:, bass.ds(x, 1)], None, ALU.subtract))
                            for j in range(SUB):
                                last = dve.tensor_scalar(pE[:, d, j, :], iota_n[:, :], lk[:, d, j:j + 1], rec_t[:, s, j, 2:3],
                                                         ALU.is_equal, ALU.mult)
                            last.then_inc(rec_free[s], 1)

                        def body(t, s):
                            d = s % 2
                            if near(t, s, 1):
                                weights(*near(t, s, 1))
                            b = dve.value_load(step_blk[1][0:1, bass.ds(t * RING + s, 1)], min_val=0, max_val=NB - 1)
                            ub = one(U[:, bass.ds(b, 1), :])
                            dve.wait_ge(used[s], t + 1)
                            dve.wait_ge(added[1 - d], t * (RING // 2) + (s + 1) // 2)
                            dve.tensor_tensor(ub, ub, psE[d][0:B, 0:D], ALU.add).then_inc(added[d], 1)

                        weights(0, 0)
                        each_step(dve, st, RING, body)

        def route_rows(selw):
            name = "topk"
            with ExitStack() as c:
                wr = sb(c, name + "_wr", [B, D])
                br = sb(c, name + "_br", [B, 1])
                w = sb(c, name + "_w", [B, NB])
                v = sb(c, name + "_v", [B, NB])
                junk = sb(c, name + "_junk", [B, D])
                eq = sb(c, name + "_eq", [B, NB])
                gt = sb(c, name + "_gt", [B, NB])
                tot = sb(c, name + "_tot", [B, NB])
                cum = sb(c, name + "_cum", [B, NB])
                cnt, pos, sign, kk, thr, take = (sb(c, f"{name}_{x}", [B, 1]) for x in ("cnt", "pos", "sign", "kk", "thr", "take"))
                T, bit, cand, add = (sb(c, f"{name}_{x}", [B, 1], I32) for x in ("T", "bit", "cand", "add"))
                ps = pb(c, name + "_ps")
                loaded, own, cnt_done, sum_done, eq_done, rank_done = (
                    sem(f"{name}_{x}") for x in ("loaded", "own", "cnt", "sum", "eq", "rank"))
                BITS = 31
                with nc.Block() as block:
                    @block.sync
                    def _(sp):
                        sp.dma_start(wr[:, :], A["L0_ffn_wr"].partition_broadcast(B)).then_inc(loaded, 16)
                        sp.dma_start(br[:, :], A["L0_ffn_br"].partition_broadcast(B)).then_inc(loaded, 16)

                    @block.tensor
                    def _(pe):
                        with loop(pe, BITS + 2) as i:
                            pe.wait_ge(cnt_done, i + 1)
                            pe.matmul(ps[0:B, 0:1], ones[0:B, 0:B], cnt[:, :], start=True, stop=True).then_inc(sum_done, 1)
                        pe.wait_ge(eq_done, 1)
                        pe.matmul(ps[0:B, 64:64 + NB], lower[0:B, 0:B], eq[:, :], start=True, stop=True)
                        pe.matmul(ps[0:B, 128:128 + NB], ones[0:B, 0:B], eq[:, :], start=True, stop=True).then_inc(rank_done, 1)

                    @block.vector
                    def _(dve):
                        st = Steps(dve, own)
                        dve.wait_ge(loaded, 32)
                        with loop(dve, NB, st, 1) as b:
                            r = bass.ds(b, 1)
                            st(dve.scalar_tensor_tensor(junk[:, :], one(XN[0:B, r, :]), 1.0, wr[:, :], ALU.mult, ALU.mult,
                                                        accum_out=w[:, r]))
                        st(dve.tensor_scalar(w[:, :], w[:, :], br[:, 0:1], None, ALU.add))
                        dve.tensor_scalar(v[:, :], w[:, :], 0.0, 0.0, ALU.is_ge, ALU.add, accum_out=cnt[:, :]).then_inc(cnt_done, 1)
                        dve.wait_ge(sum_done, 1)
                        st(dve.tensor_scalar(pos[:, :], ps[0:B, 0:1], float(TOPK), None, ALU.is_ge))
                        st(dve.tensor_scalar(sign[:, :], pos[:, :], 2.0, -1.0, ALU.mult, ALU.add))
                        st(dve.tensor_scalar(kk[:, :], pos[:, :], float(2 * TOPK - N - 1), float(N - TOPK + 1), ALU.mult, ALU.add))
                        st(dve.tensor_scalar(v[:, :], w[:, :], sign[:, 0:1], None, ALU.mult))
                        st.mark(dve.memset(T[:, :], 0))
                        st(dve.memset(bit[:, :], 1 << (BITS - 1)))
                        with loop(dve, BITS, st, 5) as i:
                            st(dve.tensor_tensor(cand[:, :], T[:, :], bit[:, :], ALU.bitwise_or))
                            dve.tensor_scalar(eq[:, :], v[:, :], cand[:, 0:1].bitcast(F32), 0.0, ALU.is_ge, ALU.add,
                                              accum_out=cnt[:, :]).then_inc(cnt_done, 1)
                            dve.wait_ge(sum_done, i + 2)
                            st(dve.tensor_scalar(take[:, :], ps[0:B, 0:1], kk[:, 0:1], None, ALU.is_ge))
                            st(dve.tensor_tensor(add[:, :], take[:, :], bit[:, :], ALU.mult))
                            st(dve.tensor_tensor(T[:, :], T[:, :], add[:, :], ALU.bitwise_or))
                            st(dve.tensor_scalar(bit[:, :], bit[:, :], 1, None, ALU.logical_shift_right))
                        st(dve.tensor_scalar(thr[:, :], T[:, 0:1].bitcast(F32), sign[:, 0:1], None, ALU.mult))
                        dve.tensor_scalar(eq[:, :], w[:, :], thr[:, 0:1], None, ALU.is_equal).then_inc(eq_done, 1)
                        st.mark(dve.tensor_scalar(gt[:, :], w[:, :], thr[:, 0:1], None, ALU.is_gt))
                        dve.tensor_scalar(v[:, :], w[:, :], thr[:, 0:1], 0.0, ALU.is_gt, ALU.add, accum_out=cnt[:, :]).then_inc(cnt_done, 1)
                        dve.wait_ge(sum_done, BITS + 2)
                        dve.wait_ge(rank_done, 1)
                        st(dve.tensor_scalar(kk[:, :], ps[0:B, 0:1], -1.0, float(TOPK), ALU.mult, ALU.add))
                        st(dve.tensor_copy(tot[:, :], ps[0:B, 128:128 + NB]))
                        st(dve.tensor_tensor_scan(cum[:, :], ones[0:B, 0:NB], tot[:, :], 0.0, ALU.mult, ALU.add))
                        st(dve.tensor_tensor(cum[:, :], cum[:, :], tot[:, :], ALU.subtract))
                        st(dve.tensor_tensor(cum[:, :], cum[:, :], ps[0:B, 64:64 + NB], ALU.add))
                        st(dve.scalar_tensor_tensor(cum[:, :], cum[:, :], kk[:, 0:1], eq[:, :], ALU.is_lt, ALU.mult))
                        st(dve.tensor_tensor(gt[:, :], gt[:, :], cum[:, :], ALU.add))
                        dve.tensor_tensor(selw[:, :], gt[:, :], w[:, :], ALU.mult)

        def route_experts(topi, topw):
            name = "route"
            n_e = 8
            cap = float(-(-N * 125 // (n_e * 100)))
            with ExitStack() as c:
                wr = sb(c, name + "_wr", [P, KF, n_e])
                br = sb(c, name + "_br", [1, n_e])
                colsum = sb(c, name + "_colsum", [B, D])
                mT = sb(c, name + "_mT", [P, KF])
                lg, ex, rw, sc, top = (sb(c, f"{name}_{x}", [1, n_e]) for x in ("lg", "ex", "rw", "sc", "top"))
                mx, sm = sb(c, name + "_mx", [1, 1]), sb(c, name + "_sm", [1, 1])
                ps, ps2, ps3 = pb(c, name + "_ps"), pb(c, name + "_ps2"), pb(c, name + "_ps3")
                loaded, own, col_done, mean_mm, mT_done, lg_mm, to_exp, exp_done, w_done, w_mm = (
                    sem(f"{name}_{x}") for x in ("loaded", "own", "col", "mean_mm", "mT", "lg_mm", "to_exp", "exp", "w", "w_mm"))
                with nc.Block() as block:
                    @block.sync
                    def _(sp):
                        sp.dma_start(wr[:, :, :], A["L1_ffn_Wr"]).then_inc(loaded, 16)
                        sp.dma_start(br[:, :], A["L1_ffn_br"]).then_inc(loaded, 16)

                    @block.tensor
                    def _(pe):
                        pe.wait_ge(col_done, 1)
                        for f in range(KF):
                            last = pe.matmul(ps[:, f:f + 1], colsum[:, f * P:(f + 1) * P], ones[0:B, 0:1], start=True, stop=True)
                        last.then_inc(mean_mm, 1)
                        pe.wait_ge(mT_done, 1)
                        pe.wait_ge(loaded, 32)
                        for f in range(KF):
                            last = pe.matmul(ps2[0:1, 0:n_e], mT[:, f:f + 1], wr[:, f, :], start=(f == 0), stop=(f == KF - 1))
                        last.then_inc(lg_mm, 1)
                        pe.wait_ge(w_done, 1)
                        pe.matmul(ps3[0:B, 0:2], ones[0:1, 0:B], lg[:, 0:2], start=True, stop=True).then_inc(w_mm, 1)

                    @block.scalar
                    def _(act):
                        for i in range(3):
                            act.wait_ge(to_exp, i + 1)
                            k = n_e if i < 2 else 2
                            act.activation(ex[:, 0:k], lg[:, 0:k], ACT.Exp).then_inc(exp_done, 1)

                    @block.vector
                    def _(dve):
                        st = Steps(dve, own)
                        dve.tensor_reduce(colsum[:, :], XN[0:B, :, :].rearrange("p b d -> p d b"), AX.X, ALU.add).then_inc(col_done, 1)
                        dve.wait_ge(mean_mm, 1)
                        dve.tensor_scalar(mT[:, :], ps[:, 0:KF], 1.0 / N, None, ALU.mult).then_inc(mT_done, 1)
                        dve.wait_ge(lg_mm, 1)
                        dve.wait_ge(loaded, 32)
                        st(dve.tensor_tensor(lg[:, :], ps2[0:1, 0:n_e], br[:, :], ALU.add))

                        def softmax(i, k, dst):
                            st(dve.tensor_reduce(mx[:, :], lg[:, 0:k], AX.X, ALU.max))
                            dve.tensor_scalar(lg[:, 0:k], lg[:, 0:k], mx[:, 0:1], None, ALU.subtract).then_inc(to_exp, 1)
                            dve.wait_ge(exp_done, i + 1)
                            st(dve.tensor_reduce(sm[:, :], ex[:, 0:k], AX.X, ALU.add))
                            st(dve.reciprocal(sm[:, :], sm[:, :]))
                            st(dve.tensor_scalar(dst, ex[:, 0:k], sm[:, 0:1], None, ALU.mult))

                        softmax(0, n_e, rw[:, :])
                        st(dve.tensor_scalar(sc[:, :], rw[:, :], float(N), cap, ALU.mult, ALU.max))
                        st(dve.reciprocal(sc[:, :], sc[:, :]))
                        st(dve.tensor_scalar(sc[:, :], sc[:, :], cap, None, ALU.mult))
                        st(dve.tensor_tensor(lg[:, :], rw[:, :], sc[:, :], ALU.mult))
                        softmax(1, n_e, rw[:, :])
                        st(dve.max(top[:, :], rw[:, :]))
                        st(dve.max_index(topi[:, :], top[:, :], rw[:, :]))
                        st(dve.tensor_copy(lg[:, 0:2], top[:, 0:2]))
                        softmax(2, 2, rw[:, 0:2])
                        dve.tensor_copy(lg[:, 0:2], rw[:, 0:2]).then_inc(w_done, 1)
                        dve.wait_ge(w_mm, 1)
                        dve.tensor_copy(topw[:, :], ps3[0:B, 0:2])

        for which, (k_, o_) in enumerate((("dst", "src"), ("src", "dst"))):
            sort_edges(which, A[k_], A[o_], A["edge_weight"])
            end_phase()

        X = sb(ctx, "X", [B, NB, D])
        XN = sb(ctx, "XN", [P, NB, D])
        U = sb(ctx, "U", [B, NB, D])
        s_x = sem("x_loaded")
        with nc.Block() as block:
            @block.sync
            def _(sp):
                for i in range(5):
                    n = NB // 5
                    sp.dma_start(X[:, i * n:(i + 1) * n, :], rows(A["x"])[:, i * n:(i + 1) * n, :]).then_inc(s_x, 16)
                sp.wait_ge(s_x, 80)
        end_phase()

        def blk(k, b):
            return bass.ds(k * CH + b, 1)

        def bias_and_self(dve, st, k, ys, b2, tmp):
            st(dve.tensor_tensor(tmp[:, :, :], ys[0], b2[0][:, :].unsqueeze(1).broadcast_to([B, CH, D]), ALU.add))
            u = U[:, bass.ds(k * CH, CH), :]
            return dve.tensor_tensor(u, u, tmp[:, :, :], ALU.add)

        def plain(dve, st, k, ys, b2, tmp):
            return dve.tensor_copy(U[:, bass.ds(k * CH, CH), :], ys[0])

        layer_norm("ln_a", X, XN)
        end_phase()
        with ExitStack() as c0:
            edge = {"kT": sb(c0, "edge_kT", [SMALL, NB, B]), "m": sb(c0, "edge_m", [B, NB]), "l": sb(c0, "edge_l", [B, NB]),
                    "wqk": A["L0_gnn_Wqk"], "bqk": A["L0_gnn_bqk"], "bk": A["L0_gnn_bk"]}
            with ExitStack() as c1:
                kvd = attention_sums(c1, "sums0", A["L0_mix_Wkv"], edge, table0, m=5)
                end_phase()
                attention_rows("att0", A["L0_mix_Wq"], kvd, True, m=3)
                end_phase()
            layer_norm("ln_b", U, U, affine=(A["L0_mix_ln1_g"], A["L0_mix_ln1_b"]))
            end_phase()
            mlp("mix0", [U], [(A["L0_mix_W1"], A["L0_mix_b1"], A["L0_mix_W2"], A["L0_mix_b2"].partition_broadcast(B))],
                D, ACT.Gelu, 1, bias_and_self, m=3)
            end_phase()
            layer_norm("ln_c", U, U, affine=(A["L0_mix_ln2_g"], A["L0_mix_ln2_b"]), into=X)
            end_phase()
            edge_softmax(edge)
            end_phase()
            own = sem("gat_end")
            with nc.Block() as block:
                @block.vector
                def _(dve):
                    st = Steps(dve, own)
                    st(dve.reciprocal(edge["l"][:, :], edge["l"][:, :]))
                    with loop(dve, NB, st, 1) as b:
                        r = bass.ds(b, 1)
                        st.mark(dve.scalar_tensor_tensor(one(X[:, r, :]), one(U[:, r, :]), edge["l"][:, r], one(X[:, r, :]), ALU.mult, ALU.add))
            end_phase()

        layer_norm("ln_d", X, XN)
        end_phase()
        with ExitStack() as c0:
            selw = sb(c0, "selw", [B, NB])
            route_rows(selw)
            end_phase()

            def weighted(dve, st, k, ys, b2, tmp):
                st(dve.tensor_tensor(tmp[:, :, :], ys[0], b2[0][:, :].unsqueeze(1).broadcast_to([B, CH, D]), ALU.add))
                for b in range(CH):
                    st(dve.scalar_tensor_tensor(tmp[:, b, :], tmp[:, b, :], selw[:, blk(k, b)], one(XN[0:B, blk(k, b), :]), ALU.mult, ALU.add))
                x = X[:, bass.ds(k * CH, CH), :]
                return dve.tensor_tensor(x, x, tmp[:, :, :], ALU.add)

            mlp("ffn0", [XN], [(A["L0_ffn_w1"], A["L0_ffn_b1"], A["L0_ffn_w2"], A["L0_ffn_b2"].partition_broadcast(B))],
                4 * D, ACT.Gelu_apprx_tanh, 1 + CH, weighted, m=7)
            end_phase()

        layer_norm("ln_e", X, XN)
        end_phase()
        with ExitStack() as c1:
            kvd = attention_sums(c1, "sums1", A["L1_mix_Wkv"], None, table1, m=5)
            end_phase()
            attention_rows("att1", A["L1_mix_Wq"], kvd, False, m=3)
            end_phase()
        linear("merge", U, A["L1_mix_Wm"], None, 0, lambda dve, st, k, y, b: dve.tensor_copy(U[:, bass.ds(k * CH, CH), :], y),
               m=7, turns=1)
        end_phase()
        layer_norm("ln_f", U, U, affine=(A["L1_mix_g1"], A["L1_mix_b1"]))
        end_phase()
        mlp("mix1", [XN, U], [(A["L1_mix_W1"], None, A["L1_mix_W2"], None)], 2 * D, ACT.Relu, 0, plain, m=5)
        end_phase()
        layer_norm("ln_g", U, U, affine=(A["L1_mix_g2"], A["L1_mix_b2"]), into=X, plus=XN)
        end_phase()
        assert moved[0] == EC
        edge_sums()
        end_phase()

        def into_x(dve, st, k, y, b2):
            x = X[:, bass.ds(k * CH, CH), :]
            st(dve.tensor_tensor(x, x, y, ALU.add))
            return dve.tensor_tensor(x, x, b2[:, :].unsqueeze(1).broadcast_to([B, CH, D]), ALU.add)

        linear("gcn_w", U, A["L1_gnn_W"], A["L1_gnn_b"], 1, into_x)
        end_phase()

        layer_norm("ln_h", X, XN)
        end_phase()
        topi = sb(ctx, "topi", [1, 8], mybir.dt.uint32)
        topw = sb(ctx, "topw", [B, 2])
        route_experts(topi, topw)
        end_phase()
        bb = sb(ctx, "expert_bias", [B, D])
        held = {}

        def expert(name, shape):
            def load(sp, e):
                if e not in held:
                    held[e] = sp.value_load(topi[0:1, e:e + 1], min_val=0, max_val=7)
                return shape(A[name][bass.ds(held[e], 1)])
            return load

        def both_biases(dve, st, b2):
            st(dve.tensor_scalar(bb[:, :], b2[0][:, :], topw[:, 0:1], None, ALU.mult))
            st(dve.scalar_tensor_tensor(bb[:, :], b2[1][:, :], topw[:, 1:2], bb[:, :], ALU.mult, ALU.add))

        def mixed(dve, st, k, ys, b2, tmp):
            xn, u = XN[0:B, bass.ds(k * CH, CH), :], U[:, bass.ds(k * CH, CH), :]
            st(dve.scalar_tensor_tensor(tmp[:, :, :], ys[0], topw[:, 0:1], xn, ALU.mult, ALU.add))
            st(dve.scalar_tensor_tensor(tmp[:, :, :], ys[1], topw[:, 1:2], tmp[:, :, :], ALU.mult, ALU.add))
            return dve.tensor_tensor(u, tmp[:, :, :], bb[:, :].unsqueeze(1).broadcast_to([B, CH, D]), ALU.add)

        spec = (expert("L1_ffn_W1", lambda a: a.rearrange("e p k f -> (e p) k f")), expert("L1_ffn_b1", lambda a: a.rearrange("e p f -> (e p) f")),
                expert("L1_ffn_W2", lambda a: a.rearrange("e p f d -> (e p) f d")), expert("L1_ffn_b2", lambda a: a.rearrange("e d -> (e d)").partition_broadcast(B)))
        mlp("ffn1", [XN], [spec, spec], 2 * D, ACT.Gelu, 2, mixed, setup=both_biases)
        end_phase()
        layer_norm("ln_i", U, U, affine=(A["L1_ffn_gamma"], A["L1_ffn_beta"]), into=X)
        end_phase()

        s_out = sem("out_written")
        with nc.Block() as block:
            @block.sync
            def _(sp):
                for i in range(5):
                    n = NB // 5
                    sp.dma_start(rows(out)[:, i * n:(i + 1) * n, :], X[:, i * n:(i + 1) * n, :]).then_inc(s_out, 16)
                sp.wait_ge(s_out, 80)


def lay_out(inputs):
    a = {k: np.asarray(v) for k, v in inputs.items()}

    def halves(w):
        return np.ascontiguousarray(w.reshape(-1, P, w.shape[-1]).transpose(1, 0, 2))

    def edges(v, fill):
        out = np.full((P * EC,), fill, v.dtype)
        out[:E] = v
        return out.reshape(P, EC)

    o = {"x": a["x"], "src": None, "dst": None}
    pad_key = NB * B + B // 2
    o["src"], o["dst"] = edges(a["src"], pad_key), edges(a["dst"], pad_key)
    o["edge_weight"] = edges(a["edge_weight"], 0)
    wq, wk = a["L0_gnn_Wq"], a["L0_gnn_Wk"]
    o["L0_gnn_Wqk"] = halves(np.concatenate([wq, wk], 1))
    o["L0_gnn_bqk"] = np.concatenate([a["L0_gnn_bq"], a["L0_gnn_bk"]])[None]
    o["L0_gnn_bk"] = a["L0_gnn_bk"][:, None]
    w = a["L0_mix_Wqkv"].T
    o["L0_mix_Wq"], o["L0_mix_Wkv"] = halves(w[:, :D]), halves(w[:, D:])
    o["L0_mix_W1"], o["L0_mix_W2"] = halves(a["L0_mix_W1"].T), halves(a["L0_mix_W2"].T)
    o["L0_mix_b1"] = np.ascontiguousarray(a["L0_mix_b1"].reshape(-1, P).T)
    for n in ("L0_mix_b2", "L0_mix_ln1_g", "L0_mix_ln1_b", "L0_mix_ln2_g", "L0_mix_ln2_b", "L0_ffn_b2", "L0_ffn_br",
              "L1_gnn_b", "L1_mix_g1", "L1_mix_b1", "L1_mix_g2", "L1_mix_b2", "L1_ffn_gamma", "L1_ffn_beta", "L1_ffn_b2"):
        o[n] = a[n]
    o["L0_ffn_wr"] = a["L0_ffn_wr"].reshape(-1)
    o["L0_ffn_w1"], o["L0_ffn_w2"] = halves(a["L0_ffn_w1"]), halves(a["L0_ffn_w2"])
    o["L0_ffn_b1"] = np.ascontiguousarray(a["L0_ffn_b1"].reshape(-1, P).T)
    o["L1_gnn_W"] = halves(a["L1_gnn_W"])
    o["L1_mix_Wq"] = halves(a["L1_mix_Wq"])
    o["L1_mix_Wkv"] = halves(np.concatenate([a["L1_mix_Wk"], a["L1_mix_Wv"]], 1))
    for n in ("L1_mix_Wm", "L1_mix_W1", "L1_mix_W2", "L1_ffn_Wr"):
        o[n] = halves(a[n])
    o["L1_ffn_br"] = a["L1_ffn_br"][None]
    o["L1_ffn_W1"] = np.stack([halves(x) for x in a["L1_ffn_W1"]])
    o["L1_ffn_W2"] = np.stack([halves(x) for x in a["L1_ffn_W2"]])
    o["L1_ffn_b1"] = np.ascontiguousarray(a["L1_ffn_b1"].reshape(8, -1, P).transpose(0, 2, 1))
    return o


def kernel(**inputs):
    import concourse.bacc as bacc
    from concourse.bass_utils import run_bass_kernel_spmd

    arrays = lay_out(inputs)
    nc = bacc.Bacc("TRN2", target_bir_lowering=False, num_devices=1)
    A = {n: nc.dram_tensor("in_" + n, v.shape, mybir.dt.from_np(v.dtype), kind="ExternalInput").ap() for n, v in arrays.items()}
    out = nc.dram_tensor("out_x", (N, D), F32, kind="ExternalOutput").ap()
    gps_kernel(nc, A, out)
    r = run_bass_kernel_spmd(nc, [{"in_" + n: v for n, v in arrays.items()}], core_ids=[0])
    return r.results[0]["out_x"]
```

```python
import concourse.bass as bass
from concourse import mybir
from contextlib import ExitStack
import numpy as np

F32 = mybir.dt.float32
I32 = mybir.dt.int32
BF16 = mybir.dt.bfloat16
U16 = mybir.dt.uint16
ALU = mybir.AluOpType
ACT = mybir.ActivationFunctionType
AX = mybir.AxisListType

P = 128
N, D, E = 6250, 256, 200000
KF = D // P
B = 125
NB = N // B
CH = 2
NC = NB // CH
TOK = CH * B
SUB = 4
G = P * SUB
NG = -(-E // G)
EP = NG * G
EC = EP // P
NS = NG + NB - 1
RING = 8
LAG = 4
AHEAD = 6
RW = 3
SMALL = 25
HEADS, HD = 8, 32
HH = P // HD
LN_EPS, ATT_EPS = 1e-5, 1e-6
TOPK = N // 2 - 1
MOVE = 7
SLOT = 17
BIG = 1e30
RS = 3
R, R_DVE = 5, 3


class Steps:

    def __init__(self, eng, sem):
        self.eng, self.sem, self.base, self.n = eng, sem, 0, 0

    def __call__(self, ins):
        ins.then_inc(self.sem, 1)
        self.n += 1
        self.eng.wait_ge(self.sem, self.base + self.n)

    def mark(self, ins):
        ins.then_inc(self.sem, 1)
        self.n += 1

    def all(self):
        self.eng.wait_ge(self.sem, self.base + self.n)


def settle(pool, cell, settled, before):
    pool.wait_ge(settled, before)
    pool.tensor_tensor(cell, cell, cell, ALU.add).then_inc(settled, 1)


class loop:

    def __init__(self, eng, times, steps=None, per=0):
        self.eng, self.times, self.steps, self.per = eng, times, steps, per

    def __enter__(self):
        self.f = self.eng.Fori(0, self.times)
        t = self.f.__enter__()
        if self.steps:
            s = self.steps
            self.before = s.base + s.n
            s.base, s.n = self.before + t * self.per, 0
        return t

    def __exit__(self, *a):
        if self.steps and a[0] is None:
            s = self.steps
            assert s.n == self.per, (s.n, self.per)
            s.base, s.n = self.before + self.times * self.per, 0
        return self.f.__exit__(*a)


def gps_kernel(nc, A, out):
    ctx = ExitStack()
    phase_sems = []

    def sem(name):
        held = nc.semaphore(name)
        phase_sems.append((held, held.__enter__()))
        return phase_sems[-1][1]

    def pool_dma_sem(name):
        return ctx.enter_context(nc.semaphore(name))

    def end_phase():
        with nc.Block() as block:
            @block.sync
            def _(sp):
                for _, s in phase_sems:
                    sp.sem_clear(s)
        while phase_sems:
            phase_sems.pop()[0].__exit__(None, None, None)

    def sb(c, name, shape, dt=F32):
        return c.enter_context(nc.sbuf_tensor(name, shape, dt))

    def pb(c, name, shape=(P, 512), dt=F32):
        return c.enter_context(nc.psum_tensor(name, list(shape), dt))

    def one(ap):
        return ap.rearrange("p a n -> p (a n)")

    def rows(dram):
        return dram.rearrange("(b p) d -> p b d", p=B)

    table0 = nc.dram_tensor("table0", [N, D + SMALL], F32).ap()
    table1 = nc.dram_tensor("table1", [N, D], F32).ap()
    spill_rec = [nc.dram_tensor(f"spill_rec{i}", [P, EC, RW], F32).ap() for i in range(2)]
    spill_pos = [nc.dram_tensor(f"spill_pos{i}", [P, EC], I32).ap() for i in range(2)]
    rec_d = [nc.dram_tensor(f"records{i}", [EP, RW], F32).ap() for i in range(2)]

    with ctx:
        ident = sb(ctx, "ident", [P, P])
        ones = sb(ctx, "ones", [P, P])
        lower = sb(ctx, "lower", [P, P])
        iota_n = sb(ctx, "iota_n", [P, B])
        iota_p = sb(ctx, "iota_p", [P, 1])
        eps = sb(ctx, "eps", [P, 1])
        ident16 = sb(ctx, "ident16", [P, P], BF16)
        cell = sb(ctx, "cell", [1, 1], I32)
        slot_pos = sb(ctx, "slot_pos", [P, 2, SLOT], I32)
        slot_rec = sb(ctx, "slot_rec", [P, 2, SLOT, RW])
        sent = [pool_dma_sem(f"sent{h}") for h in range(2)]
        sent_unsorted = [pool_dma_sem(f"sent_unsorted{h}") for h in range(2)]
        step_blk = [sb(ctx, f"step_blk{i}", [1, NS], I32) for i in range(2)]
        step_grp = [sb(ctx, f"step_grp{i}", [1, NS], I32) for i in range(2)]
        first_step = [sb(ctx, f"first_step{i}", [1, NG + 1], I32) for i in range(2)]
        step_node = [sb(ctx, f"step_node{i}", [P, NS]) for i in range(2)]
        X = sb(ctx, "X", [B, NB, D])
        room = sb(ctx, "room", [P, NB, D])
        U = room[0:B, :, :]
        words = room[:, :, :].rearrange("p b d -> p (b d)")
        taken = [2 * NB * SMALL]

        def piece(n, dt=F32):
            w = n // 2 if dt in (BF16, U16) else n
            taken[0] += w
            part = words[:, taken[0] - w:taken[0]]
            return part if dt == F32 else part.bitcast(dt)

        pos = piece(EC)
        posi = piece(EC, I32)
        run = piece(2 * EC).rearrange("p (a n) -> p a n", a=2)
        same = piece(2 * EC, U16).rearrange("p (a n) -> p a n", a=2)
        blkf = piece(EC, BF16)
        one_ = piece(EC, BF16)
        cls, base, pace = piece(NB + 1), piece(NB + 1), piece(2)

        class Places:

            def __init__(self, dve, own):
                self.dve, self.st = dve, Steps(dve, own)

            def blocks(self, b, n):
                dve, st, at = self.dve, self.st, self.st.base + self.st.n
                for i in range(n):
                    st.mark(dve.tensor_scalar(same[:, i, :], blkf[:, :], cls[:, bass.ds(b + i, 1)], None, ALU.is_equal))
                for i in range(n):
                    dve.wait_ge(st.sem, at + 1 + i)
                    st.mark(dve.tensor_tensor_scan(run[:, i, :], one_[:, :], same[:, i, :], base[:, bass.ds(b + i, 1)],
                                                   ALU.mult, ALU.add))
                for i in range(n):
                    dve.wait_ge(st.sem, at + (2 * n + 2 * i if i else n + 1))
                    st.mark(dve.tensor_copy(pace[:, i:i + 1], ones[:, 0:1]))
                    st.mark(dve.copy_predicated(pos[:, :], same[:, i, :], run[:, i, :]))
                st.all()

            def finish(self, done):
                self.blocks(2 * NC, 1)
                self.dve.tensor_scalar(posi[:, :], pos[:, :], -1.0, None, ALU.add).then_inc(done, 1)

        s_c = sem("constants_step")
        with nc.Block() as block:
            @block.gpsimd
            def _(pool):
                st = Steps(pool, s_c)
                st(pool.memset(ident[:, :], 0.0))
                st(pool.affine_select(out=ident[:, :], in_=ident[:, :], compare_op=ALU.not_equal, fill=1.0,
                                      base=0, pattern=[[-1, P]], channel_multiplier=1))
                st(pool.memset(lower[:, :], 1.0))
                st(pool.affine_select(out=lower[:, :], in_=lower[:, :], compare_op=ALU.is_gt, fill=0.0,
                                      base=0, pattern=[[1, P]], channel_multiplier=-1))
                pool.tensor_copy(ident16[:, :], ident[:, :])
                pool.memset(ones[:, :], 1.0)
                pool.memset(eps[:, :], LN_EPS)
                pool.memset(cell[:, :], 0)
                pool.iota(iota_n[:, :], pattern=[[1, B]], base=0, channel_multiplier=0,
                          allow_small_or_imprecise_dtypes=True)
                st(pool.iota(iota_p[:, :], pattern=[[0, 1]], base=0, channel_multiplier=1,
                             allow_small_or_imprecise_dtypes=True))
        end_phase()

        def sort_edges(which, key, other, val):
            t_ = f"sort{which}_"
            with ExitStack() as c:
                keyi = sb(c, t_ + "key", [P, EC], I32)
                othi = sb(c, t_ + "other", [P, EC], I32)
                rec = sb(c, t_ + "rec", [P, EC, RW])
                blki = sb(c, t_ + "blki", [P, EC], I32)
                mask = sb(c, t_ + "mask", [P, RS, EC], U16)
                scan = sb(c, t_ + "scan", [P, EC])
                cnt = sb(c, t_ + "cnt", [P, NB + 1])
                tot = sb(c, t_ + "tot", [P, NB + 1])
                cum = sb(c, t_ + "cum", [P, NB + 1])
                tcol = sb(c, t_ + "tcol", [NB, 1])
                bnd = sb(c, t_ + "bnd", [NB, 1])
                bndi = sb(c, t_ + "bndi", [NB, 1], I32)
                incl = sb(c, t_ + "incl", [P, P])
                after_ = sb(c, t_ + "after", [P, 2], I32)
                falls = sb(c, t_ + "falls", [P, 2])
                fallen = sb(c, t_ + "fallen", [1, 1], I32)
                ge = sb(c, t_ + "ge", [NB, NS])
                ended = sb(c, t_ + "ended", [NB, NG + 1])
                ps3 = pb(c, t_ + "ps3")
                stepf = sb(c, t_ + "stepf", [P, NS])
                iota_s = sb(c, t_ + "iota_s", [P, NS])
                ps = pb(c, t_ + "ps")
                ps2 = pb(c, t_ + "ps2")
                loaded, own, count_done, sums_done = (sem(t_ + x) for x in ("loaded", "own", "counted", "summed"))
                tcol_done, cum_done, bnd_done, step_done = (sem(t_ + x) for x in ("tcol", "cumsum", "bounds", "steps"))
                pool_c, pos_done, rec_done, spilled, order_done, order_mm, order_set = (
                    sem(t_ + x) for x in ("iota", "positions", "records", "spilled", "order", "order_mm", "order_set"))

                with nc.Block() as block:
                    @block.sync
                    def _(sp):
                        sp.dma_start(keyi[:, :], key).then_inc(loaded, 16)
                        sp.dma_start(othi[:, :], other).then_inc(loaded, 16)
                        sp.dma_start(scan[:, :], val).then_inc(loaded, 16)
                        if which == 0:
                            sp.dma_start(after_[0:P - 1, :], key[1:P, 0:2]).then_inc(loaded, 16)
                        sp.wait_ge(rec_done, 1)
                        sp.dma_start(spill_rec[which], rec[:, :, :]).then_inc(spilled, 16)
                        if which == 0:
                            sp.dma_start(rec_d[0].rearrange("(p t) w -> p t w", p=P), rec[:, :, :]).then_inc(spilled, 16)
                            sp.wait_ge(spilled, 32)
                        else:
                            sp.dma_start(X[:, :, :], rows(A["x"])).then_inc(spilled, 16)
                            sp.wait_ge(spilled, 32)

                    @block.gpsimd
                    def _(pool):
                        pool.iota(cls[:, :], pattern=[[1, NB + 1]], base=0, channel_multiplier=0,
                                  allow_small_or_imprecise_dtypes=True).then_inc(pool_c, 1)
                        pool.iota(iota_s[:, :], pattern=[[1, NS]], base=0, channel_multiplier=0,
                                  allow_small_or_imprecise_dtypes=True).then_inc(pool_c, 1)
                        pool.tensor_tensor(incl[:, :], lower[:, :], ident[:, :], ALU.add).then_inc(pool_c, 1)
                        if which == 0:
                            pool.memset(falls[:, :], 0.0).then_inc(pool_c, 1)

                    @block.vector
                    def _(dve):
                        st = Steps(dve, own)
                        dve.memset(one_[:, :], 1.0)
                        st(dve.memset(pos[:, :], 1.0))
                        dve.wait_ge(pool_c, 4 if which == 0 else 3)
                        dve.wait_ge(loaded, 64 if which == 0 else 48)
                        st(dve.tensor_scalar(blki[:, :], keyi[:, :], -float(B // 2), 1.0 / B, ALU.add, ALU.mult))
                        st.mark(dve.tensor_copy(blkf[:, :], blki[:, :]))
                        st.mark(dve.tensor_copy(rec[:, :, 0], keyi[:, :]))
                        st.mark(dve.tensor_scalar(rec[:, :, 1].bitcast(I32), othi[:, :], N - 1, None, ALU.min))
                        dve.tensor_copy(rec[:, :, 2], scan[:, :]).then_inc(rec_done, 1)
                        dve.wait_ge(rec_done, 1)
                        with loop(dve, (NB + 1) // RS, st, RS) as t:
                            for i in range(RS):
                                b = bass.ds(t * RS + i, 1)
                                st.mark(dve.tensor_scalar(mask[:, i, :], blkf[:, :], cls[:, b], 0.0,
                                                          ALU.is_equal, ALU.add, accum_out=cnt[:, b]))
                            st.all()
                        dve.tensor_copy(tot[:, :], cnt[:, :]).then_inc(count_done, 1)
                        dve.wait_ge(sums_done, 1)
                        st(dve.tensor_copy(tot[:, :], ps[:, 64:64 + NB + 1]))
                        st(dve.tensor_tensor_scan(cum[:, :], ones[:, 0:NB + 1], tot[:, :], 0.0, ALU.mult, ALU.add))
                        st(dve.tensor_tensor(cum[:, :], cum[:, :], tot[:, :], ALU.subtract))
                        st(dve.tensor_tensor(base[:, :], cum[:, :], ps[:, 0:NB + 1], ALU.add))
                        dve.tensor_copy(tcol[:, :], ps[0:NB, 128:129]).then_inc(tcol_done, 1)
                        dve.wait_ge(cum_done, 1)
                        st(dve.tensor_scalar(bndi[:, :], ps2[0:NB, 0:1], 1.0 / G, 0.5 - 0.5 / G, ALU.mult, ALU.add))
                        st(dve.tensor_copy(bnd[:, :], bndi[:, :]))
                        st(dve.tensor_scalar(bnd[:, :], bnd[:, :], 1.0, None, ALU.max))
                        st.mark(dve.tensor_scalar(ended[:, :], iota_s[0:NB, 0:NG + 1], bnd[:, 0:1], None, ALU.is_ge))
                        st(dve.tensor_scalar(bnd[:, :], bnd[:, :], iota_p[0:NB, 0:1], None, ALU.add))
                        dve.tensor_scalar(ge[:, :], iota_s[0:NB, :], bnd[:, 0:1], None, ALU.is_ge).then_inc(bnd_done, 1)
                        dve.wait_ge(step_done, 1)
                        st.mark(dve.tensor_tensor(first_step[which][:, :], iota_s[0:1, 0:NG + 1], ps3[0:1, 0:NG + 1], ALU.add))
                        st(dve.tensor_scalar(stepf[:, :], ps2[:, 0:NS], float(NB - 1), None, ALU.min))
                        st.mark(dve.tensor_scalar(step_node[which][:, :], stepf[:, :], float(B), None, ALU.mult))
                        st.mark(dve.tensor_copy(step_blk[which][:, :], stepf[0:1, :]))
                        st(dve.tensor_tensor(iota_s[:, :], iota_s[:, :], stepf[:, :], ALU.subtract))
                        st(dve.tensor_scalar(iota_s[:, :], iota_s[:, :], float(NG - 1), None, ALU.min))
                        st(dve.tensor_copy(step_grp[which][:, :], iota_s[0:1, :]))
                        if which == 0:
                            st(dve.tensor_tensor(scan[:, 0:EC - 1], keyi[:, 1:EC], keyi[:, 0:EC - 1], ALU.is_lt))
                            st(dve.tensor_reduce(falls[:, 0:1], scan[:, 0:EC - 1], AX.X, ALU.add))
                            st(dve.tensor_tensor(falls[0:P - 1, 1:2], after_[0:P - 1, 0:1], keyi[0:P - 1, EC - 1:EC], ALU.is_lt))
                            dve.tensor_tensor(falls[:, 0:1], falls[:, 0:1], falls[:, 1:2], ALU.add).then_inc(order_done, 1)
                            dve.wait_ge(order_mm, 1)
                            dve.tensor_copy(fallen[:, :], ps[0:1, 256:257]).then_inc(order_set, 1)
                            dve.wait_ge(order_set, 1)
                            with dve.If(dve.value_load(fallen[0:1, 0:1], min_val=0, max_val=EP) > 0):
                                places = Places(dve, own)
                                places.st = st
                                with loop(dve, NC, st, 8) as t:
                                    places.blocks(t * 2, 2)
                                places.finish(pos_done)

                    @block.tensor
                    def _(pe):
                        pe.wait_ge(count_done, 1)
                        pe.matmul(ps[:, 0:NB + 1], lower[:, :], tot[:, :], start=True, stop=True)
                        pe.matmul(ps[:, 64:64 + NB + 1], ones[:, :], tot[:, :], start=True, stop=True)
                        pe.matmul(ps[0:NB, 128:129], tot[:, 0:NB], ones[:, 0:1], start=True, stop=True).then_inc(sums_done, 1)
                        pe.wait_ge(tcol_done, 1)
                        pe.matmul(ps2[0:NB, 0:1], incl[0:NB, 0:NB], tcol[:, :], start=True, stop=True).then_inc(cum_done, 1)
                        pe.wait_ge(bnd_done, 1)
                        pe.matmul(ps3[0:1, 0:NG + 1], ones[0:NB - 1, 0:1], ended[0:NB - 1, :], start=True, stop=True)
                        pe.matmul(ps2[:, 0:NS], ones[0:NB - 1, :], ge[0:NB - 1, :], start=True, stop=True).then_inc(step_done, 1)
                        if which == 0:
                            pe.wait_ge(order_done, 1)
                            pe.matmul(ps[0:1, 256:257], falls[:, 0:1], ones[:, 0:1], start=True, stop=True).then_inc(order_mm, 1)

                if which == 0:
                    turns = EC // (2 * SLOT)
                    mv = Mover("unsorted", 0, 0, SLOT, turns, sent_unsorted, 0)
                    stored = sem(t_ + "pos_stored")
                    with nc.Block() as block:
                        @block.sync
                        def _(sp):
                            with sp.If(sp.value_load(fallen[0:1, 0:1], min_val=0, max_val=EP) > 0):
                                sp.wait_ge(pos_done, 1)
                                sp.dma_start(spill_pos[0], posi[:, :]).then_inc(stored, 16)
                                sp.wait_ge(stored, 16)
                                mv.sp(sp)

                        @block.gpsimd
                        def _(pool):
                            with pool.If(pool.value_load(fallen[0:1, 0:1], min_val=0, max_val=EP) > 0):
                                mv.pool(pool)

        class Mover:

            def __init__(self, name, which, at, m, turns, sent, before):
                self.which, self.at, self.m, self.turns = which, at, m, turns
                self.sent, self.before = sent, before
                if turns:
                    self.filled = [sem(f"{name}_filled{h}") for h in range(2)]
                    self.settled = sem(name + "_settled")

            def sp(self, sp):
                m = self.m
                if self.turns:
                    with loop(sp, self.turns) as k:
                        for h in range(2):
                            cols = bass.ds(k * (2 * m) + (self.at + h * m), m)
                            sp.wait_ge(self.sent[h], k * (16 * m) + self.before)
                            sp.dma_start(slot_rec[:, h, 0:m, :], spill_rec[self.which][:, cols, :]).then_inc(self.filled[h], 16)
                            sp.dma_start(slot_pos[:, h, 0:m], spill_pos[self.which][:, cols]).then_inc(self.filled[h], 16)

            def pool(self, pool):
                m = self.m
                if self.turns:
                    with loop(pool, self.turns) as k:
                        for h in range(2):
                            pool.wait_ge(self.filled[h], k * 32 + 32)
                            settle(pool, cell[0:1, 0:1], self.settled, k * 2 + h)
                            for j in range(m):
                                pool.indirect_dma_start(
                                    out=rec_d[self.which],
                                    out_offset=bass.IndirectOffsetOnAxis(ap=slot_pos[:, h, j:j + 1], axis=0),
                                    in_=slot_rec[:, h, j, :], in_offset=None).then_inc(self.sent[h], 16)
                    for h in range(2):
                        pool.wait_ge(self.sent[h], self.before + 16 * m * self.turns)

        moved = [0]

        def mover(name, turns):
            m = min(MOVE, (EC - moved[0]) // 2)
            mv = Mover(name, 1, moved[0], m, turns, sent, 8 * moved[0])
            moved[0] += 2 * m * turns
            return mv

        def layer_norm(name, src, dst, affine=None, into=None, plus=None, turns=0):
            with ExitStack() as c:
                stats = sb(c, name + "_stats", [B, NB, 6])
                mean = sb(c, name + "_mean", [B, NB])
                half = sb(c, name + "_half", [B, NB])
                var = sb(c, name + "_var", [B, NB])
                rstd = sb(c, name + "_rstd", [B, NB])
                gain = sb(c, name + "_gain", [B, D])
                offset = sb(c, name + "_offset", [B, D])
                shift = sb(c, name + "_shift", [B, NB])
                own, var_done, sd_done, loaded, plus_done, shift_done, scaled = (
                    sem(name + x) for x in ("_own", "_var", "_sd", "_loaded", "_plus", "_shift", "_scaled"))
                mv = mover(name, turns)
                with nc.Block() as block:
                    @block.sync
                    def _(sp):
                        if affine:
                            sp.dma_start(gain[:, :], affine[0].partition_broadcast(B)).then_inc(loaded, 16)
                            sp.dma_start(offset[:, :], affine[1].partition_broadcast(B)).then_inc(loaded, 16)
                        mv.sp(sp)

                    @block.gpsimd
                    def _(pool):
                        if plus is not None:
                            with loop(pool, NB // R) as t:
                                for i in range(R):
                                    r = bass.ds(t * R + i, 1)
                                    pool.tensor_tensor(one(into[:, r, :]), one(into[:, r, :]), one(plus[0:B, r, :]), ALU.add).then_inc(plus_done, 1)
                            pool.wait_ge(plus_done, NB)
                        mv.pool(pool)
                        if into is not None:
                            with loop(pool, NB // R) as t:
                                pool.wait_ge(scaled, t * R + R)
                                for i in range(R):
                                    r = bass.ds(t * R + i, 1)
                                    pool.tensor_tensor(one(into[:, r, :]), one(into[:, r, :]), one(src[0:B, r, :]), ALU.add)

                    @block.scalar
                    def _(act):
                        act.wait_ge(var_done, 1)
                        act.activation(rstd[:, :], var[:, :], ACT.Sqrt, bias=eps[0:B, 0:1]).then_inc(sd_done, 1)
                        if not affine:
                            act.wait_ge(shift_done, 1)
                            with loop(act, NB // R) as t:
                                for i in range(R_DVE, R):
                                    r = bass.ds(t * R + i, 1)
                                    act.activation(one(dst[0:B, r, :]), one(src[0:B, r, :]), ACT.Identity, bias=shift[:, r], scale=rstd[:, r])

                    @block.vector
                    def _(dve):
                        st = Steps(dve, own)
                        with loop(dve, NB // R, st, R) as t:
                            for i in range(R):
                                r = bass.ds(t * R + i, 1)
                                st.mark(dve.bn_stats(one(stats[:, r, :]), one(src[0:B, r, :])))
                        st.all()
                        me, mo, qe, qo = (stats[:, :, i] for i in (1, 4, 2, 5))
                        st.mark(dve.tensor_tensor(mean[:, :], me, mo, ALU.add))
                        st.mark(dve.tensor_tensor(half[:, :], me, mo, ALU.subtract))
                        st(dve.tensor_tensor(var[:, :], qe, qo, ALU.add))
                        st.mark(dve.tensor_scalar(mean[:, :], mean[:, :], 0.5, None, ALU.mult))
                        st(dve.scalar_tensor_tensor(half[:, :], half[:, :], 0.25, half[:, :], ALU.mult, ALU.mult))
                        dve.scalar_tensor_tensor(var[:, :], var[:, :], 1.0 / D, half[:, :], ALU.mult, ALU.add).then_inc(var_done, 1)
                        dve.wait_ge(sd_done, 1)
                        st(dve.reciprocal(rstd[:, :], rstd[:, :]))
                        if affine:
                            dve.wait_ge(loaded, 32)
                            with loop(dve, NB // R, st, R) as t:
                                for i in range(R):
                                    r = bass.ds(t * R + i, 1)
                                    s = one(src[0:B, r, :])
                                    st.mark(dve.scalar_tensor_tensor(s, s, mean[:, r], gain[:, :], ALU.subtract, ALU.mult))
                                st.all()
                                for i in range(R):
                                    r = bass.ds(t * R + i, 1)
                                    s = one(src[0:B, r, :])
                                    dve.scalar_tensor_tensor(s, s, rstd[:, r], offset[:, :], ALU.mult, ALU.add).then_inc(scaled, 1)
                        else:
                            dve.scalar_tensor_tensor(shift[:, :], mean[:, :], -1.0, rstd[:, :], ALU.mult, ALU.mult).then_inc(shift_done, 1)
                            with loop(dve, NB // R) as t:
                                for i in range(R_DVE):
                                    r = bass.ds(t * R + i, 1)
                                    dve.tensor_scalar(one(dst[0:B, r, :]), one(src[0:B, r, :]), mean[:, r], rstd[:, r],
                                                      ALU.subtract, ALU.mult)

        def transposed(c, name, srcs):
            n_src = len(srcs)
            stage = sb(c, name + "_stage", [B, n_src, CH, D])
            xT = sb(c, name + "_xT", [P, n_src * KF, TOK])
            psT = [pb(c, f"{name}_psT{i}") for i in range(n_src)]
            staged, turned, xT_done = (sem(name + x) for x in ("_staged", "_turned", "_xT"))

            def stage_rows(act, k):
                for i, src in enumerate(srcs):
                    act.wait_ge(turned, k)
                    act.activation(stage[:, i, :, :], src[0:B, bass.ds(k * CH, CH), :], ACT.Copy).then_inc(staged, 1)

            def turn(pe, k):
                pe.wait_ge(staged, k * n_src + n_src)
                for i in range(n_src):
                    for f in range(KF):
                        for b in range(CH):
                            at = (f * CH + b) * B
                            last = pe.transpose(psT[i][:, at:at + B], stage[:, i, b, f * P:(f + 1) * P], ident[0:B, 0:B])
                last.then_inc(turned, 1)

            def pe_chunks(pe, first, second):
                def chunk(k, end):
                    pe.wait_ge(xT_done, k * n_src + n_src)
                    first(k)
                    if not end:
                        turn(pe, k + 1)
                    second(k)

                turn(pe, 0)
                with loop(pe, NC - 1) as k:
                    chunk(k, False)
                chunk(NC - 1, True)

            def act_chunks(act, rest):
                def chunk(k, end):
                    act.wait_ge(turned, k + 1)
                    for i in range(n_src):
                        act.activation(xT[:, i * KF:(i + 1) * KF, :].rearrange("p f t -> p (f t)"),
                                       psT[i][:, 0:KF * TOK], ACT.Copy).then_inc(xT_done, 1)
                    if not end:
                        stage_rows(act, k + 1)
                    rest(k)

                stage_rows(act, 0)
                with loop(act, NC - 1) as k:
                    chunk(k, False)
                chunk(NC - 1, True)

            return xT, pe_chunks, act_chunks

        def mlp(name, srcs, experts, width, func, per, final, setup=None, turns=0):
            nk, nf = KF * len(srcs), width // P
            with ExitStack() as c:
                xT, pe_chunks, act_chunks = transposed(c, name, srcs)
                w1 = [sb(c, f"{name}_w1_{e}", [P, nk, width]) for e in range(len(experts))]
                w2 = [sb(c, f"{name}_w2_{e}", [P, nf, D]) for e in range(len(experts))]
                b1 = [sb(c, f"{name}_b1_{e}", [P, nf]) for e in range(len(experts))]
                b2 = [sb(c, f"{name}_b2_{e}", [B, D]) for e in range(len(experts))]
                hT = sb(c, name + "_hT", [P, len(experts) * nf, TOK])
                tmp = sb(c, name + "_tmp", [B, CH, D])
                psH = [pb(c, f"{name}_psH{i}") for i in range(2)]
                psY = [pb(c, f"{name}_psY{e}") for e in range(len(experts))]
                loaded, h_mm, h_done, y_mm, fin, own = (
                    sem(name + x) for x in ("_loaded", "_h_mm", "_h", "_y_mm", "_fin", "_own"))
                total = len(experts) * nf
                mv = mover(name, turns)
                with nc.Block() as block:
                    @block.sync
                    def _(sp):
                        for e, w in enumerate(experts):
                            for dst, src in ((w1[e][:, :, :], w[0]), (b1[e][:, :], w[1]), (w2[e][:, :, :], w[2]), (b2[e][:, :], w[3])):
                                if src is not None:
                                    src = src(sp, e) if callable(src) else src
                                    sp.dma_start(dst, src).then_inc(loaded, 16)
                        mv.sp(sp)
                    n_loads = 16 * sum(x is not None for w in experts for x in w)

                    @block.gpsimd
                    def _(pool):
                        mv.pool(pool)

                    @block.tensor
                    def _(pe):
                        pe.wait_ge(loaded, n_loads)

                        def first(k):
                            for i in range(total):
                                e, f = divmod(i, nf)
                                if i >= 2:
                                    pe.wait_ge(h_done, k * total + i - 1)
                                for j in range(nk):
                                    last = pe.matmul(psH[i % 2][:, 0:TOK], w1[e][:, j, f * P:(f + 1) * P], xT[:, j, :],
                                                     start=(j == 0), stop=(j == nk - 1))
                                last.then_inc(h_mm, 1)

                        def second(k):
                            pe.wait_ge(fin, k)
                            pe.wait_ge(h_done, k * total + total)
                            for e in range(len(experts)):
                                for b in range(CH):
                                    for f in range(nf):
                                        last = pe.matmul(psY[e][0:B, b * D:(b + 1) * D],
                                                         hT[:, e * nf + f, b * B:(b + 1) * B], w2[e][:, f, :],
                                                         start=(f == 0), stop=(f == nf - 1))
                            last.then_inc(y_mm, 1)

                        pe_chunks(pe, first, second)

                    @block.scalar
                    def _(act):
                        act.wait_ge(loaded, n_loads)

                        def rest(k):
                            for i in range(total):
                                e, f = divmod(i, nf)
                                act.wait_ge(h_mm, k * total + i + 1)
                                kw = {} if experts[e][1] is None else {"bias": b1[e][:, f:f + 1]}
                                act.activation(hT[:, i, :], psH[i % 2][:, 0:TOK], func, **kw).then_inc(h_done, 1)

                        act_chunks(act, rest)

                    @block.vector
                    def _(dve):
                        st = Steps(dve, own)
                        dve.wait_ge(loaded, n_loads)
                        if setup:
                            setup(dve, st, b2)
                        with loop(dve, NC, st, per) as k:
                            dve.wait_ge(y_mm, k + 1)
                            final(dve, st, k, [p[0:B, :].rearrange("p (b d) -> p b d", b=CH) for p in psY], b2, tmp).then_inc(fin, 1)

        def linear(name, src, w_dram, bias, per, final, turns=0):
            with ExitStack() as c:
                xT, pe_chunks, act_chunks = transposed(c, name, [src])
                w = sb(c, name + "_w", [P, KF, D])
                b2 = sb(c, name + "_b", [B, D])
                psY = pb(c, name + "_psY")
                loaded, y_mm, fin, own = (sem(name + x) for x in ("_loaded", "_y_mm", "_fin", "_own"))
                mv = mover(name, turns)
                with nc.Block() as block:
                    @block.sync
                    def _(sp):
                        sp.dma_start(w[:, :, :], w_dram).then_inc(loaded, 16)
                        if bias is not None:
                            sp.dma_start(b2[:, :], bias.partition_broadcast(B)).then_inc(loaded, 16)
                        mv.sp(sp)
                    n_loads = 32 if bias is not None else 16

                    @block.gpsimd
                    def _(pool):
                        mv.pool(pool)

                    @block.tensor
                    def _(pe):
                        pe.wait_ge(loaded, n_loads)

                        def first(k):
                            pe.wait_ge(fin, k)
                            for b in range(CH):
                                for f in range(KF):
                                    last = pe.matmul(psY[0:B, b * D:(b + 1) * D], xT[:, f, b * B:(b + 1) * B], w[:, f, :],
                                                     start=(f == 0), stop=(f == KF - 1))
                            last.then_inc(y_mm, 1)

                        pe_chunks(pe, first, lambda k: None)

                    @block.scalar
                    def _(act):
                        act_chunks(act, lambda k: None)

                    @block.vector
                    def _(dve):
                        st = Steps(dve, own)
                        dve.wait_ge(loaded, n_loads)
                        with loop(dve, NC, st, per) as k:
                            dve.wait_ge(y_mm, k + 1)
                            final(dve, st, k, psY[0:B, :].rearrange("p (b d) -> p b d", b=CH), b2).then_inc(fin, 1)

        def attention_sums(c0, name, wkv_dram, edge=None, table=None, turns=0):
            kvd = sb(c0, name + "_kvd", [P, KF, P + HH])
            with ExitStack() as c:
                xT, pe_chunks, act_chunks = transposed(c, name, [XN])
                wkv = sb(c, name + "_wkv", [P, KF, 2 * D])
                k_sb = sb(c, name + "_k", [B, CH, D])
                e_sb = sb(c, name + "_e", [B, CH, D])
                v_sb = sb(c, name + "_v", [B, CH, KF, P + 1])
                kva = words[:, NB * D - KF * (P + 1):NB * D]
                psKV = [pb(c, f"{name}_psKV{i}") for i in range(CH)]
                psA = pb(c, name + "_psA")
                if edge:
                    wqk = sb(c, name + "_wqk", [P, KF, 2 * SMALL])
                    bqk = sb(c, name + "_bqk", [1, 2 * SMALL])
                    bk = sb(c, name + "_bk", [SMALL, 1])
                    flat = words[0:B, :]
                    q_all = flat[:, 0:NB * SMALL].rearrange("p (b n) -> p b n", n=SMALL)
                    k_all = flat[:, NB * SMALL:2 * NB * SMALL].rearrange("p (b n) -> p b n", n=SMALL)
                    psQ = pb(c, name + "_psQ")
                    psK = pb(c, name + "_psK")
                loaded, kv_mm, e_done, k_done, v_done, a_mm, a_done, own, stored, setup = (
                    sem(name + x) for x in ("_loaded", "_kv_mm", "_e", "_k", "_v", "_a_mm", "_a", "_own", "_stored", "_setup"))
                mv = mover(name, turns)
                pos_own, pos_done = sem(name + "_pos_own"), sem(name + "_positions")
                qk_mm, qk_done, low_done = sem(name + "_qk_mm"), sem(name + "_qk"), sem(name + "_low")
                with nc.Block() as block:
                    @block.sync
                    def _(sp):
                        sp.dma_start(wkv[:, :, :], wkv_dram).then_inc(loaded, 16)
                        if edge:
                            sp.dma_start(wqk[:, :, :], edge["wqk"]).then_inc(loaded, 16)
                            sp.dma_start(bqk[:, :], edge["bqk"]).then_inc(loaded, 16)
                            sp.dma_start(bk[:, :], edge["bk"]).then_inc(loaded, 16)
                        for i in range(5):
                            n = NB // 5
                            sp.dma_start(rows(table)[:, i * n:(i + 1) * n, 0:D], XN[0:B, i * n:(i + 1) * n, :]).then_inc(stored, 16)
                        mv.sp(sp)
                        if edge:
                            sp.wait_ge(pos_done, 1)
                            sp.dma_start(spill_pos[1], posi[:, :]).then_inc(stored, 16)
                            sp.wait_ge(qk_done, 3 * NC)
                            sp.dma_start(rows(table)[:, :, D:D + SMALL], q_all[:, :, :]).then_inc(stored, 16)
                        sp.wait_ge(stored, 16 * (7 if edge else 5))

                    n_loads = 64 if edge else 16

                    @block.gpsimd
                    def _(pool):
                        mv.pool(pool)

                    @block.tensor
                    def _(pe):
                        pe.wait_ge(loaded, n_loads)
                        pe.wait_ge(setup, 1)

                        def first(k):
                            for b in range(CH):
                                for f in range(KF):
                                    last = pe.matmul(psKV[b][0:B, :], xT[:, f, b * B:(b + 1) * B], wkv[:, f, :],
                                                     start=(f == 0), stop=(f == KF - 1))
                            last.then_inc(kv_mm, 1)
                            if edge:
                                for b in range(CH):
                                    o = psQ[0:B, b * 64:b * 64 + 2 * SMALL]
                                    pe.matmul(o, ones[0:1, 0:B], bqk[:, :], start=True, stop=False)
                                    for f in range(KF):
                                        pe.matmul(o, xT[:, f, b * B:(b + 1) * B], wqk[:, f, :], start=False, stop=(f == KF - 1))
                                for f in range(KF):
                                    last = pe.matmul(psK[0:SMALL, 0:TOK], wqk[:, f, SMALL:2 * SMALL], xT[:, f, :],
                                                     start=(f == 0), stop=(f == KF - 1))
                                last.then_inc(qk_mm, 1)

                        def second(k):
                            pe.wait_ge(k_done, k + 1)
                            pe.wait_ge(v_done, k * CH + CH)
                            pe.wait_ge(a_done, k)
                            if edge:
                                pe.wait_ge(qk_done, 3 * k + 3)
                            for f in range(KF):
                                for b in range(CH):
                                    last = pe.matmul(psA[:, f * (P + 1):(f + 1) * (P + 1)], k_sb[:, b, f * P:(f + 1) * P],
                                                     v_sb[:, b, f, :], start=(b == 0), stop=(b == CH - 1))
                            last.then_inc(a_mm, 1)

                        pe_chunks(pe, first, second)

                    @block.scalar
                    def _(act):
                        act.wait_ge(loaded, n_loads)
                        act.wait_ge(setup, 1)

                        def rest(k):
                            act.wait_ge(low_done, k + 1)
                            for b in range(CH):
                                act.activation(v_sb[:, b, :, 0:P], psKV[b][0:B, D:2 * D].rearrange("p (f d) -> p f d", f=KF),
                                               ACT.Copy).then_inc(v_done, 1)
                            act.activation(e_sb[:, :, :], e_sb[:, :, :], ACT.Exp).then_inc(e_done, 1)
                            if edge:
                                act.wait_ge(qk_mm, k + 1)
                                q = psQ[0:B, 0:64 * CH].rearrange("p (b n) -> p b n", b=CH)
                                act.activation(q_all[:, bass.ds(k * CH, CH), :], q[:, :, 0:SMALL], ACT.Tanh).then_inc(qk_done, 1)
                                act.activation(k_all[:, bass.ds(k * CH, CH), :], q[:, :, SMALL:2 * SMALL], ACT.Copy).then_inc(qk_done, 1)
                                act.activation(edge["kT"][:, bass.ds(k * CH, CH), :], psK[0:SMALL, 0:TOK].rearrange("p (b n) -> p b n", b=CH),
                                               ACT.Identity, bias=bk[:, 0:1]).then_inc(qk_done, 1)

                        act_chunks(act, rest)

                    @block.vector
                    def _(dve):
                        st = Steps(dve, own)
                        dve.memset(kvd[:, :, :], 0.0)
                        st(dve.memset(kva[:, :], 0.0))
                        dve.memset(v_sb[:, :, :, P:P + 1], 1.0).then_inc(setup, 1)
                        places = Places(dve, pos_own)
                        with loop(dve, NC, places.st, 8 if edge else 0) as k:
                            dve.wait_ge(kv_mm, k + 1)
                            for b in range(CH):
                                last = dve.tensor_scalar(e_sb[:, b, :], psKV[b][0:B, 0:D], 0.0, None, ALU.min)
                            last.then_inc(low_done, 1)
                            dve.wait_ge(e_done, k + 1)
                            for b in range(CH):
                                last = dve.scalar_tensor_tensor(k_sb[:, b, :], psKV[b][0:B, 0:D], 0.0, e_sb[:, b, :], ALU.max, ALU.add)
                            last.then_inc(k_done, 1)
                            if edge:
                                places.blocks(k * 2, 2)
                            dve.wait_ge(a_mm, k + 1)
                            dve.wait_ge(a_done, k)
                            dve.tensor_tensor(kva[:, :], kva[:, :], psA[:, 0:KF * (P + 1)], ALU.add).then_inc(a_done, 1)
                        if edge:
                            places.finish(pos_done)
                        dve.wait_ge(a_done, NC)
                        for f in range(KF):
                            for h in range(HH):
                                r = slice(h * HD, (h + 1) * HD)
                                dve.tensor_copy(kvd[r, f, h * HD:(h + 1) * HD], kva[r, f * (P + 1) + h * HD:f * (P + 1) + (h + 1) * HD])
                                dve.tensor_copy(kvd[r, f, P + h:P + h + 1], kva[r, f * (P + 1) + P:f * (P + 1) + P + 1])
                        if edge:
                            dve.wait_ge(qk_done, 3 * NC)
                            st(dve.tensor_tensor(k_all[:, :, :], k_all[:, :, :], q_all[:, :, :], ALU.mult))
                            dve.tensor_reduce(edge["m"][:, :], k_all[:, :, :], AX.X, ALU.add)
                            dve.memset(edge["l"][:, :], 1.0)
            return kvd

        def attention_rows(name, wq_dram, kvd, residual, turns=0):
            with ExitStack() as c:
                xT, pe_chunks, act_chunks = transposed(c, name, [XN])
                wq = sb(c, name + "_wq", [P, KF, D])
                e_sb = sb(c, name + "_e", [P, KF, TOK])
                qT = sb(c, name + "_qT", [P, KF, TOK])
                z = sb(c, name + "_z", [B, CH, HEADS])
                psQ = [pb(c, f"{name}_psQ{i}") for i in range(KF)]
                psM = [pb(c, f"{name}_psM{i}") for i in range(CH)]
                loaded, q_mm, low_done, e_done, q_done, m_mm, fin, own = (
                    sem(name + x) for x in ("_loaded", "_q_mm", "_low", "_e", "_q", "_m_mm", "_fin", "_own"))
                mv = mover(name, turns)
                with nc.Block() as block:
                    @block.sync
                    def _(sp):
                        sp.dma_start(wq[:, :, :], wq_dram).then_inc(loaded, 16)
                        mv.sp(sp)

                    @block.gpsimd
                    def _(pool):
                        mv.pool(pool)

                    @block.tensor
                    def _(pe):
                        pe.wait_ge(loaded, 16)

                        def first(k):
                            for f in range(KF):
                                for j in range(KF):
                                    last = pe.matmul(psQ[f][:, 0:TOK], wq[:, j, f * P:(f + 1) * P], xT[:, j, :],
                                                     start=(j == 0), stop=(j == KF - 1))
                            last.then_inc(q_mm, 1)

                        def second(k):
                            pe.wait_ge(q_done, k + 1)
                            pe.wait_ge(fin, k)
                            for b in range(CH):
                                for f in range(KF):
                                    last = pe.matmul(psM[b][0:B, f * (P + HH):(f + 1) * (P + HH)], qT[:, f, b * B:(b + 1) * B],
                                                     kvd[:, f, :], start=True, stop=True)
                            last.then_inc(m_mm, 1)

                        pe_chunks(pe, first, second)

                    @block.scalar
                    def _(act):
                        def rest(k):
                            act.wait_ge(low_done, k + 1)
                            act.activation(e_sb[:, :, :], e_sb[:, :, :], ACT.Exp).then_inc(e_done, 1)

                        act_chunks(act, rest)

                    @block.vector
                    def _(dve):
                        st = Steps(dve, own)
                        with loop(dve, NC, st, 2 + CH if residual else 2) as k:
                            dve.wait_ge(q_mm, k + 1)
                            for f in range(KF):
                                last = dve.tensor_scalar(e_sb[:, f, :], psQ[f][:, 0:TOK], 0.0, None, ALU.min)
                            last.then_inc(low_done, 1)
                            dve.wait_ge(e_done, k + 1)
                            for f in range(KF):
                                last = dve.scalar_tensor_tensor(qT[:, f, :], psQ[f][:, 0:TOK], 0.0, e_sb[:, f, :], ALU.max, ALU.add)
                            last.then_inc(q_done, 1)
                            dve.wait_ge(m_mm, k + 1)
                            msg = [psM[b][0:B, 0:KF * (P + HH)].rearrange("p (f n) -> p f n", f=KF) for b in range(CH)]
                            for b in range(CH):
                                last = dve.tensor_scalar(z[:, b, :].rearrange("p (f h) -> p f h", f=KF), msg[b][:, :, P:P + HH],
                                                         ATT_EPS, None, ALU.add)
                            st(last)
                            st(dve.reciprocal(z[:, :, :], z[:, :, :]))
                            for b in range(CH):
                                u = one(U[:, bass.ds(k * CH + b, 1), :])
                                n = dve.tensor_tensor(u.rearrange("p (f h d) -> p f h d", f=KF, h=HH),
                                                      msg[b][:, :, 0:P].rearrange("p f (h d) -> p f h d", h=HH),
                                                      z[:, b, :].rearrange("p (f h) -> p f h", f=KF).unsqueeze(3).broadcast_to([B, KF, HH, HD]), ALU.mult)
                                if residual:
                                    st(n)
                                    n = dve.tensor_tensor(u, u, one(XN[0:B, bass.ds(k * CH + b, 1), :]), ALU.add)
                            n.then_inc(fin, 1)


        def edge_walk(name, which, table, width, rec_t, rec_free):
            T = NG // RING
            rec_g = XN[:, :, :].rearrange("p b d -> p (b d)")[:, NB * D - RING * SUB * RW:NB * D].rearrange(
                "p (r s w) -> p r s w", r=RING, s=SUB)
            rows_t = XN[:, :, :].rearrange("p b d -> p (b d)")[:, 0:RING * SUB * width].rearrange(
                "p (r s w) -> p r s w", r=RING, s=SUB)
            rec_v = rec_d[which].rearrange("(g p s) w -> g p (s w)", p=P, s=SUB)
            group_ready = [sem(f"{name}_group{s}") for s in range(RING)]
            rec_ready = [sem(f"{name}_rec{s}") for s in range(RING)]
            got = [pool_dma_sem(f"{name}_got{s}") for s in range(RING)]
            arrived, used, settled = (sem(f"{name}_{x}") for x in ("arrived", "used", "settled"))

            def each_group(eng, body):
                for s in range(RING):
                    body(0, s)
                with loop(eng, T - 1) as u:
                    for s in range(RING):
                        body(u + 1, s)
                for s in range(NG - T * RING):
                    body(T, s)

            def load_records(eng, g, dst, ready):
                eng.dma_start(dst.rearrange("p s w -> p (s w)"),
                              rec_v[bass.ds(g, 1), :, :].rearrange("g p w -> (g p) w")).then_inc(ready, 16)

            def sp_part(sp):
                def arrive(t, s):
                    sp.wait_ge(got[s], t * (16 * SUB) + 16 * SUB)
                    sp.sem_inc(arrived, 1)

                def body(t, s):
                    load_records(sp, t * RING + s, rec_g[:, s, :, :], group_ready[s])
                    if near(t, s, -LAG):
                        arrive(*near(t, s, -LAG))

                each_group(sp, body)
                for g in range(NG - LAG, NG):
                    arrive(g // RING, g % RING)

            def pool_part(pool):
                def body(t, s):
                    pool.wait_ge(group_ready[s], t * 16 + 16)
                    if not (isinstance(t, int) and t == 0):
                        n = pool.value_load(first_step[which][0:1, bass.ds((t - 1) * RING + s + 1, 1)], min_val=1, max_val=NS)
                        pool.wait_ge(used, n)
                    settle(pool, cell[0:1, 0:1], settled, t * RING + s)
                    for j in range(SUB):
                        pool.indirect_dma_start(out=rows_t[:, s, j, :], out_offset=None, in_=table,
                                                in_offset=bass.IndirectOffsetOnAxis(ap=rec_g[:, s, j, 1:2].bitcast(I32), axis=0)).then_inc(got[s], 16)

                each_group(pool, body)

            def group_of(eng, x):
                return eng.value_load(step_grp[which][0:1, bass.ds(x, 1)], min_val=0, max_val=NG - 1)

            def step_records(act, t, s):
                g = group_of(act, step(t, s))
                act.wait_ge(rec_free[s], t)
                load_records(act, g, rec_t[:, s, :, :], rec_ready[s])

            def slot_of(g):
                return bass.ds(g % RING, 1)

            return rows_t, rec_ready, arrived, used, sp_part, pool_part, group_of, step_records, slot_of

        def each_step(eng, steps, per, body):
            T = NS // RING
            for s in range(RING):
                body(0, s)
            with loop(eng, T - 2, steps, per) as u:
                for s in range(RING):
                    body(u + 1, s)
            for s in range(RING):
                body(T - 1, s)

        def step(t, s):
            return t * RING + s

        def near(t, s, n):
            if isinstance(t, int) and not 0 <= t * RING + s + n < NS:
                return None
            return t + (s + n) // RING, (s + n) % RING

        def begins(t, s, n=1):
            return isinstance(t, int) and t * RING + s < n

        def edge_softmax(edge):
            name, W = "gat", D + SMALL
            kT, m, l = edge["kT"], edge["m"], edge["l"]
            SC = 1.0 / float(np.sqrt(SMALL))
            with ExitStack() as c:
                rec_t = sb(c, name + "_rec", [P, RING, SUB, RW])
                lf = sb(c, name + "_lf", [P, RING, SUB])
                lk = sb(c, name + "_lk", [P, RING, SUB], BF16)
                kTs = sb(c, name + "_kTs", [SMALL, 2, B])
                free = RING * SUB * W

                def room_for(p, n):
                    nonlocal free
                    free += 2 * n
                    return XN[0:p, :, :].rearrange("p b d -> p (b d)")[:, free - 2 * n:free].rearrange("p (a n) -> p a n", a=2)

                qT, S, pT = room_for(SMALL, G), room_for(B, G), room_for(B, G)
                q_rows = room_for(P, SUB * SMALL)
                pE = sb(c, name + "_pE", [P, 2, SUB * B])
                pen = sb(c, name + "_pen", [B, 2, G])
                mx, mo, mn, nm, df, sc, rs, scl, rsl = (
                    sb(c, f"{name}_{x}", [B, 2]) for x in ("mx", "mo", "mn", "nm", "df", "sc", "rs", "scl", "rsl"))
                psA, psB, psP = pb(c, name + "_psA"), pb(c, name + "_psB", dt=BF16), pb(c, name + "_psP")
                psS = [pb(c, f"{name}_psS{i}") for i in range(2)]
                psE = [pb(c, f"{name}_psE{i}") for i in range(2)]
                q_ready = sem(name + "_q_rows")
                qk_done, pen_done, s_mm, s_done, e_done, p_turned, p_done, own, ready = (
                    sem(f"{name}_{x}") for x in ("qk", "pen", "s_mm", "s", "e", "p_turned", "p", "own", "ready"))
                added = [sem(f"{name}_added{i}") for i in range(2)]
                near_done = [sem(f"{name}_near{s}") for s in range(RING)]
                turned = [sem(f"{name}_turned{s}") for s in range(RING)]
                rows_t, rec_ready, arrived, used, sp_part, pool_part, group_of, step_records, slot_of = edge_walk(
                    name, 0, table0, W, rec_t, near_done)

                with nc.Block() as block:
                    @block.vector
                    def _(dve):
                        dve.tensor_copy(U[:, :, :], XN[0:B, :, :])

                with nc.Block() as block:
                    @block.sync
                    def _(sp):
                        sp_part(sp)

                    @block.gpsimd
                    def _(pool):
                        pool_part(pool)

                    @block.tensor
                    def _(pe):
                        def turn(t, s):
                            x = step(t, s)
                            pe.wait_ge(q_ready, x + 1)
                            pe.wait_ge(near_done[s], t + 1)
                            if not begins(t, s):
                                pe.wait_ge(qk_done, x)
                                pe.wait_ge(pen_done, x)
                            for j in range(SUB):
                                pe.transpose(psA[0:SMALL, j * P:(j + 1) * P], q_rows[:, s % 2, j * SMALL:(j + 1) * SMALL], ident[:, :])
                            for j in range(SUB):
                                last = pe.transpose(psB[0:B, j * P:(j + 1) * P],
                                                    lk[:, s, j:j + 1].broadcast_to([P, B]), ident16[:, :])
                            last.then_inc(turned[s], 1)

                        def scores(t, s):
                            x, d = step(t, s), s % 2
                            pe.wait_ge(qk_done, x + 1)
                            if not begins(t, s, 2):
                                pe.wait_ge(s_done, x - 1)
                            pe.matmul(psS[d][0:B, :], kTs[:, d, :], qT[:, d, :], start=True, stop=True).then_inc(s_mm, 1)

                        def weights(t, s):
                            x, d = step(t, s), s % 2
                            pe.wait_ge(e_done, x + 1)
                            pe.wait_ge(p_done, x)
                            for j in range(SUB):
                                last = pe.transpose(psP[:, j * B:(j + 1) * B], pT[:, d, j * P:(j + 1) * P], ident[0:B, 0:B])
                            last.then_inc(p_turned, 1)

                        def sums(t, s):
                            x, d = step(t, s), s % 2
                            pe.wait_ge(p_done, x + 1)
                            pe.wait_ge(added[d], t * (RING // 2) + s // 2)
                            g = group_of(pe, x)
                            for j in range(SUB):
                                last = pe.matmul(psE[d][0:B, 0:D], pE[:, d, j * B:(j + 1) * B],
                                                 rows_t[:, slot_of(g), j, 0:D].rearrange("p a w -> p (a w)"),
                                                 start=(j == 0), stop=(j == SUB - 1))
                            last.then_inc(used, 1)

                        def body(t, s):
                            if near(t, s, 1):
                                scores(*near(t, s, 1))
                            if near(t, s, 2):
                                turn(*near(t, s, 2))
                            if near(t, s, -1):
                                sums(*near(t, s, -1))
                            weights(t, s)

                        turn(0, 0)
                        turn(0, 1)
                        scores(0, 0)
                        each_step(pe, None, 0, body)
                        sums(NS // RING - 1, RING - 1)

                    @block.scalar
                    def _(act):
                        def qk(t, s):
                            d = s % 2
                            b = act.value_load(step_blk[0][0:1, bass.ds(step(t, s), 1)], min_val=0, max_val=NB - 1)
                            act.wait_ge(turned[s], t + 1)
                            if not begins(t, s, 2):
                                act.wait_ge(s_mm, step(t, s) - 1)
                            act.activation(kTs[:, d, :], one(kT[:, bass.ds(b, 1), :]), ACT.Copy)
                            act.activation(qT[:, d, :], psA[0:SMALL, :], ACT.Copy).then_inc(qk_done, 1)

                        def take_q(t, s):
                            g = group_of(act, step(t, s))
                            act.wait_ge(arrived, g + 1)
                            if not begins(t, s, 2):
                                u, v = near(t, s, -2)
                                act.wait_ge(turned[v], u + 1)
                            act.activation(q_rows[:, s % 2, :].rearrange("p (s n) -> p s n", s=SUB),
                                           rows_t[:, slot_of(g), :, D:W].rearrange("p a s w -> p (a s) w"), ACT.Copy).then_inc(q_ready, 1)

                        def body(t, s):
                            d, x = s % 2, step(t, s)
                            if near(t, s, AHEAD):
                                step_records(act, *near(t, s, AHEAD))
                            if near(t, s, 3):
                                take_q(*near(t, s, 3))
                            act.wait_ge(s_done, x + 1)
                            act.activation(pT[:, d, :], S[:, d, :], ACT.Exp, bias=nm[:, d:d + 1], scale=SC, accum_out=rs[:, d:d + 1])
                            act.activation(sc[:, d:d + 1], df[:, d:d + 1], ACT.Exp).then_inc(e_done, 1)
                            if near(t, s, 2):
                                qk(*near(t, s, 2))
                            act.wait_ge(p_turned, x + 1)
                            act.activation(pE[:, d, :], psP[:, 0:SUB * B], ACT.Copy).then_inc(p_done, 1)

                        for i in range(AHEAD):
                            step_records(act, 0, i)
                        for i in range(2):
                            take_q(0, i)
                        qk(0, 0)
                        take_q(0, 2)
                        qk(0, 1)
                        each_step(act, None, 0, body)

                    @block.vector
                    def _(dve):
                        st = Steps(dve, own)

                        def targets(t, s):
                            x = step(t, s)
                            dve.wait_ge(rec_ready[s], t * 16 + 16)
                            st(dve.tensor_scalar(lf[:, s, :], rec_t[:, s, :, 0], step_node[0][:, bass.ds(x, 1)], -1.0, ALU.subtract, ALU.max))
                            dve.tensor_scalar(lk[:, s, :], lf[:, s, :], float(B), None, ALU.min).then_inc(near_done[s], 1)

                        def masks(t, s):
                            d = s % 2
                            dve.wait_ge(turned[s], t + 1)
                            dve.tensor_scalar(pen[:, d, :], psB[0:B, :], iota_p[0:B, 0:1], -BIG, ALU.not_equal, ALU.mult).then_inc(pen_done, 1)

                        def maxima(t, s):
                            x, d = step(t, s), s % 2
                            b = dve.value_load(step_blk[0][0:1, bass.ds(x, 1)], min_val=0, max_val=NB - 1)
                            mb = m[:, bass.ds(b, 1)]
                            dve.wait_ge(pen_done, x + 1)
                            dve.wait_ge(s_mm, x + 1)
                            if not begins(t, s, 2):
                                dve.wait_ge(e_done, x - 1)
                            st.all()
                            st.mark(dve.tensor_copy(mo[:, d:d + 1], mb))
                            st(dve.tensor_tensor_reduce(out=S[:, d, :], in0=psS[d][0:B, :], in1=pen[:, d, :], scale=1.0, scalar=-BIG,
                                                        op0=ALU.add, op1=ALU.max, accum_out=mx[:, d:d + 1]))
                            st(dve.tensor_tensor(mn[:, d:d + 1], mo[:, d:d + 1], mx[:, d:d + 1], ALU.max))
                            st(dve.tensor_scalar(nm[:, d:d + 1], mn[:, d:d + 1], -SC, None, ALU.mult))
                            dve.scalar_tensor_tensor(df[:, d:d + 1], mo[:, d:d + 1], SC, nm[:, d:d + 1], ALU.mult, ALU.add).then_inc(s_done, 1)
                            st.mark(dve.tensor_copy(mb, mn[:, d:d + 1]))

                        def add(t, s):
                            d = s % 2
                            b = dve.value_load(step_blk[0][0:1, bass.ds(step(t, s), 1)], min_val=0, max_val=NB - 1)
                            lb, ub = l[:, bass.ds(b, 1)], one(U[:, bass.ds(b, 1), :])
                            dve.wait_ge(used, step(t, s) + 1)
                            st.all()
                            st.mark(dve.scalar_tensor_tensor(lb, lb, scl[:, d:d + 1], rsl[:, d:d + 1], ALU.mult, ALU.add))
                            dve.wait_ge(added[1 - d], t * (RING // 2) + (s + 1) // 2)
                            dve.scalar_tensor_tensor(ub, ub, scl[:, d:d + 1], psE[d][0:B, 0:D], ALU.mult, ALU.add).then_inc(added[d], 1)

                        def keep(t, s):
                            d = s % 2
                            dve.wait_ge(e_done, step(t, s) + 1)
                            st.mark(dve.tensor_copy(scl[:, d:d + 1], sc[:, d:d + 1]))
                            st.mark(dve.tensor_copy(rsl[:, d:d + 1], rs[:, d:d + 1]))

                        def body(t, s):
                            if near(t, s, 1):
                                maxima(*near(t, s, 1))
                            if near(t, s, 3):
                                targets(*near(t, s, 3))
                            if near(t, s, 2):
                                masks(*near(t, s, 2))
                            if near(t, s, -1):
                                add(*near(t, s, -1))
                            keep(t, s)

                        for i in range(3):
                            targets(0, i)
                        masks(0, 0)
                        masks(0, 1)
                        maxima(0, 0)
                        each_step(dve, st, RING * 9, body)
                        add(NS // RING - 1, RING - 1)

        def edge_sums():
            name = "gcn"
            with ExitStack() as c:
                rec_t = sb(c, name + "_rec", [P, RING, SUB, RW])
                lk = sb(c, name + "_lk", [P, 2, SUB])
                pE = sb(c, name + "_pE", [P, 2, SUB, B])
                psE = [pb(c, f"{name}_psE{i}") for i in range(2)]
                rec_free = [sem(f"{name}_rec_free{s}") for s in range(RING)]
                rows_t, rec_ready, arrived, used, sp_part, pool_part, group_of, step_records, slot_of = edge_walk(
                    name, 1, table1, D, rec_t, rec_free)
                own = sem(name + "_own")
                added = [sem(f"{name}_added{i}") for i in range(2)]

                with nc.Block() as block:
                    @block.vector
                    def _(dve):
                        dve.memset(U[:, :, :], 0.0)

                with nc.Block() as block:
                    @block.sync
                    def _(sp):
                        sp_part(sp)

                    @block.gpsimd
                    def _(pool):
                        pool_part(pool)

                    @block.scalar
                    def _(act):
                        with loop(act, NS // RING) as t:
                            for s in range(RING):
                                step_records(act, t, s)

                    @block.tensor
                    def _(pe):
                        with loop(pe, NS // RING) as t:
                            for s in range(RING):
                                d = s % 2
                                g = group_of(pe, t * RING + s)
                                pe.wait_ge(arrived, g + 1)
                                pe.wait_ge(rec_free[s], t + 1)
                                pe.wait_ge(added[d], t * (RING // 2) + s // 2)
                                for j in range(SUB):
                                    last = pe.matmul(psE[d][0:B, 0:D], pE[:, d, j, :],
                                                     rows_t[:, slot_of(g), j, :].rearrange("p a w -> p (a w)"),
                                                     start=(j == 0), stop=(j == SUB - 1))
                                last.then_inc(used, 1)

                    @block.vector
                    def _(dve):
                        st = Steps(dve, own)

                        def weights(t, s):
                            x, d = t * RING + s, s % 2
                            dve.wait_ge(rec_ready[s], t * 16 + 16)
                            if near(t, s, -2):
                                dve.wait_ge(used, x - 1)
                            st(dve.tensor_scalar(lk[:, d, :], rec_t[:, s, :, 0], step_node[1][:, bass.ds(x, 1)], None, ALU.subtract))
                            for j in range(SUB):
                                last = dve.tensor_scalar(pE[:, d, j, :], iota_n[:, :], lk[:, d, j:j + 1], rec_t[:, s, j, 2:3],
                                                         ALU.is_equal, ALU.mult)
                            last.then_inc(rec_free[s], 1)

                        def body(t, s):
                            d = s % 2
                            if near(t, s, 1):
                                weights(*near(t, s, 1))
                            b = dve.value_load(step_blk[1][0:1, bass.ds(t * RING + s, 1)], min_val=0, max_val=NB - 1)
                            ub = one(U[:, bass.ds(b, 1), :])
                            dve.wait_ge(used, t * RING + s + 1)
                            dve.wait_ge(added[1 - d], t * (RING // 2) + (s + 1) // 2)
                            dve.tensor_tensor(ub, ub, psE[d][0:B, 0:D], ALU.add).then_inc(added[d], 1)

                        weights(0, 0)
                        each_step(dve, st, RING, body)

        def route_rows(selw, turns):
            name = "topk"
            with ExitStack() as c:
                wr = sb(c, name + "_wr", [B, D])
                br = sb(c, name + "_br", [B, 1])
                w = sb(c, name + "_w", [B, NB])
                v = sb(c, name + "_v", [B, NB])
                junk = sb(c, name + "_junk", [B, R, D])
                eq = sb(c, name + "_eq", [B, NB])
                gt = sb(c, name + "_gt", [B, NB])
                tot = sb(c, name + "_tot", [B, NB])
                cum = sb(c, name + "_cum", [B, NB])
                cnt, pos, sign, kk, thr, take = (sb(c, f"{name}_{x}", [B, 1]) for x in ("cnt", "pos", "sign", "kk", "thr", "take"))
                T, bit, cand, add = (sb(c, f"{name}_{x}", [B, 1], I32) for x in ("T", "bit", "cand", "add"))
                ps = pb(c, name + "_ps")
                loaded, own, cnt_done, sum_done, eq_done, rank_done = (
                    sem(f"{name}_{x}") for x in ("loaded", "own", "cnt", "sum", "eq", "rank"))
                mv = mover(name, turns)
                BITS = 31
                with nc.Block() as block:
                    @block.sync
                    def _(sp):
                        sp.dma_start(wr[:, :], A["L0_ffn_wr"].partition_broadcast(B)).then_inc(loaded, 16)
                        sp.dma_start(br[:, :], A["L0_ffn_br"].partition_broadcast(B)).then_inc(loaded, 16)
                        mv.sp(sp)

                    @block.gpsimd
                    def _(pool):
                        mv.pool(pool)

                    @block.tensor
                    def _(pe):
                        with loop(pe, BITS + 2) as i:
                            pe.wait_ge(cnt_done, i + 1)
                            pe.matmul(ps[0:B, 0:1], ones[0:B, 0:B], cnt[:, :], start=True, stop=True).then_inc(sum_done, 1)
                        pe.wait_ge(eq_done, 1)
                        pe.matmul(ps[0:B, 64:64 + NB], lower[0:B, 0:B], eq[:, :], start=True, stop=True)
                        pe.matmul(ps[0:B, 128:128 + NB], ones[0:B, 0:B], eq[:, :], start=True, stop=True).then_inc(rank_done, 1)

                    @block.vector
                    def _(dve):
                        st = Steps(dve, own)
                        dve.wait_ge(loaded, 32)
                        with loop(dve, NB // R, st, R) as t:
                            for i in range(R):
                                r = bass.ds(t * R + i, 1)
                                st.mark(dve.scalar_tensor_tensor(junk[:, i, :], one(XN[0:B, r, :]), 1.0, wr[:, :], ALU.mult, ALU.mult,
                                                                 accum_out=w[:, r]))
                            st.all()
                        st(dve.tensor_scalar(w[:, :], w[:, :], br[:, 0:1], None, ALU.add))
                        dve.tensor_scalar(v[:, :], w[:, :], 0.0, 0.0, ALU.is_ge, ALU.add, accum_out=cnt[:, :]).then_inc(cnt_done, 1)
                        dve.wait_ge(sum_done, 1)
                        st(dve.tensor_scalar(pos[:, :], ps[0:B, 0:1], float(TOPK), None, ALU.is_ge))
                        st(dve.tensor_scalar(sign[:, :], pos[:, :], 2.0, -1.0, ALU.mult, ALU.add))
                        st(dve.tensor_scalar(kk[:, :], pos[:, :], float(2 * TOPK - N - 1), float(N - TOPK + 1), ALU.mult, ALU.add))
                        st(dve.tensor_scalar(v[:, :], w[:, :], sign[:, 0:1], None, ALU.mult))
                        st.mark(dve.memset(T[:, :], 0))
                        st(dve.memset(bit[:, :], 1 << (BITS - 1)))
                        with loop(dve, BITS, st, 5) as i:
                            st(dve.tensor_tensor(cand[:, :], T[:, :], bit[:, :], ALU.bitwise_or))
                            dve.tensor_scalar(eq[:, :], v[:, :], cand[:, 0:1].bitcast(F32), 0.0, ALU.is_ge, ALU.add,
                                              accum_out=cnt[:, :]).then_inc(cnt_done, 1)
                            dve.wait_ge(sum_done, i + 2)
                            st(dve.tensor_scalar(take[:, :], ps[0:B, 0:1], kk[:, 0:1], None, ALU.is_ge))
                            st(dve.tensor_tensor(add[:, :], take[:, :], bit[:, :], ALU.mult))
                            st(dve.tensor_tensor(T[:, :], T[:, :], add[:, :], ALU.bitwise_or))
                            st(dve.tensor_scalar(bit[:, :], bit[:, :], 1, None, ALU.logical_shift_right))
                        st(dve.tensor_scalar(thr[:, :], T[:, 0:1].bitcast(F32), sign[:, 0:1], None, ALU.mult))
                        dve.tensor_scalar(eq[:, :], w[:, :], thr[:, 0:1], None, ALU.is_equal).then_inc(eq_done, 1)
                        st.mark(dve.tensor_scalar(gt[:, :], w[:, :], thr[:, 0:1], None, ALU.is_gt))
                        dve.tensor_scalar(v[:, :], w[:, :], thr[:, 0:1], 0.0, ALU.is_gt, ALU.add, accum_out=cnt[:, :]).then_inc(cnt_done, 1)
                        dve.wait_ge(sum_done, BITS + 2)
                        dve.wait_ge(rank_done, 1)
                        st(dve.tensor_scalar(kk[:, :], ps[0:B, 0:1], -1.0, float(TOPK), ALU.mult, ALU.add))
                        st(dve.tensor_copy(tot[:, :], ps[0:B, 128:128 + NB]))
                        st(dve.tensor_tensor_scan(cum[:, :], ones[0:B, 0:NB], tot[:, :], 0.0, ALU.mult, ALU.add))
                        st(dve.tensor_tensor(cum[:, :], cum[:, :], tot[:, :], ALU.subtract))
                        st(dve.tensor_tensor(cum[:, :], cum[:, :], ps[0:B, 64:64 + NB], ALU.add))
                        st(dve.scalar_tensor_tensor(cum[:, :], cum[:, :], kk[:, 0:1], eq[:, :], ALU.is_lt, ALU.mult))
                        st(dve.tensor_tensor(gt[:, :], gt[:, :], cum[:, :], ALU.add))
                        dve.tensor_tensor(selw[:, :], gt[:, :], w[:, :], ALU.mult)

        def route_experts(topi, topw):
            name = "route"
            n_e = 8
            cap = float(-(-N * 125 // (n_e * 100)))
            with ExitStack() as c:
                wr = sb(c, name + "_wr", [P, KF, n_e])
                br = sb(c, name + "_br", [1, n_e])
                colsum = sb(c, name + "_colsum", [B, D])
                mT = sb(c, name + "_mT", [P, KF])
                lg, ex, rw, sc, top = (sb(c, f"{name}_{x}", [1, n_e]) for x in ("lg", "ex", "rw", "sc", "top"))
                mx, sm = sb(c, name + "_mx", [1, 1]), sb(c, name + "_sm", [1, 1])
                ps, ps2, ps3 = pb(c, name + "_ps"), pb(c, name + "_ps2"), pb(c, name + "_ps3")
                loaded, own, col_done, mean_mm, mT_done, lg_mm, to_exp, exp_done, w_done, w_mm = (
                    sem(f"{name}_{x}") for x in ("loaded", "own", "col", "mean_mm", "mT", "lg_mm", "to_exp", "exp", "w", "w_mm"))
                with nc.Block() as block:
                    @block.sync
                    def _(sp):
                        sp.dma_start(wr[:, :, :], A["L1_ffn_Wr"]).then_inc(loaded, 16)
                        sp.dma_start(br[:, :], A["L1_ffn_br"]).then_inc(loaded, 16)

                    @block.tensor
                    def _(pe):
                        pe.wait_ge(col_done, 1)
                        for f in range(KF):
                            last = pe.matmul(ps[:, f:f + 1], colsum[:, f * P:(f + 1) * P], ones[0:B, 0:1], start=True, stop=True)
                        last.then_inc(mean_mm, 1)
                        pe.wait_ge(mT_done, 1)
                        pe.wait_ge(loaded, 32)
                        for f in range(KF):
                            last = pe.matmul(ps2[0:1, 0:n_e], mT[:, f:f + 1], wr[:, f, :], start=(f == 0), stop=(f == KF - 1))
                        last.then_inc(lg_mm, 1)
                        pe.wait_ge(w_done, 1)
                        pe.matmul(ps3[0:B, 0:2], ones[0:1, 0:B], lg[:, 0:2], start=True, stop=True).then_inc(w_mm, 1)

                    @block.scalar
                    def _(act):
                        for i in range(3):
                            act.wait_ge(to_exp, i + 1)
                            k = n_e if i < 2 else 2
                            act.activation(ex[:, 0:k], lg[:, 0:k], ACT.Exp).then_inc(exp_done, 1)

                    @block.vector
                    def _(dve):
                        st = Steps(dve, own)
                        dve.tensor_reduce(colsum[:, :], XN[0:B, :, :].rearrange("p b d -> p d b"), AX.X, ALU.add).then_inc(col_done, 1)
                        dve.wait_ge(mean_mm, 1)
                        dve.tensor_scalar(mT[:, :], ps[:, 0:KF], 1.0 / N, None, ALU.mult).then_inc(mT_done, 1)
                        dve.wait_ge(lg_mm, 1)
                        dve.wait_ge(loaded, 32)
                        st(dve.tensor_tensor(lg[:, :], ps2[0:1, 0:n_e], br[:, :], ALU.add))

                        def softmax(i, k, dst):
                            st(dve.tensor_reduce(mx[:, :], lg[:, 0:k], AX.X, ALU.max))
                            dve.tensor_scalar(lg[:, 0:k], lg[:, 0:k], mx[:, 0:1], None, ALU.subtract).then_inc(to_exp, 1)
                            dve.wait_ge(exp_done, i + 1)
                            st(dve.tensor_reduce(sm[:, :], ex[:, 0:k], AX.X, ALU.add))
                            st(dve.reciprocal(sm[:, :], sm[:, :]))
                            st(dve.tensor_scalar(dst, ex[:, 0:k], sm[:, 0:1], None, ALU.mult))

                        softmax(0, n_e, rw[:, :])
                        st(dve.tensor_scalar(sc[:, :], rw[:, :], float(N), cap, ALU.mult, ALU.max))
                        st(dve.reciprocal(sc[:, :], sc[:, :]))
                        st(dve.tensor_scalar(sc[:, :], sc[:, :], cap, None, ALU.mult))
                        st(dve.tensor_tensor(lg[:, :], rw[:, :], sc[:, :], ALU.mult))
                        softmax(1, n_e, rw[:, :])
                        st(dve.max(top[:, :], rw[:, :]))
                        st(dve.max_index(topi[:, :], top[:, :], rw[:, :]))
                        st(dve.tensor_copy(lg[:, 0:2], top[:, 0:2]))
                        softmax(2, 2, rw[:, 0:2])
                        dve.tensor_copy(lg[:, 0:2], rw[:, 0:2]).then_inc(w_done, 1)
                        dve.wait_ge(w_mm, 1)
                        dve.tensor_copy(topw[:, :], ps3[0:B, 0:2])

        for which, (k_, o_) in enumerate((("dst", "src"), ("src", "dst"))):
            sort_edges(which, A[k_], A[o_], A["edge_weight"])
            end_phase()

        XN = sb(ctx, "XN", [P, NB, D])

        def blk(k, b):
            return bass.ds(k * CH + b, 1)

        def bias_and_self(dve, st, k, ys, b2, tmp):
            st(dve.tensor_tensor(tmp[:, :, :], ys[0], b2[0][:, :].unsqueeze(1).broadcast_to([B, CH, D]), ALU.add))
            u = U[:, bass.ds(k * CH, CH), :]
            return dve.tensor_tensor(u, u, tmp[:, :, :], ALU.add)

        def plain(dve, st, k, ys, b2, tmp):
            return dve.tensor_copy(U[:, bass.ds(k * CH, CH), :], ys[0])

        layer_norm("ln_a", X, XN)
        end_phase()
        with ExitStack() as c0:
            edge = {"kT": sb(c0, "edge_kT", [SMALL, NB, B]), "m": sb(c0, "edge_m", [B, NB]), "l": sb(c0, "edge_l", [B, NB]),
                    "wqk": A["L0_gnn_Wqk"], "bqk": A["L0_gnn_bqk"], "bk": A["L0_gnn_bk"]}
            with ExitStack() as c1:
                kvd = attention_sums(c1, "sums0", A["L0_mix_Wkv"], edge, table0, turns=0)
                end_phase()
                attention_rows("att0", A["L0_mix_Wq"], kvd, True, turns=10)
                end_phase()
            layer_norm("ln_b", U, U, affine=(A["L0_mix_ln1_g"], A["L0_mix_ln1_b"]), turns=4)
            end_phase()
            mlp("mix0", [U], [(A["L0_mix_W1"], A["L0_mix_b1"], A["L0_mix_W2"], A["L0_mix_b2"].partition_broadcast(B))],
                D, ACT.Gelu, 1, bias_and_self, turns=8)
            end_phase()
            layer_norm("ln_c", U, U, affine=(A["L0_mix_ln2_g"], A["L0_mix_ln2_b"]), into=X, turns=2)
            end_phase()
            edge_softmax(edge)
            end_phase()
            own = sem("gat_end")
            mv = mover("gat_end", 1)
            with nc.Block() as block:
                @block.sync
                def _(sp):
                    mv.sp(sp)

                @block.gpsimd
                def _(pool):
                    mv.pool(pool)

                @block.vector
                def _(dve):
                    st = Steps(dve, own)
                    st(dve.reciprocal(edge["l"][:, :], edge["l"][:, :]))
                    with loop(dve, NB // R, st, R) as t:
                        for i in range(R):
                            r = bass.ds(t * R + i, 1)
                            st.mark(dve.scalar_tensor_tensor(one(X[:, r, :]), one(U[:, r, :]), edge["l"][:, r], one(X[:, r, :]), ALU.mult, ALU.add))
            end_phase()

        layer_norm("ln_d", X, XN, turns=2)
        end_phase()
        with ExitStack() as c0:
            selw = sb(c0, "selw", [B, NB])
            route_rows(selw, turns=8)
            end_phase()

            def weighted(dve, st, k, ys, b2, tmp):
                st(dve.tensor_tensor(tmp[:, :, :], ys[0], b2[0][:, :].unsqueeze(1).broadcast_to([B, CH, D]), ALU.add))
                for b in range(CH):
                    st(dve.scalar_tensor_tensor(tmp[:, b, :], tmp[:, b, :], selw[:, blk(k, b)], one(XN[0:B, blk(k, b), :]), ALU.mult, ALU.add))
                x = X[:, bass.ds(k * CH, CH), :]
                return dve.tensor_tensor(x, x, tmp[:, :, :], ALU.add)

            mlp("ffn0", [XN], [(A["L0_ffn_w1"], A["L0_ffn_b1"], A["L0_ffn_w2"], A["L0_ffn_b2"].partition_broadcast(B))],
                4 * D, ACT.Gelu_apprx_tanh, 1 + CH, weighted, turns=24)
            end_phase()

        layer_norm("ln_e", X, XN, turns=2)
        end_phase()
        with ExitStack() as c1:
            kvd = attention_sums(c1, "sums1", A["L1_mix_Wkv"], None, table1, turns=13)
            end_phase()
            attention_rows("att1", A["L1_mix_Wq"], kvd, False, turns=9)
            end_phase()
        linear("merge", U, A["L1_mix_Wm"], None, 0, lambda dve, st, k, y, b: dve.tensor_copy(U[:, bass.ds(k * CH, CH), :], y),
               turns=4)
        end_phase()
        layer_norm("ln_f", U, U, affine=(A["L1_mix_g1"], A["L1_mix_b1"]), turns=4)
        end_phase()
        mlp("mix1", [XN, U], [(A["L1_mix_W1"], None, A["L1_mix_W2"], None)], 2 * D, ACT.Relu, 0, plain, turns=20)
        end_phase()
        layer_norm("ln_g", U, U, affine=(A["L1_mix_g2"], A["L1_mix_b2"]), into=X, plus=XN, turns=1)
        end_phase()
        assert moved[0] == EC, moved
        edge_sums()
        end_phase()

        def into_x(dve, st, k, y, b2):
            x = X[:, bass.ds(k * CH, CH), :]
            st(dve.tensor_tensor(x, x, y, ALU.add))
            return dve.tensor_tensor(x, x, b2[:, :].unsqueeze(1).broadcast_to([B, CH, D]), ALU.add)

        linear("gcn_w", U, A["L1_gnn_W"], A["L1_gnn_b"], 1, into_x)
        end_phase()

        layer_norm("ln_h", X, XN)
        end_phase()
        topi = sb(ctx, "topi", [1, 8], mybir.dt.uint32)
        topw = sb(ctx, "topw", [B, 2])
        route_experts(topi, topw)
        end_phase()
        bb = sb(ctx, "expert_bias", [B, D])
        held = {}

        def expert(name, shape):
            def load(sp, e):
                if e not in held:
                    held[e] = sp.value_load(topi[0:1, e:e + 1], min_val=0, max_val=7)
                return shape(A[name][bass.ds(held[e], 1)])
            return load

        def both_biases(dve, st, b2):
            st(dve.tensor_scalar(bb[:, :], b2[0][:, :], topw[:, 0:1], None, ALU.mult))
            st(dve.scalar_tensor_tensor(bb[:, :], b2[1][:, :], topw[:, 1:2], bb[:, :], ALU.mult, ALU.add))

        def mixed(dve, st, k, ys, b2, tmp):
            xn, u = XN[0:B, bass.ds(k * CH, CH), :], U[:, bass.ds(k * CH, CH), :]
            st(dve.scalar_tensor_tensor(tmp[:, :, :], ys[0], topw[:, 0:1], xn, ALU.mult, ALU.add))
            st(dve.scalar_tensor_tensor(tmp[:, :, :], ys[1], topw[:, 1:2], tmp[:, :, :], ALU.mult, ALU.add))
            return dve.tensor_tensor(u, tmp[:, :, :], bb[:, :].unsqueeze(1).broadcast_to([B, CH, D]), ALU.add)

        spec = (expert("L1_ffn_W1", lambda a: a.rearrange("e p k f -> (e p) k f")), expert("L1_ffn_b1", lambda a: a.rearrange("e p f -> (e p) f")),
                expert("L1_ffn_W2", lambda a: a.rearrange("e p f d -> (e p) f d")), expert("L1_ffn_b2", lambda a: a.rearrange("e d -> (e d)").partition_broadcast(B)))
        mlp("ffn1", [XN], [spec, spec], 2 * D, ACT.Gelu, 2, mixed, setup=both_biases)
        end_phase()
        layer_norm("ln_i", U, U, affine=(A["L1_ffn_gamma"], A["L1_ffn_beta"]), into=X)
        end_phase()

        s_out = sem("out_written")
        with nc.Block() as block:
            @block.sync
            def _(sp):
                for i in range(5):
                    n = NB // 5
                    sp.dma_start(rows(out)[:, i * n:(i + 1) * n, :], X[:, i * n:(i + 1) * n, :]).then_inc(s_out, 16)
                sp.wait_ge(s_out, 80)


def lay_out(inputs):
    a = {k: np.asarray(v) for k, v in inputs.items()}

    def halves(w):
        return np.ascontiguousarray(w.reshape(-1, P, w.shape[-1]).transpose(1, 0, 2))

    def edges(v, fill):
        out = np.full((P * EC,), fill, v.dtype)
        out[:E] = v
        return out.reshape(P, EC)

    o = {"x": a["x"], "src": None, "dst": None}
    pad_key = NB * B + B // 2
    o["src"], o["dst"] = edges(a["src"], pad_key), edges(a["dst"], pad_key)
    o["edge_weight"] = edges(a["edge_weight"], 0)
    wq, wk = a["L0_gnn_Wq"], a["L0_gnn_Wk"]
    o["L0_gnn_Wqk"] = halves(np.concatenate([wq, wk], 1))
    o["L0_gnn_bqk"] = np.concatenate([a["L0_gnn_bq"], a["L0_gnn_bk"]])[None]
    o["L0_gnn_bk"] = a["L0_gnn_bk"][:, None]
    w = a["L0_mix_Wqkv"].T
    o["L0_mix_Wq"], o["L0_mix_Wkv"] = halves(w[:, :D]), halves(w[:, D:])
    o["L0_mix_W1"], o["L0_mix_W2"] = halves(a["L0_mix_W1"].T), halves(a["L0_mix_W2"].T)
    o["L0_mix_b1"] = np.ascontiguousarray(a["L0_mix_b1"].reshape(-1, P).T)
    for n in ("L0_mix_b2", "L0_mix_ln1_g", "L0_mix_ln1_b", "L0_mix_ln2_g", "L0_mix_ln2_b", "L0_ffn_b2", "L0_ffn_br",
              "L1_gnn_b", "L1_mix_g1", "L1_mix_b1", "L1_mix_g2", "L1_mix_b2", "L1_ffn_gamma", "L1_ffn_beta", "L1_ffn_b2"):
        o[n] = a[n]
    o["L0_ffn_wr"] = a["L0_ffn_wr"].reshape(-1)
    o["L0_ffn_w1"], o["L0_ffn_w2"] = halves(a["L0_ffn_w1"]), halves(a["L0_ffn_w2"])
    o["L0_ffn_b1"] = np.ascontiguousarray(a["L0_ffn_b1"].reshape(-1, P).T)
    o["L1_gnn_W"] = halves(a["L1_gnn_W"])
    o["L1_mix_Wq"] = halves(a["L1_mix_Wq"])
    o["L1_mix_Wkv"] = halves(np.concatenate([a["L1_mix_Wk"], a["L1_mix_Wv"]], 1))
    for n in ("L1_mix_Wm", "L1_mix_W1", "L1_mix_W2", "L1_ffn_Wr"):
        o[n] = halves(a[n])
    o["L1_ffn_br"] = a["L1_ffn_br"][None]
    o["L1_ffn_W1"] = np.stack([halves(x) for x in a["L1_ffn_W1"]])
    o["L1_ffn_W2"] = np.stack([halves(x) for x in a["L1_ffn_W2"]])
    o["L1_ffn_b1"] = np.ascontiguousarray(a["L1_ffn_b1"].reshape(8, -1, P).transpose(0, 2, 1))
    return o


def kernel(**inputs):
    import concourse.bacc as bacc
    from concourse.bass_utils import run_bass_kernel_spmd

    arrays = lay_out(inputs)
    nc = bacc.Bacc("TRN2", target_bir_lowering=False, num_devices=1)
    A = {n: nc.dram_tensor("in_" + n, v.shape, mybir.dt.from_np(v.dtype), kind="ExternalInput").ap() for n, v in arrays.items()}
    out = nc.dram_tensor("out_x", (N, D), F32, kind="ExternalOutput").ap()
    gps_kernel(nc, A, out)
    r = run_bass_kernel_spmd(nc, [{"in_" + n: v for n, v in arrays.items()}], core_ids=[0])
    return r.results[0]["out_x"]
```
